# Optimizing a Trainium2 kernel written in Bass

```python
import numpy as np
import jax
import jax.numpy as jnp

def _softmax(x, axis=-1):
    return jax.nn.softmax(x, axis=axis)

def _gelu(x):
    return jax.nn.gelu(x, approximate=True)

def _silu(x):
    return jax.nn.silu(x)

def _sigmoid(x):
    return jax.nn.sigmoid(x)

def _layernorm(x, axis=-1, eps=1e-05):
    m = jnp.mean(x, axis=axis, keepdims=True)
    v = jnp.var(x, axis=axis, keepdims=True)
    return (x - m) / jnp.sqrt(v + eps)

def _scatter_add(tgt, idx, src, axis=0):
    return tgt.at[idx].add(src)

def _segment_sum(src, seg, n):
    return jax.ops.segment_sum(src, seg, n)
kernel_name = 'mk_xattn_ffn_d2_seqx_r8_050bbc'

def setup_inputs(seed: int=0):
    np.random.seed(seed)
    _w = jnp.asarray

    def _rec_inputs():
        import jax
        import jax.numpy as jnp
        _rk = jax.random.key(seed)
        x = -0.0002928 + 1 * jax.random.normal(jax.random.fold_in(_rk, 1), (32, 56, 256), jnp.float32)
        _lenS = 56 - jax.random.randint(jax.random.fold_in(_rk, 7), (32,), 0, max(1, 56 // 4) + 1, jnp.int32)
        _lenS2 = 1500 - jax.random.randint(jax.random.fold_in(_rk, 8), (32,), 0, max(1, 1500 // 4) + 1, jnp.int32)
        _ctx_2048P = jax.random.normal(jax.random.fold_in(_rk, 11), (32, 16, 256), jnp.float32)
        _ctx_2048c = jax.random.dirichlet(jax.random.fold_in(_rk, 511), 0.3 * jnp.ones((16,), jnp.float32), (32, 1500))
        _ctx_2048t = jnp.einsum('bsk,bkd->bsd', _ctx_2048c, _ctx_2048P)
        _ctx_2048t = _ctx_2048t * jax.lax.rsqrt(jnp.mean(jnp.square(_ctx_2048t)) + 1e-12) * 0.953939
        ctx_2048 = 4.13588e-05 + 0.999923 * (_ctx_2048t + 0.3 * jax.random.normal(jax.random.fold_in(_rk, 611), (32, 1500, 256), jnp.float32))
        _validS = jnp.arange(56)[None, :] < _lenS[:, None]
        _validS2 = jnp.arange(1500)[None, :] < _lenS2[:, None]
        _causal = jnp.tril(jnp.ones((56, 56), dtype=bool))
        mask_1xSxS2_ff0 = jnp.where(jnp.ones((1, 56, 1500), dtype=bool), 0.0, -1000000000.0).astype(jnp.float32)
        return (x, ctx_2048, mask_1xSxS2_ff0)
    x, ctx_2048, mask_1xSxS2_ff0 = _rec_inputs()

    def _L0_xattn_setup():
        import jax, jax.numpy as jnp
        import numpy as np
        H = 256
        NH = 16
        NKV = 4
        HD = 128
        GROUPS = NH // NKV
        EPS = 1e-06
        B, S, SE = (1, 256, 512)

        def _rmsnorm(x, w, eps=EPS):
            xf = x.astype(jnp.float32)
            var = jnp.mean(xf * xf, axis=-1, keepdims=True)
            return (xf * jax.lax.rsqrt(var + eps)).astype(x.dtype) * w
        key = jax.random.key(seed)
        ks = jax.random.split(key, 12)
        sc = 0.02
        return {'hidden_states': jax.random.normal(ks[0], (B, S, H), jnp.float32), 'encoder_hidden_states': jax.random.normal(ks[1], (B, SE, H), jnp.float32), 'attention_mask': jnp.zeros((B, S, SE), jnp.float32), 'Wq': jax.random.normal(ks[2], (H, NH * HD), jnp.float32) * sc, 'bq': jax.random.normal(ks[3], (NH * HD,), jnp.float32) * sc, 'Wk': jax.random.normal(ks[4], (H, NKV * HD), jnp.float32) * sc, 'bk': jax.random.normal(ks[5], (NKV * HD,), jnp.float32) * sc, 'Wv': jax.random.normal(ks[6], (H, NKV * HD), jnp.float32) * sc, 'bv': jax.random.normal(ks[7], (NKV * HD,), jnp.float32) * sc, 'Wo': jax.random.normal(ks[8], (NH * HD, H), jnp.float32) * sc, 'qn_w': jnp.ones((HD,), jnp.float32), 'kn_w': jnp.ones((HD,), jnp.float32)}
    _L0_xattn_all = _L0_xattn_setup()
    _L0_xattn_in = {k: v for k, v in _L0_xattn_all.items() if k in ('Wq', 'bq', 'Wk', 'bk', 'Wv', 'bv', 'Wo', 'qn_w', 'kn_w')}
    del _L0_xattn_all

    def _L0_ffn_setup():
        import jax, jax.numpy as jnp
        import numpy as np
        NUM_EXPERTS = 32
        TOP_K = 6
        N_GROUPS = 4
        N_LIMITED_GROUPS = 2
        key = jax.random.key(seed)
        ks = jax.random.split(key, 8)
        H, M = (256, 176)
        SH = 2 * M
        s = 0.02
        return {'hidden_states': jax.random.normal(ks[0], (4, 256, H), jnp.float32), 'gate_w': jax.random.normal(ks[1], (H, NUM_EXPERTS), jnp.float32) * s, 'w_gate': jax.random.normal(ks[2], (NUM_EXPERTS, H, M), jnp.float32) * s, 'w_up': jax.random.normal(ks[3], (NUM_EXPERTS, H, M), jnp.float32) * s, 'w_down': jax.random.normal(ks[4], (NUM_EXPERTS, M, H), jnp.float32) * s, 'sw_gate': jax.random.normal(ks[5], (H, SH), jnp.float32) * s, 'sw_up': jax.random.normal(ks[6], (H, SH), jnp.float32) * s, 'sw_down': jax.random.normal(ks[7], (SH, H), jnp.float32) * s}
    _L0_ffn_all = _L0_ffn_setup()
    _L0_ffn_in = {k: v for k, v in _L0_ffn_all.items() if k in ('gate_w', 'w_gate', 'w_up', 'w_down', 'sw_gate', 'sw_up', 'sw_down')}
    del _L0_ffn_all

    def _L1_xattn_setup():
        import jax, jax.numpy as jnp
        import numpy as np
        NUM_HEADS = 16

        def _qdq(x):
            s = jnp.maximum(jnp.max(jnp.abs(x), axis=-1, keepdims=True) / 127.0, 1e-08)
            return jnp.clip(jnp.round(x / s), -127.0, 127.0) * s
        key = jax.random.key(seed)
        ks = jax.random.split(key, 8)
        B, N, M, D = (2, 512, 64, 256)
        w_std = 0.02
        return {'x': jax.random.normal(ks[0], (B, N, D), jnp.float32), 'cond': jax.random.normal(ks[1], (B, M, D), jnp.float32), 'wq': jax.random.normal(ks[2], (D, D), jnp.float32) * w_std, 'bq': jax.random.normal(ks[3], (D,), jnp.float32) * w_std, 'wkv': jax.random.normal(ks[4], (2 * D, D), jnp.float32) * w_std, 'bkv': jax.random.normal(ks[5], (2 * D,), jnp.float32) * w_std, 'wp': jax.random.normal(ks[6], (D, D), jnp.float32) * w_std, 'bp': jax.random.normal(ks[7], (D,), jnp.float32) * w_std}
    _L1_xattn_all = _L1_xattn_setup()
    _L1_xattn_in = {k: v for k, v in _L1_xattn_all.items() if k in ('wq', 'bq', 'wkv', 'bkv', 'wp', 'bp')}
    del _L1_xattn_all

    def _L1_ffn_setup():
        import jax, jax.numpy as jnp
        import numpy as np
        BITS = 4
        SIGNED_MIN, SIGNED_MAX = (-2 ** (BITS - 1), 2 ** (BITS - 1) - 1)
        UNSIGNED_MIN, UNSIGNED_MAX = (0, 2 ** BITS - 1)
        INT32_MIN, INT32_MAX = (-2.0 ** 31, 2.0 ** 31 - 1)

        def fake_quant(x, scale, qmin, qmax):
            q = jnp.clip(jnp.round(x / scale), qmin, qmax) * scale
            return x + jax.lax.stop_gradient(q - x)

        def weight_scale(W):
            return jax.lax.stop_gradient(jnp.max(jnp.abs(W))) / SIGNED_MAX
        key = jax.random.key(seed)
        ks = jax.random.split(key, 5)
        B, S, D, F = (4, 256, 256, 1024)
        return {'x': jax.random.normal(ks[0], (B, S, D), dtype=jnp.float32), 'W1': jax.random.normal(ks[1], (F, D), dtype=jnp.float32) * 0.02, 'b1': jax.random.normal(ks[2], (F,), dtype=jnp.float32) * 0.02, 'W2': jax.random.normal(ks[3], (D, F), dtype=jnp.float32) * 0.02, 'b2': jax.random.normal(ks[4], (D,), dtype=jnp.float32) * 0.02, 's_act1': jnp.full((1,), 0.1, dtype=jnp.float32), 's_act2': jnp.full((1,), 0.1, dtype=jnp.float32)}
    _L1_ffn_all = _L1_ffn_setup()
    _L1_ffn_in = {k: v for k, v in _L1_ffn_all.items() if k in ('W1', 'b1', 'W2', 'b2', 's_act1', 's_act2')}
    del _L1_ffn_all
    return {'x': x, 'ctx_2048': ctx_2048, 'mask_1xSxS2_ff0': mask_1xSxS2_ff0, 'L0_xattn_Wq': _L0_xattn_in['Wq'], 'L0_xattn_bq': _L0_xattn_in['bq'], 'L0_xattn_Wk': _L0_xattn_in['Wk'], 'L0_xattn_bk': _L0_xattn_in['bk'], 'L0_xattn_Wv': _L0_xattn_in['Wv'], 'L0_xattn_bv': _L0_xattn_in['bv'], 'L0_xattn_Wo': _L0_xattn_in['Wo'], 'L0_xattn_qn_w': _L0_xattn_in['qn_w'], 'L0_xattn_kn_w': _L0_xattn_in['kn_w'], 'L0_ffn_gate_w': _L0_ffn_in['gate_w'], 'L0_ffn_w_gate': _L0_ffn_in['w_gate'], 'L0_ffn_w_up': _L0_ffn_in['w_up'], 'L0_ffn_w_down': _L0_ffn_in['w_down'], 'L0_ffn_sw_gate': _L0_ffn_in['sw_gate'], 'L0_ffn_sw_up': _L0_ffn_in['sw_up'], 'L0_ffn_sw_down': _L0_ffn_in['sw_down'], 'L1_xattn_wq': _L1_xattn_in['wq'], 'L1_xattn_bq': _L1_xattn_in['bq'], 'L1_xattn_wkv': _L1_xattn_in['wkv'], 'L1_xattn_bkv': _L1_xattn_in['bkv'], 'L1_xattn_wp': _L1_xattn_in['wp'], 'L1_xattn_bp': _L1_xattn_in['bp'], 'L1_ffn_W1': _L1_ffn_in['W1'], 'L1_ffn_b1': _L1_ffn_in['b1'], 'L1_ffn_W2': _L1_ffn_in['W2'], 'L1_ffn_b2': _L1_ffn_in['b2'], 'L1_ffn_s_act1': _L1_ffn_in['s_act1'], 'L1_ffn_s_act2': _L1_ffn_in['s_act2']}

def reference(x, ctx_2048, mask_1xSxS2_ff0, L0_xattn_Wq, L0_xattn_bq, L0_xattn_Wk, L0_xattn_bk, L0_xattn_Wv, L0_xattn_bv, L0_xattn_Wo, L0_xattn_qn_w, L0_xattn_kn_w, L0_ffn_gate_w, L0_ffn_w_gate, L0_ffn_w_up, L0_ffn_w_down, L0_ffn_sw_gate, L0_ffn_sw_up, L0_ffn_sw_down, L1_xattn_wq, L1_xattn_bq, L1_xattn_wkv, L1_xattn_bkv, L1_xattn_wp, L1_xattn_bp, L1_ffn_W1, L1_ffn_b1, L1_ffn_W2, L1_ffn_b2, L1_ffn_s_act1, L1_ffn_s_act2):
    import jax
    import jax.numpy as jnp

    def _L0_xattn_ref(hidden_states, encoder_hidden_states, attention_mask, Wq, bq, Wk, bk, Wv, bv, Wo, qn_w, kn_w):
        import jax, jax.numpy as jnp
        import numpy as np
        H = 256
        NH = 16
        NKV = 4
        HD = 128
        GROUPS = NH // NKV
        EPS = 1e-06
        B, S, SE = (1, 256, 512)

        def _rmsnorm(x, w, eps=EPS):
            xf = x.astype(jnp.float32)
            var = jnp.mean(xf * xf, axis=-1, keepdims=True)
            return (xf * jax.lax.rsqrt(var + eps)).astype(x.dtype) * w
        b, s, _ = hidden_states.shape
        se = encoder_hidden_states.shape[1]
        q = (hidden_states @ Wq + bq).reshape(b, s, NH, HD).transpose(0, 2, 1, 3)
        k = (encoder_hidden_states @ Wk + bk).reshape(b, se, NKV, HD).transpose(0, 2, 1, 3)
        v = (encoder_hidden_states @ Wv + bv).reshape(b, se, NKV, HD).transpose(0, 2, 1, 3)
        k = jnp.repeat(k, GROUPS, axis=1)
        v = jnp.repeat(v, GROUPS, axis=1)
        q = _rmsnorm(q, qn_w)
        k = _rmsnorm(k, kn_w)
        scale = 1.0 / np.sqrt(HD).astype(np.float32)
        scores = jnp.einsum('bhsd,bhed->bhse', q, k) * scale
        scores = scores + attention_mask[:, None, :, :]
        probs = jax.nn.softmax(scores.astype(jnp.float32), axis=-1).astype(q.dtype)
        out = jnp.einsum('bhse,bhed->bhsd', probs, v)
        out = out.transpose(0, 2, 1, 3).reshape(b, s, NH * HD)
        return out @ Wo

    def _L0_ffn_ref(hidden_states, gate_w, w_gate, w_up, w_down, sw_gate, sw_up, sw_down):
        import jax, jax.numpy as jnp
        import numpy as np
        NUM_EXPERTS = 32
        TOP_K = 6
        N_GROUPS = 4
        N_LIMITED_GROUPS = 2
        B, S, H = hidden_states.shape
        E, K = (NUM_EXPERTS, TOP_K)
        x = hidden_states.reshape(-1, H)
        T = x.shape[0]
        scores = jax.nn.sigmoid(x @ gate_w)
        original_scores = scores
        epg = E // N_GROUPS
        sg = scores.reshape(T, N_GROUPS, epg)
        group_scores = jnp.max(sg, axis=-1)
        _, top_groups = jax.lax.top_k(group_scores, N_LIMITED_GROUPS)
        mask = jnp.ones((T, N_GROUPS), dtype=bool)
        mask = mask.at[jnp.arange(T)[:, None], top_groups].set(False)
        sg = jnp.where(mask[:, :, None], -jnp.inf, sg)
        masked_scores = sg.reshape(T, E)
        _, selected_experts = jax.lax.top_k(masked_scores, K)
        weights = jnp.take_along_axis(original_scores, selected_experts, axis=-1)
        weights = weights / jnp.sum(weights, axis=-1, keepdims=True)
        sel_flat = selected_experts.ravel()
        x_exp = jnp.repeat(x, K, axis=0)
        sort_idx = jnp.argsort(sel_flat)
        xs = x_exp[sort_idx]
        group_sizes = jnp.bincount(sel_flat, length=E).astype(jnp.int32)
        g = jax.lax.ragged_dot(xs, w_gate, group_sizes)
        u = jax.lax.ragged_dot(xs, w_up, group_sizes)
        d = jax.lax.ragged_dot(jax.nn.silu(g) * u, w_down, group_sizes)
        unsort_idx = jnp.argsort(sort_idx)
        out = d[unsort_idx].reshape(T, K, H)
        expert_out = jnp.sum(out * weights[..., None], axis=1)
        shared = jax.nn.silu(x @ sw_gate) * (x @ sw_up) @ sw_down
        return (expert_out + shared).reshape(B, S, H)

    def _L1_xattn_ref(x, cond, wq, bq, wkv, bkv, wp, bp):
        import jax, jax.numpy as jnp
        import numpy as np
        NUM_HEADS = 16

        def _qdq(x):
            s = jnp.maximum(jnp.max(jnp.abs(x), axis=-1, keepdims=True) / 127.0, 1e-08)
            return jnp.clip(jnp.round(x / s), -127.0, 127.0) * s
        B, N, C = x.shape
        M = cond.shape[1]
        H = NUM_HEADS
        Dh = C // H
        q = _qdq(x) @ _qdq(wq).T + bq
        kv = cond @ wkv.T + bkv
        k, v = jnp.split(kv, 2, axis=-1)
        q = q.reshape(B, N, H, Dh)
        k = k.reshape(B, M, H, Dh)
        v = v.reshape(B, M, H, Dh)
        scale = 1.0 / np.sqrt(Dh)
        attn = jax.nn.softmax(jnp.einsum('bnhd,bmhd->bhnm', q, k) * scale, axis=-1)
        o = jnp.einsum('bhnm,bmhd->bnhd', attn, v).reshape(B, N, C)
        out = _qdq(o) @ _qdq(wp).T + bp
        return out

    def _L1_ffn_ref(x, W1, b1, W2, b2, s_act1, s_act2):
        import jax, jax.numpy as jnp
        import numpy as np
        BITS = 4
        SIGNED_MIN, SIGNED_MAX = (-2 ** (BITS - 1), 2 ** (BITS - 1) - 1)
        UNSIGNED_MIN, UNSIGNED_MAX = (0, 2 ** BITS - 1)
        INT32_MIN, INT32_MAX = (-2.0 ** 31, 2.0 ** 31 - 1)

        def fake_quant(x, scale, qmin, qmax):
            q = jnp.clip(jnp.round(x / scale), qmin, qmax) * scale
            return x + jax.lax.stop_gradient(q - x)

        def weight_scale(W):
            return jax.lax.stop_gradient(jnp.max(jnp.abs(W))) / SIGNED_MAX
        s1 = s_act1[0]
        s2 = s_act2[0]
        x_q = fake_quant(x, s1, SIGNED_MIN, SIGNED_MAX)
        sw1 = weight_scale(W1)
        W1_q = fake_quant(W1, sw1, SIGNED_MIN, SIGNED_MAX)
        b1_q = fake_quant(b1, s1 * sw1, INT32_MIN, INT32_MAX)
        h = jnp.einsum('bsd,fd->bsf', x_q, W1_q) + b1_q
        h_q = fake_quant(jax.nn.relu(h), s2, UNSIGNED_MIN, UNSIGNED_MAX)
        sw2 = weight_scale(W2)
        W2_q = fake_quant(W2, sw2, SIGNED_MIN, SIGNED_MAX)
        b2_q = fake_quant(b2, s2 * sw2, INT32_MIN, INT32_MAX)
        out = jnp.einsum('bsf,df->bsd', h_q, W2_q) + b2_q
        return out
    x = x + _L0_xattn_ref(_layernorm(x, axis=-1), ctx_2048, mask_1xSxS2_ff0, L0_xattn_Wq, L0_xattn_bq, L0_xattn_Wk, L0_xattn_bk, L0_xattn_Wv, L0_xattn_bv, L0_xattn_Wo, L0_xattn_qn_w, L0_xattn_kn_w)
    x = x + _L0_ffn_ref(_layernorm(x, axis=-1), L0_ffn_gate_w, L0_ffn_w_gate, L0_ffn_w_up, L0_ffn_w_down, L0_ffn_sw_gate, L0_ffn_sw_up, L0_ffn_sw_down)
    x = x + _L1_xattn_ref(_layernorm(x, axis=-1), ctx_2048, L1_xattn_wq, L1_xattn_bq, L1_xattn_wkv, L1_xattn_bkv, L1_xattn_wp, L1_xattn_bp)
    x = x + _L1_ffn_ref(_layernorm(x, axis=-1), L1_ffn_W1, L1_ffn_b1, L1_ffn_W2, L1_ffn_b2, L1_ffn_s_act1, L1_ffn_s_act2)
    return x

_drawn_inputs = setup_inputs


def setup_inputs(seed=0):
    import zlib

    import numpy as np

    out = dict(_drawn_inputs(seed))
    spreads = {'L0_xattn_qn_w': (1.0, 0.6), 'L0_xattn_kn_w': (1.0, 0.6)}
    factors = {'L0_xattn_bq': 8.0,
     'L0_xattn_bk': 8.0,
     'L0_xattn_bv': 2.901,
     'L0_ffn_gate_w': 6.679,
     'L0_ffn_w_gate': 6.343,
     'L0_ffn_w_up': 6.303,
     'L0_ffn_w_down': 6.32,
     'L1_xattn_wq': 149.754,
     'L1_xattn_bq': 200.0,
     'L1_xattn_bkv': 19.105,
     'L1_ffn_b1': 34.917,
     'L1_ffn_b2': 14.622,
     'L0_ffn_sw_gate': 5.683,
     'L0_ffn_sw_up': 5.63,
     'L0_ffn_sw_down': 5.61,
     'L1_xattn_bp': 5.523,
     'L1_ffn_W1': 3.528}
    for name, (base, spread) in spreads.items():
        noise = np.random.default_rng([zlib.crc32(name.encode()), seed]).standard_normal(out[name].shape)
        drawn = base * np.exp(spread * noise) if base else spread * noise
        out[name] = jnp.asarray(drawn.astype(out[name].dtype))
    for name, factor in factors.items():
        out[name] = (out[name] * factor).astype(out[name].dtype)
    return out
```

```python
import numpy as np
import concourse.bass as bass
from concourse import mybir
from contextlib import ExitStack, contextmanager

F32 = mybir.dt.float32
F16 = mybir.dt.float16
ALU = mybir.AluOpType
ACT = mybir.ActivationFunctionType
AX = mybir.AxisListType
ds = bass.ds

B, S, SE, H = 32, 56, 1500, 256
TOK = B * S
TT = 2 * S
NT = TOK // TT
KC = H // 128
KT, KP = 12, 125
NH, NKV, HD = 16, 4, 128
KVW = NKV * HD
NR = 8
HP = 64
HD1 = H // NH
NE, NX, M = 32, 34, 176
EPG, NG, TOPG, TOPK = 8, 4, 2, 6
MT = M - 128
F = 1024
FB = F // 128
WS = 64.0
MAGIC = 12582912.0
LN_EPS, RMS_EPS = 1e-5, 1e-6


class Counted:

    def __init__(self, eng, sem):
        self.eng, self.sem, self.n, self.marks = eng, sem, 0, 0

    def __call__(self, ins):
        ins.then_inc(self.sem, 1)
        self.n += 1
        self.marks += 1
        return self

    def done(self):
        self.eng.wait_ge(self.sem, self.n)


def wait(eng, sem, value):
    if isinstance(value, int) and value <= 0:
        return
    eng.wait_ge(sem, value)


def each(eng, n, body):
    body(0)
    with eng.Fori(1, n) as i:
        body(i)


def passed(eng, gate):
    eng.sem_inc(gate, 1)


def three_products(nc, out, a_hi, a_lo, b_hi, b_lo, start, stop):
    nc.tensor.matmul(out, a_hi, b_hi, start=start, stop=False)
    nc.tensor.matmul(out, a_hi, b_lo, start=False, stop=False)
    return nc.tensor.matmul(out, a_lo, b_hi, start=False, stop=stop)


class Alloc:
    def __init__(self, nc, ctx):
        self.nc, self.ctx, self.sems = nc, ctx, []

    def sb(self, name, shape, dt=F32):
        return self.ctx.enter_context(self.nc.sbuf_tensor(name, shape, dt))

    def ps(self, name, shape, dt=F32):
        return self.ctx.enter_context(self.nc.psum_tensor(name, shape, dt))

    def sem(self, name):
        self.sems.append(self.nc.alloc_semaphore(name))
        return self.sems[-1]


@contextmanager
def phase(nc):
    with ExitStack() as ctx:
        a = Alloc(nc, ctx)
        yield ctx, a
    nc.clear_and_free_semaphores(a.sems)
    nc.all_engine_barrier()


def constants(nc, g):
    with phase(nc) as (ctx, a):
        made = a.sem("const_made")
        block = ctx.enter_context(nc.Block())

        @block.gpsimd
        def _(pool):
            c = Counted(pool, made)
            c(nc.gpsimd.memset(g.ident[:], 0.0))
            c(nc.gpsimd.memset(g.ident16[:], 0.0))
            c(nc.gpsimd.memset(g.blk16[:], 1.0))
            c(nc.gpsimd.memset(g.mhalf[:], -0.5)).done()
            for t in (g.ident, g.ident16):
                c(nc.gpsimd.affine_select(out=t[:], in_=t[:], compare_op=ALU.not_equal, fill=1.0, base=0,
                                          pattern=[[-1, 128]], channel_multiplier=1))
            c(nc.gpsimd.affine_select(out=g.blk16[:], in_=g.blk16[:], compare_op=ALU.is_ge, fill=0.0, base=0,
                                      pattern=[[-16, 8]], channel_multiplier=1)).done()
            c(nc.gpsimd.affine_select(out=g.blk16[:], in_=g.blk16[:], compare_op=ALU.is_ge, fill=0.0, base=15,
                                      pattern=[[16, 8]], channel_multiplier=-1)).done()

        @block.vector
        def _(dve):
            dve.wait_ge(made, 8)
            nc.vector.tensor_reduce(g.evenodd[:], g.blk16[:].rearrange("p (c e) -> p e c", e=2), AX.X, ALU.add)


def q0_phase(nc, g, io):
    with phase(nc) as (ctx, a):
        wst = a.sb("q_wst", [128, KC, NH * HD])
        wqh = a.sb("q_wqh", [128, KC, NH * HD], F16)
        wql = a.sb("q_wql", [128, KC, NH * HD], F16)
        bq = a.sb("q_bq", [TT, NH * HD])
        wcol = a.sb("q_wcol", [128, 3])
        xt = a.sb("q_x", [TT, 2, H])
        st6 = a.sb("q_st6", [TT, 6])
        mv = a.sb("q_mv", [TT, 2])
        ve = a.sb("q_ve", [TT, 1])
        rs = a.sb("q_rs", [TT, 1])
        xn = a.sb("q_xn", [TT, H])
        xTh = a.sb("q_xTh", [128, KC, TT], F16)
        xTl = a.sb("q_xTl", [128, KC, TT], F16)
        qb = a.sb("q_qb", [TT, NH * HD])
        qq = a.sb("q_qq", [TT, NH * HD])
        ss = a.sb("q_ss", [TT, NH])
        ssv = a.sb("q_ssv", [TT, NH])
        rq = a.sb("q_rq", [TT, NH])
        qTh = a.sb("q_qTh", [128, 2, 2, NR, 2, HP], F16)
        qTl = a.sb("q_qTl", [128, 2, 2, NR, 2, HP], F16)
        pX = a.ps("q_pX", [128, 512])
        pQ = [a.ps(f"q_pQ{i}", [128, 512]) for i in range(4)]
        w_in, b_in = a.sem("q_w_in"), a.sem("q_b_in")
        x_in = [a.sem(f"q_x_in{i}") for i in range(2)]
        out_done = [a.sem(f"q_out{i}") for i in range(2)]
        w_hi, pads = a.sem("q_w_hi"), a.sem("q_pads")
        dve_own, pool_own, gate = a.sem("q_dve"), a.sem("q_pool"), a.sem("q_gate")
        var_ready, rstd_ready, xn_ready = a.sem("q_var"), a.sem("q_rstd"), a.sem("q_xn")
        xT_done, xT_hi, xT_lo = a.sem("q_xTd"), a.sem("q_xTh_"), a.sem("q_xTl_")
        q_done, q_biased, q_sq, q_ss, q_norm = (a.sem("q_" + s) for s in ("done", "biased", "sq", "ssd", "norm"))
        qT_done, qT_hi, qT_lo = a.sem("q_qTd"), a.sem("q_qTh_"), a.sem("q_qTl_")
        block = ctx.enter_context(nc.Block())

        @block.sync
        def _(sp):
            sp.dma_start(wst[:], io.Wq.rearrange("(c p) n -> p c n", p=128)).then_inc(w_in, 16)
            sp.dma_start(bq[:], io.bq.rearrange("(a n) -> a n", a=1).to_broadcast([TT, NH * HD])).then_inc(b_in, 16)
            sp.dma_start(wcol[:, 0:1], io.qn_w.rearrange("(p a) -> p a", a=1)).then_inc(b_in, 16)
            sp.dma_start(wcol[:, 1:2], io.kn_w.rearrange("(p a) -> p a", a=1)).then_inc(b_in, 16)
            def pair(i):
                for k in range(2):
                    wait(sp, xn_ready, 2 * i + k)
                    sp.dma_start(xt[:, k, :], io.x[ds((2 * i + k) * TT, TT), :]).then_inc(x_in[k], 16)
                    sp.wait_ge(qT_lo, 8 * (2 * i + k + 1))
                    for b in range(2):
                        for t, o in ((qTh, io.qh), (qTl, io.ql)):
                            sp.dma_start(o[ds(2 * (2 * i + k) + b, 1), :, :].rearrange("a p n -> p (a n)"),
                                         t[:, k, b].rearrange("p r e q -> p (r e q)")).then_inc(out_done[k], 16)

            each(sp, NT // 2, pair)
            for k in range(2):
                sp.wait_ge(out_done[k], 64 * (NT // 2))

        @block.gpsimd
        def _(pool):
            nc.gpsimd.memset(qTh[:], 0.0).then_inc(pads, 1)
            nc.gpsimd.memset(qTl[:], 0.0).then_inc(pads, 1)
            def pair(i):
                for k in range(2):
                    t = 2 * i + k
                    pool.wait_ge(var_ready, t + 1)
                    nc.gpsimd.tensor_tensor(rs[:], ve[:], g.mhalf[0:TT, 0:1], ALU.pow).then_inc(rstd_ready, 1)
                    pool.wait_ge(q_biased, 4 * t + 4)
                    nc.gpsimd.tensor_tensor(qq[:], qb[:], qb[:], ALU.mult).then_inc(q_sq, 1)
                    pool.wait_ge(q_ss, t + 1)
                    nc.gpsimd.tensor_tensor(rq[:], ssv[:], g.mhalf[0:TT, 0:NH], ALU.pow).then_inc(pool_own, 1)
                    pool.wait_ge(pool_own, t + 1)
                    nc.gpsimd.tensor_tensor(qb[:].rearrange("p (h d) -> p h d", d=HD),
                                            qb[:].rearrange("p (h d) -> p h d", d=HD),
                                            rq[:].unsqueeze(2).to_broadcast([TT, NH, HD]),
                                            ALU.mult).then_inc(q_norm, 1)

            each(pool, NT // 2, pair)

        @block.scalar
        def _(act):
            act.wait_ge(w_in, 16)
            for c in range(KC):
                nc.scalar.activation(wqh[:, c, :], wst[:, c, :], ACT.Copy, scale=WS).then_inc(w_hi, 1)
            act.wait_ge(pads, 2)
            def pair(i):
                for k in range(2):
                    t = 2 * i + k
                    act.wait_ge(xT_done, t + 1)
                    nc.scalar.activation(xTh[:], pX[:, 0:KC * TT].rearrange("p (c q) -> p c q", q=TT),
                                         ACT.Copy).then_inc(xT_hi, 1)
                    wait(act, out_done[k], 64 * i)
                    for j in range(4):
                        act.wait_ge(qT_done, 4 * t + j + 1)
                        nc.scalar.activation(qTh[:, k, :, 2 * j:2 * j + 2, :, 0:S].rearrange("p b r e q -> p b (r e) q"),
                                             pQ[j][:, 0:4 * TT].rearrange("p (h b q) -> p b h q", h=4, b=2),
                                             ACT.Copy, scale=wcol[:, 2:3]).then_inc(qT_hi, 1)

            each(act, NT // 2, pair)

        @block.vector
        def _(dve):
            own = Counted(dve, dve_own)
            dve.wait_ge(b_in, 48)
            own(nc.vector.tensor_tensor(wcol[:, 2:3], wcol[:, 0:1], wcol[:, 1:2], ALU.mult)).done()
            own(nc.vector.tensor_scalar(wcol[:, 2:3], wcol[:, 2:3], float(HD) ** -0.5, None, ALU.mult))
            for c in range(KC):
                dve.wait_ge(w_hi, c + 1)
                own(nc.vector.scalar_tensor_tensor(wql[:, c, :], wst[:, c, :], WS, wqh[:, c, :],
                                                   ALU.mult, ALU.subtract))
            own.done()
            base = own.n
            def pair(i):
                for k in range(2):
                    t = 2 * i + k
                    dve.wait_ge(x_in[k], 16 * i + 16)
                    nc.vector.bn_stats(st6[:], xt[:, k, :]).then_inc(dve_own, 1)
                    dve.wait_ge(dve_own, base + 3 * t + 1)
                    passed(dve, gate)
                    nc.vector.bn_aggr(mv[:], st6[:]).then_inc(dve_own, 1)
                    dve.wait_ge(dve_own, base + 3 * t + 2)
                    nc.vector.tensor_scalar(ve[:], mv[:, 1:2], LN_EPS, None, ALU.add).then_inc(var_ready, 1)
                    dve.wait_ge(rstd_ready, t + 1)
                    nc.vector.tensor_scalar(xn[:], xt[:, k, :], mv[:, 0:1], rs[:], ALU.subtract,
                                            ALU.mult).then_inc(xn_ready, 1)
                    dve.wait_ge(xT_hi, t + 1)
                    nc.vector.tensor_tensor(xTl[:], pX[:, 0:KC * TT].rearrange("p (c q) -> p c q", q=TT), xTh[:],
                                            ALU.subtract).then_inc(xT_lo, 1)
                    for j in range(4):
                        dve.wait_ge(q_done, 4 * t + j + 1)
                        nc.vector.scalar_tensor_tensor(qb[:, j * 512:(j + 1) * 512], pQ[j][0:TT, :], 1 / WS,
                                                       bq[:, j * 512:(j + 1) * 512], ALU.mult,
                                                       ALU.add).then_inc(q_biased, 1)
                    dve.wait_ge(q_sq, t + 1)
                    nc.vector.tensor_reduce(ss[:], qq[:].rearrange("p (h d) -> p h d", d=HD), AX.X,
                                            ALU.add).then_inc(dve_own, 1)
                    dve.wait_ge(dve_own, base + 3 * t + 3)
                    nc.vector.tensor_scalar(ssv[:], ss[:], 1.0 / HD, RMS_EPS, ALU.mult, ALU.add).then_inc(q_ss, 1)
                    for j in range(4):
                        dve.wait_ge(qT_hi, 4 * t + j + 1)
                        for b in range(2):
                            ins = nc.vector.scalar_tensor_tensor(
                                qTl[:, k, b, 2 * j:2 * j + 2, :, 0:S].rearrange("p r e q -> p (r e) q"),
                                pQ[j][:, 0:4 * TT].rearrange("p (h b q) -> p b h q", h=4, b=2)[:, b],
                                wcol[:, 2:3],
                                qTh[:, k, b, 2 * j:2 * j + 2, :, 0:S].rearrange("p r e q -> p (r e) q"),
                                ALU.mult, ALU.subtract)
                            ins.then_inc(qT_lo, 1)

            each(dve, NT // 2, pair)

        @block.tensor
        def _(pe):
            pe.wait_ge(dve_own, 4)
            def pair(i):
                for k in range(2):
                    t = 2 * i + k
                    pe.wait_ge(xn_ready, t + 1)
                    wait(pe, xT_lo, t)
                    for c in range(KC):
                        last = nc.tensor.transpose(pX[:, c * TT:(c + 1) * TT], xn[:, c * 128:(c + 1) * 128],
                                                   g.ident[0:TT, 0:TT])
                    last.then_inc(xT_done, 1)
                    pe.wait_ge(xT_lo, t + 1)
                    for j in range(4):
                        wait(pe, qT_lo, 8 * t)
                        for c in range(KC):
                            cols = slice(j * 512, (j + 1) * 512)
                            last = three_products(nc, pQ[j][0:TT, :], xTh[:, c, :], xTl[:, c, :], wqh[:, c, cols],
                                                  wql[:, c, cols], start=(c == 0), stop=(c == KC - 1))
                        last.then_inc(q_done, 1)
                    pe.wait_ge(q_norm, t + 1)
                    for j in range(4):
                        for h in range(4):
                            last = nc.tensor.transpose(pQ[j][:, h * TT:(h + 1) * TT],
                                                       qb[:, (4 * j + h) * HD:(4 * j + h + 1) * HD],
                                                       g.ident[0:TT, 0:TT])
                        last.then_inc(qT_done, 1)

            each(pe, NT // 2, pair)


UNITS = KT + 3


def attention_order():
    order, u = [], -1
    for r in range(NR):
        order.append(("scores", r, 0))
        if r:
            order += [("values", r - 1, 0), ("values", r - 1, 1), ("turn", r - 1, 2)]
        order.append(("unit", u, 0))
        u += 1
        if r:
            order.append(("values", r - 1, 2))
        if r in (0, 2, 3, 5, 6):
            order.append(("unit", u, 0))
            u += 1
        order += [("turn", r, 0), ("turn", r, 1)]
    order += [("unit", u, 0), ("values", 7, 0), ("values", 7, 1), ("turn", 7, 2), ("unit", u + 1, 0),
              ("values", 7, 2)]
    assert u + 1 == KT + 1
    return order


def unit_work(u):
    w = []
    if u + 1 < KT:
        w.append(("ctx", u + 1))
    if 0 <= u < KT:
        w += [("keys", u), ("vals", u)]
    if 0 <= u - 2 < KT:
        w.append(("keysT", u - 2))
    return w


def attn0_phase(nc, g, io):
    ORDER = attention_order()
    WORK = [w for u in range(-1, KT + 2) for w in unit_work(u)]
    AT = {w: n for n, w in enumerate(WORK)}
    NW = len(WORK)
    HI = {w: n for n, w in enumerate([w for w in WORK if w[0] != "keys"])}
    NHI = len(HI)
    with phase(nc) as (ctx, a):
        wst = a.sb("a_wst", [128, KC, KVW])
        wk = a.sb("a_wk", [128, KC, 2, KVW], F16)
        wv = a.sb("a_wv", [128, KC, 2, KVW], F16)
        bk = a.sb("a_bk", [KP, KVW])
        cx = a.sb("a_ctx", [KP, 2, KT, H])
        cTh = a.sb("a_cTh", [128, 2, KC, KP], F16)
        cTl = a.sb("a_cTl", [128, 2, KC, KP], F16)
        kb = a.sb("a_kb", [KP, 4, KVW])
        ksq = a.sb("a_ksq", [KP, 2, KVW])
        ssk = a.sb("a_ssk", [KP, 2, NKV])
        rk = a.sb("a_rk", [KP, 2, 2, NKV])
        kTh = a.sb("a_kTh", [128, 2, NKV, SE], F16)
        kTl = a.sb("a_kTl", [128, 2, NKV, SE], F16)
        vh = a.sb("a_vh", [KP, 2, KT, KVW], F16)
        vl = a.sb("a_vl", [KP, 2, KT, KVW], F16)
        qh = a.sb("a_qh", [128, 2, NR, 128], F16)
        ql = a.sb("a_ql", [128, 2, NR, 128], F16)
        pr = a.sb("a_pr", [128, 2, SE])
        pTh = a.sb("a_pTh", [KP, 2, KT, 128], F16)
        pTl = a.sb("a_pTl", [KP, 2, KT, 128], F16)
        nmax = a.sb("a_nmax", [128, 2, NR])
        rsum = a.sb("a_rsum", [128, 2, NR])
        inv = a.sb("a_inv", [128, 2, NR])
        mask = a.sb("a_mask", [128, SE])
        ot = a.sb("a_ot", [128, 2, NR, HD])
        ps_s = a.ps("a_ps", [128, 3, 512])
        ps_t = [a.ps(f"a_pt{i}", [128, 512]) for i in range(2)]
        ps_w = [a.ps(f"a_pw{i}", [128, 512]) for i in range(2)]
        ps_o = a.ps("a_po", [128, HD])
        w_in = [a.sem(f"a_w_in{i}") for i in range(2)]
        pool_own, pool_gate = a.sem("a_pool_own"), a.sem("a_pool_gate")
        b_in, w_hi, w_lo, gate = a.sem("a_b_in"), a.sem("a_w_hi"), a.sem("a_w_lo"), a.sem("a_gate")
        ctx_in = [a.sem(f"a_ctx_in{i}") for i in range(2)]
        q_in = [a.sem(f"a_q_in{i}") for i in range(2)]
        stored = [a.sem(f"a_stored{i}") for i in range(2)]
        names = ("scores_done nmax_ready exp_done turn_done turn_hi turn_lo values_done inv_ready o_taken ot_free "
                 "work_done work_hi work_taken k_squared k_ssq inv_scaled k_normed own")
        s = {n: a.sem("a_" + n) for n in names.split()}
        block = ctx.enter_context(nc.Block())

        def steps(eng, step):
            step(0, 0, 0, 0, True)
            with eng.Fori(0, (B - 2) // 2) as i:
                step(2 * i + 1, 1, i, i + 1, True)
                step(2 * i + 2, 0, i + 1, i + 1, True)
            step(B - 1, 1, (B - 1) // 2, B // 2, False)

        @block.sync
        def _(sp):
            sp.sem_inc(s["ot_free"], 2)
            sp.dma_start(wst[:], io.Wk.rearrange("(c p) n -> p c n", p=128)).then_inc(w_in[0], 16)
            sp.dma_start(bk[:], io.bk.rearrange("(a n) -> a n", a=1).to_broadcast([KP, KVW])).then_inc(b_in, 16)

            def load_ctx(G, par):
                src = io.ctx[ds(G, 1), :, :].rearrange("a (p k) d -> (a p) k d", k=KT)
                sp.dma_start(cx[0:120, par], src[0:120]).then_inc(ctx_in[par], 16)
                sp.dma_start(cx[120:KP, par], src[120:KP]).then_inc(ctx_in[par], 16)

            def load_q(G, par):
                for t, o in ((qh, io.qh), (ql, io.ql)):
                    sp.dma_start(t[:, par].rearrange("p r c -> p (r c)"),
                                 o[ds(G, 1), :, :].rearrange("a p n -> p (a n)")).then_inc(q_in[par], 16)

            sp.wait_ge(s["own"], 1)
            for e in range(2):
                sp.dma_start(mask[HP * e:HP * e + S, :], io.mask[0]).then_inc(b_in, 16)
            load_ctx(0, 0)
            load_ctx(1, 1)
            load_q(0, 0)
            sp.wait_ge(w_lo, 1)
            sp.dma_start(wst[:], io.Wv.rearrange("(c p) n -> p c n", p=128)).then_inc(w_in[1], 16)

            def step(g_, par, half, nxt, produce):
                if produce:
                    wait(sp, s["scores_done"], NR * g_)
                    load_q(g_ + 1, 1 - par)
                sp.wait_ge(s["o_taken"], NR * g_ + NR)
                for e in range(2):
                    sp.dma_start(io.o0[ds(g_ * S, S), :].rearrange("q (r e d) -> q r e d", e=2, d=HD)[:, :, e, :],
                                 ot[HP * e:HP * e + S, par]).then_inc(stored[par], 16)
                sp.wait_ge(stored[par], 32 * half + 32)
                sp.sem_inc(s["ot_free"], 1)

            def step_ctx(g_, par, half, nxt, produce, load):
                if load:
                    sp.wait_ge(s["work_done"], NW * g_ + AT["ctx", KT - 1] + 1)
                    load_ctx(g_ + 2, par)
                step(g_, par, half, nxt, produce)

            step_ctx(0, 0, 0, 0, True, True)
            with sp.Fori(0, (B - 4) // 2) as i:
                step_ctx(2 * i + 1, 1, i, i + 1, True, True)
                step_ctx(2 * i + 2, 0, i + 1, i + 1, True, True)
            step_ctx(B - 3, 1, (B - 3) // 2, 0, True, True)
            step_ctx(B - 2, 0, (B - 2) // 2, 0, True, False)
            step_ctx(B - 1, 1, (B - 1) // 2, 0, False, False)
            for k in range(2):
                sp.wait_ge(stored[k], 32 * (B // 2))

        @block.scalar
        def _(act):
            for n, w in enumerate((wk, wv)):
                act.wait_ge(w_in[n], 16)
                nc.scalar.activation(w[:, :, 0, :], wst[:], ACT.Copy, scale=WS).then_inc(w_hi, 1)

            def unit(G, par, u):
                for what, kt in unit_work(u):
                    n = AT[what, kt]
                    if what == "keys":
                        continue
                    act.wait_ge(s["work_done"], NW * G + n + 1)
                    bank = ps_w[n % 2]
                    if what == "ctx":
                        out, src = cTh[:, kt % 2], bank[:, 0:KC * KP].rearrange("p (c k) -> p c k", k=KP)
                    elif what == "vals":
                        out, src = vh[:, par, kt], bank[0:KP, :]
                    else:
                        out = kTh[:, par, :, kt * KP:(kt + 1) * KP]
                        src = bank[:, 0:NKV * KP].rearrange("p (h k) -> p h k", k=KP)
                    nc.scalar.activation(out, src, ACT.Copy).then_inc(s["work_hi"], 1)

            for u in range(-1, KT + 2):
                unit(0, 0, u)

            def step(g_, par, half, nxt, produce):
                for what, r, gr in ORDER:
                    R = NR * g_ + r
                    if what == "scores":
                        act.wait_ge(s["nmax_ready"], R + 1)
                        nc.scalar.activation(pr[:, r % 2], pr[:, r % 2], ACT.Exp, scale=-1.0,
                                             bias=nmax[:, par, r:r + 1], accum_out=rsum[:, par, r:r + 1]).then_inc(s["exp_done"], 1)
                    elif what == "turn":
                        q = 3 * r + gr
                        act.wait_ge(s["turn_done"], 3 * NR * g_ + q + 1)
                        nc.scalar.activation(pTh[:, r % 2, 4 * gr:4 * gr + 4].rearrange("p k c -> p (k c)"),
                                             ps_t[q % 2][0:KP, :], ACT.Copy).then_inc(s["turn_hi"], 1)
                    elif what == "values" and gr == 2:
                        if r == 0:
                            act.wait_ge(s["ot_free"], g_ + 1)
                        act.wait_ge(s["inv_ready"], R + 1)
                        act.wait_ge(s["values_done"], R + 1)
                        nc.scalar.activation(ot[:, par, r], ps_o[:], ACT.Copy,
                                             scale=inv[:, par, r:r + 1]).then_inc(s["o_taken"], 1)
                    elif what == "unit" and produce:
                        unit(g_ + 1, 1 - par, r)

            steps(act, step)

        @block.vector
        def _(dve):
            nc.vector.memset(mask[:], 0.0).then_inc(s["own"], 1)
            for n, w in enumerate((wk, wv)):
                dve.wait_ge(w_hi, n + 1)
                nc.vector.scalar_tensor_tensor(w[:, :, 1, :], wst[:], WS, w[:, :, 0, :], ALU.mult,
                                               ALU.subtract).then_inc(w_lo, 1)
            dve.wait_ge(b_in, 48)

            def ssq(G, kt):
                dve.wait_ge(s["k_squared"], KT * G + kt + 1)
                wait(dve, s["k_normed"], KT * G + kt - 1)
                nc.vector.tensor_reduce(ssk[:, kt % 2], ksq[:, kt % 2].rearrange("p (h d) -> p h d", d=HD),
                                        AX.X, ALU.add).then_inc(s["k_ssq"], 1)

            def unit(G, par, u):
                if 0 <= u - 1 < KT:
                    ssq(G, u - 1)
                for what, kt in unit_work(u):
                    n = AT[what, kt]
                    bank = ps_w[n % 2]
                    if what == "keys":
                        dve.wait_ge(s["work_done"], NW * G + n + 1)
                        ins = nc.vector.scalar_tensor_tensor(kb[:, kt % 4], bank[0:KP, :], 1 / WS, bk[:], ALU.mult,
                                                             ALU.add)
                    else:
                        dve.wait_ge(s["work_hi"], NHI * G + HI[what, kt] + 1)
                        if what == "ctx":
                            out, hi = cTl[:, kt % 2], cTh[:, kt % 2]
                            src = bank[:, 0:KC * KP].rearrange("p (c k) -> p c k", k=KP)
                        elif what == "vals":
                            out, hi, src = vl[:, par, kt], vh[:, par, kt], bank[0:KP, :]
                        else:
                            cols = slice(kt * KP, (kt + 1) * KP)
                            out, hi = kTl[:, par, :, cols], kTh[:, par, :, cols]
                            src = bank[:, 0:NKV * KP].rearrange("p (h k) -> p h k", k=KP)
                        ins = nc.vector.tensor_tensor(out, src, hi, ALU.subtract)
                    ins.then_inc(s["work_taken"], 1)

            for u in range(-1, KT + 2):
                unit(0, 0, u)

            def step(g_, par, half, nxt, produce):
                for what, r, gr in ORDER:
                    R = NR * g_ + r
                    if what == "scores":
                        dve.wait_ge(s["scores_done"], R + 1)
                        passed(dve, gate)
                        nc.vector.tensor_tensor_reduce(
                            out=pr[:, r % 2].rearrange("p (a k) -> p a k", k=500), in0=ps_s[:, :, 0:500],
                            in1=mask[:].rearrange("p (a k) -> p a k", k=500), scale=-1.0, scalar=3.0e38,
                            op0=ALU.add, op1=ALU.min, accum_out=nmax[:, par, r:r + 1]).then_inc(s["nmax_ready"], 1)
                    elif what == "turn":
                        q = 3 * r + gr
                        if gr == 0:
                            dve.wait_ge(s["exp_done"], R + 1)
                            nc.vector.tensor_scalar(inv[:, par, r:r + 1], rsum[:, par, r:r + 1], WS, None,
                                                    ALU.mult).then_inc(s["inv_scaled"], 1)
                            dve.wait_ge(s["inv_scaled"], R + 1)
                            nc.vector.reciprocal(inv[:, par, r:r + 1], inv[:, par, r:r + 1]).then_inc(s["inv_ready"], 1)
                        dve.wait_ge(s["turn_hi"], 3 * NR * g_ + q + 1)
                        part = (slice(None), r % 2, slice(4 * gr, 4 * gr + 4))
                        nc.vector.tensor_tensor(pTl[part].rearrange("p k c -> p (k c)"), ps_t[q % 2][0:KP, :],
                                                pTh[part].rearrange("p k c -> p (k c)"),
                                                ALU.subtract).then_inc(s["turn_lo"], 1)
                    elif what == "unit" and produce:
                        unit(g_ + 1, 1 - par, r)

            steps(dve, step)

        @block.gpsimd
        def _(pool):
            def unit(G, u):
                if 0 <= u - 1 < KT:
                    kt = u - 1
                    pool.wait_ge(s["k_ssq"], KT * G + kt + 1)
                    passed(pool, pool_gate)
                    nc.gpsimd.tensor_scalar(rk[:, kt % 2, 0], ssk[:, kt % 2], 1.0 / HD, RMS_EPS, ALU.mult,
                                            ALU.add).then_inc(pool_own, 1)
                    pool.wait_ge(pool_own, 2 * (KT * G + kt) + 1)
                    nc.gpsimd.tensor_tensor(rk[:, kt % 2, 1], rk[:, kt % 2, 0], g.mhalf[0:KP, 0:NKV],
                                            ALU.pow).then_inc(pool_own, 1)
                    pool.wait_ge(pool_own, 2 * (KT * G + kt) + 2)
                    k4 = kb[:, kt % 4].rearrange("p (h d) -> p h d", d=HD)
                    nc.gpsimd.tensor_tensor(k4, k4, rk[:, kt % 2, 1].unsqueeze(2).to_broadcast([KP, NKV, HD]),
                                            ALU.mult).then_inc(s["k_normed"], 1)
                if 0 <= u < KT:
                    pool.wait_ge(s["work_taken"], NW * G + AT["keys", u] + 1)
                    wait(pool, s["k_ssq"], KT * G + u - 1)
                    nc.gpsimd.tensor_tensor(ksq[:, u % 2], kb[:, u % 4], kb[:, u % 4],
                                            ALU.mult).then_inc(s["k_squared"], 1)

            for u in range(-1, KT + 2):
                unit(0, u)
            with pool.Fori(1, B) as G:
                for u in range(-1, KT + 2):
                    unit(G, u)

        @block.tensor
        def _(pe):
            pe.wait_ge(w_lo, 2)

            def unit(G, par, u, half):
                for what, kt in unit_work(u):
                    n = AT[what, kt]
                    bank = ps_w[n % 2]
                    wait(pe, s["work_taken"], NW * G + n - 1)
                    if what == "ctx":
                        if kt == 0:
                            pe.wait_ge(ctx_in[par], 32 * half + 32)
                        for c in range(KC):
                            last = nc.tensor.transpose(bank[:, c * KP:(c + 1) * KP],
                                                       cx[:, par, kt, c * 128:(c + 1) * 128],
                                                       g.ident[0:KP, 0:KP])
                    elif what in ("keys", "vals"):
                        pe.wait_ge(s["work_taken"], NW * G + AT["ctx", kt] + 1)
                        w = wk if what == "keys" else wv
                        for c in range(KC):
                            last = three_products(nc, bank[0:KP, :], cTh[:, kt % 2, c], cTl[:, kt % 2, c],
                                                  w[:, c, 0], w[:, c, 1], start=(c == 0), stop=(c == KC - 1))
                    else:
                        pe.wait_ge(s["k_normed"], KT * G + kt + 1)
                        for h in range(NKV):
                            last = nc.tensor.transpose(bank[:, h * KP:(h + 1) * KP],
                                                       kb[:, kt % 4, h * HD:(h + 1) * HD], g.ident[0:KP, 0:KP])
                    last.then_inc(s["work_done"], 1)

            for u in range(-1, KT + 2):
                unit(0, 0, u, 0)

            def step(g_, par, half, nxt, produce):
                for what, r, gr in ORDER:
                    R = NR * g_ + r
                    kv = r // 2
                    if what == "scores":
                        if r == 0:
                            pe.wait_ge(q_in[par], 32 * half + 32)
                            pe.wait_ge(s["work_taken"], NW * g_ + NW)
                        wait(pe, s["nmax_ready"], R)
                        for j in range(3):
                            cols = slice(500 * j, 500 * j + 500)
                            last = three_products(nc, ps_s[:, j, 0:500], qh[:, par, r], ql[:, par, r],
                                                  kTh[:, par, kv, cols], kTl[:, par, kv, cols], True, True)
                        last.then_inc(s["scores_done"], 1)
                    elif what == "turn":
                        q = 3 * r + gr
                        if gr == 0:
                            pe.wait_ge(s["exp_done"], R + 1)
                        wait(pe, s["turn_lo"], 3 * NR * g_ + q - 1)
                        for j in range(4):
                            kt = 4 * gr + j
                            last = nc.tensor.transpose(ps_t[q % 2][0:KP, 128 * j:128 * j + 128],
                                                       pr[:, r % 2, kt * KP:(kt + 1) * KP], g.ident[:])
                        last.then_inc(s["turn_done"], 1)
                    elif what == "values":
                        if gr == 0:
                            wait(pe, s["o_taken"], R)
                        pe.wait_ge(s["turn_lo"], 3 * NR * g_ + 3 * r + gr + 1)
                        for kt in range(4 * gr, 4 * gr + 4):
                            cols = slice(kv * HD, (kv + 1) * HD)
                            last = three_products(nc, ps_o[:], pTh[:, r % 2, kt], pTl[:, r % 2, kt],
                                                  vh[:, par, kt, cols], vl[:, par, kt, cols],
                                                  start=(kt == 0), stop=(kt == KT - 1))
                        if gr == 2:
                            last.then_inc(s["values_done"], 1)
                    elif produce:
                        unit(g_ + 1, 1 - par, r, nxt)

            steps(pe, step)


def mix0_phase(nc, g, io):
    with phase(nc) as (ctx, a):
        wst = a.sb("m_wst", [128, 4, H])
        wo = a.sb("m_wo", [128, 2, NH, H], F16)
        gst = a.sb("m_gst", [128, KC, NE])
        gw = a.sb("m_gw", [128, 2, KC, NE], F16)
        bv = a.sb("m_bv", [128, NKV])
        ot = a.sb("m_ot", [TT, 2, NH * HD])
        xt = a.sb("m_x", [TT, 2, H])
        oTh = a.sb("m_oTh", [128, NH, TT], F16)
        oTl = a.sb("m_oTl", [128, NH, TT], F16)
        st6 = a.sb("m_st6", [TT, 6])
        mv = a.sb("m_mv", [TT, 2])
        ve = a.sb("m_ve", [TT, 1])
        rs = a.sb("m_rs", [TT, 1])
        xn = a.sb("m_xn", [TT, H])
        cur = a.sb("m_cur", [128, 2, KC, TT], F16)
        lg = a.sb("m_lg", [TT, NT, NE])
        sc = a.sb("m_sc", [TT, NT, NE])
        gm = a.sb("m_gm", [TT, NT, 16])
        g8 = a.sb("m_g8", [TT, NT, 8])
        gr = a.sb("m_gr", [TT, NT, 16])
        gk = a.sb("m_gk", [TT, NT, 2, NG])
        ms = a.sb("m_ms", [TT, NT, NE + 8])
        er = a.sb("m_er", [TT, NT, NE + 8])
        sm = a.sb("m_sm", [TT, NT])
        pT = [a.ps(f"m_pT{i}", [128, 512]) for i in range(4)]
        pY = a.ps("m_pY", [128, 512])
        pX = a.ps("m_pX", [128, 512])
        pL = a.ps("m_pL", [128, 512])
        w_in = [a.sem(f"m_w_in{i}") for i in range(4)]
        b_in, g_in, gate = a.sem("m_b_in"), a.sem("m_g_in"), a.sem("m_gate")
        o_in = [a.sem(f"m_o_in{i}") for i in range(2)]
        names = ("w_hi w_lo g_hi oT_done oT_hi oT_lo y_done x_ready var rstd xn_ready xT_done xT_hi xT_lo kept "
                 "lg_done lg_taken dve exp")
        s = {n: a.sem("m_" + n) for n in names.split()}
        block = ctx.enter_context(nc.Block())

        @block.sync
        def _(sp):
            sp.dma_start(gst[:], io.gate_w.rearrange("(c p) n -> p c n", p=128)).then_inc(g_in, 16)
            with nc.allow_non_contiguous_dma(reason="512 values"):
                sp.dma_start(bv[:], io.bv.rearrange("(h p) -> p h", p=128)).then_inc(b_in, 16)
            for n in range(4):
                wait(sp, s["w_lo"], n)
                sp.dma_start(wst[:], io.Wo[512 * n:512 * n + 512, :].rearrange("(h p) n -> p h n", p=128))\
                    .then_inc(w_in[n], 16)
            def pair(i):
                for k in range(2):
                    t = 2 * i + k
                    wait(sp, s["x_ready"], t)
                    sp.dma_start(ot[:, k, :], io.o0[ds(t * TT, TT), :]).then_inc(o_in[k], 16)
                    sp.dma_start(xt[:, k, :], io.x[ds(t * TT, TT), :]).then_inc(o_in[k], 16)

            each(sp, NT // 2, pair)

        @block.gpsimd
        def _(pool):
            def tile(t):
                pool.wait_ge(s["var"], t + 1)
                nc.gpsimd.tensor_tensor(rs[:], ve[:], g.mhalf[0:TT, 0:1], ALU.pow).then_inc(s["rstd"], 1)
                pool.wait_ge(s["xT_lo"], t + 1)
                for n in range(2):
                    nc.gpsimd.tensor_copy(g.xT[:, n, :, ds(t * TT, TT)], cur[:, n]).then_inc(s["kept"], 1)

            each(pool, NT, tile)

        @block.scalar
        def _(act):
            act.wait_ge(g_in, 16)
            nc.scalar.activation(gw[:, 0], gst[:], ACT.Copy, scale=WS).then_inc(s["g_hi"], 1)
            for n in range(4):
                act.wait_ge(w_in[n], 16)
                nc.scalar.activation(wo[:, 0, 4 * n:4 * n + 4], wst[:], ACT.Copy, scale=WS).then_inc(s["w_hi"], 1)
            act.wait_ge(b_in, 16)
            def tile(t):
                for j in range(4):
                    act.wait_ge(s["oT_done"], 4 * t + j + 1)
                    nc.scalar.activation(oTh[:, 4 * j:4 * j + 4].rearrange("p h q -> p (h q)"), pT[j][:, 0:4 * TT],
                                         ACT.Identity, bias=bv[:, j:j + 1]).then_inc(s["oT_hi"], 1)
                act.wait_ge(s["xT_done"], t + 1)
                wait(act, s["kept"], 2 * t)
                nc.scalar.activation(cur[:, 0], pX[:, 0:KC * TT].rearrange("p (c q) -> p c q", q=TT),
                                     ACT.Copy).then_inc(s["xT_hi"], 1)
                act.wait_ge(s["lg_done"], t + 1)
                nc.scalar.activation(lg[:, ds(t, 1), :].rearrange("p a n -> p (a n)"), pL[0:TT, 0:NE],
                                     ACT.Copy).then_inc(s["lg_taken"], 1)

            each(act, NT, tile)
            act.wait_ge(s["lg_taken"], NT)
            nc.scalar.activation(sc[:], lg[:], ACT.Exp, scale=-1.0 / WS).then_inc(s["exp"], 1)

        @block.vector
        def _(dve):
            own = Counted(dve, s["dve"])
            own(nc.vector.memset(gm[:], -5.0))
            own(nc.vector.memset(ms[:], -5.0))
            dve.wait_ge(s["g_hi"], 1)
            own(nc.vector.scalar_tensor_tensor(gw[:, 1], gst[:], WS, gw[:, 0], ALU.mult, ALU.subtract))
            for n in range(4):
                dve.wait_ge(s["w_hi"], n + 1)
                nc.vector.scalar_tensor_tensor(wo[:, 1, 4 * n:4 * n + 4], wst[:], WS, wo[:, 0, 4 * n:4 * n + 4],
                                               ALU.mult, ALU.subtract).then_inc(s["w_lo"], 1)
            base = own.n
            def pair(i):
                for k in range(2):
                    t = 2 * i + k
                    for j in range(4):
                        dve.wait_ge(s["oT_hi"], 4 * t + j + 1)
                        part = oTh[:, 4 * j:4 * j + 4].rearrange("p h q -> p (h q)")
                        nc.vector.scalar_tensor_tensor(oTl[:, 4 * j:4 * j + 4].rearrange("p h q -> p (h q)"),
                                                       pT[j][:, 0:4 * TT], bv[:, j:j + 1], part, ALU.add,
                                                       ALU.subtract).then_inc(s["oT_lo"], 1)
                    dve.wait_ge(o_in[k], 32 * i + 32)
                    dve.wait_ge(s["y_done"], t + 1)
                    xrow = g.xs[:, ds(t, 1), :].rearrange("p a n -> p (a n)")
                    nc.vector.scalar_tensor_tensor(xrow, pY[0:TT, 0:H], 1 / WS, xt[:, k], ALU.mult,
                                                   ALU.add).then_inc(s["x_ready"], 1)
                    dve.wait_ge(s["x_ready"], t + 1)
                    passed(dve, gate)
                    nc.vector.bn_stats(st6[:], xrow).then_inc(s["dve"], 1)
                    dve.wait_ge(s["dve"], base + 2 * t + 1)
                    passed(dve, gate)
                    nc.vector.bn_aggr(mv[:], st6[:]).then_inc(s["dve"], 1)
                    dve.wait_ge(s["dve"], base + 2 * t + 2)
                    nc.vector.tensor_scalar(ve[:], mv[:, 1:2], LN_EPS, None, ALU.add).then_inc(s["var"], 1)
                    dve.wait_ge(s["rstd"], t + 1)
                    nc.vector.tensor_scalar(xn[:], xrow, mv[:, 0:1], rs[:], ALU.subtract,
                                            ALU.mult).then_inc(s["xn_ready"], 1)
                    dve.wait_ge(s["xT_hi"], t + 1)
                    nc.vector.tensor_tensor(cur[:, 1], pX[:, 0:KC * TT].rearrange("p (c q) -> p c q", q=TT),
                                            cur[:, 0], ALU.subtract).then_inc(s["xT_lo"], 1)

            each(dve, NT // 2, pair)
            own.n = base + 2 * NT
            dve.wait_ge(s["exp"], 1)
            own(nc.vector.tensor_scalar(sc[:], sc[:], 1.0, None, ALU.add)).done()
            own(nc.vector.reciprocal(sc[:], sc[:])).done()
            own(nc.vector.tensor_reduce(gm[:, :, 0:NG], sc[:].rearrange("p t (g e) -> p t g e", e=EPG), AX.X,
                                        ALU.max)).done()
            for t in range(NT):
                own(nc.vector.max(g8[:, t], gm[:, t]))
            own.done()
            own(nc.vector.memset(g8[:, :, TOPG:8], -5.0)).done()
            for t in range(NT):
                own(nc.vector.match_replace(out=gr[:, t], in_to_replace=g8[:, t], in_values=gm[:, t], imm_value=9.0))
            own.done()
            own(nc.vector.tensor_scalar(gk[:, :, 0], gr[:, :, 0:NG], 9.0, None, ALU.is_equal)).done()
            own(nc.vector.tensor_scalar(gk[:, :, 1], gk[:, :, 0], 1.0, None, ALU.subtract)).done()
            for e in range(NG):
                cols = slice(EPG * e, EPG * e + EPG)
                own(nc.vector.tensor_tensor(ms[:, :, cols], sc[:, :, cols],
                                            gk[:, :, 0, e:e + 1].to_broadcast([TT, NT, EPG]), ALU.mult))
            own.done()
            for e in range(NG):
                cols = slice(EPG * e, EPG * e + EPG)
                own(nc.vector.tensor_tensor(ms[:, :, cols], ms[:, :, cols],
                                            gk[:, :, 1, e:e + 1].to_broadcast([TT, NT, EPG]), ALU.add))
            own.done()
            for t in range(NT):
                own(nc.vector.max(g8[:, t], ms[:, t]))
            own.done()
            own(nc.vector.memset(g8[:, :, TOPK:8], -5.0)).done()
            for t in range(NT):
                own(nc.vector.match_replace(out=er[:, t], in_to_replace=g8[:, t], in_values=ms[:, t], imm_value=9.0))
            own.done()
            own(nc.vector.tensor_scalar(er[:, :, 0:NE], er[:, :, 0:NE], 9.0, None, ALU.is_equal)).done()
            own(nc.vector.tensor_tensor(er[:, :, 0:NE], er[:, :, 0:NE], sc[:], ALU.mult)).done()
            own(nc.vector.tensor_reduce(sm[:], er[:, :, 0:NE], AX.X, ALU.add)).done()
            own(nc.vector.tensor_scalar(sm[:], sm[:], WS, None, ALU.mult)).done()
            own(nc.vector.reciprocal(sm[:], sm[:])).done()
            own(nc.vector.tensor_tensor(g.comb[:, :, 0:NE], er[:, :, 0:NE],
                                        sm[:].unsqueeze(2).to_broadcast([TT, NT, NE]), ALU.mult))
            own(nc.vector.memset(g.comb[:, :, NE:NX], 1.0 / WS)).done()

        @block.tensor
        def _(pe):
            pe.wait_ge(s["w_lo"], 4)
            pe.wait_ge(s["dve"], 3)
            def pair(i):
                for k in range(2):
                    t = 2 * i + k
                    pe.wait_ge(o_in[k], 32 * i + 32)
                    for j in range(4):
                        wait(pe, s["oT_lo"], 4 * t)
                        for h in range(4):
                            last = nc.tensor.transpose(pT[j][:, h * TT:(h + 1) * TT],
                                                       ot[:, k, (4 * j + h) * HD:(4 * j + h + 1) * HD],
                                                       g.ident[0:TT, 0:TT])
                        last.then_inc(s["oT_done"], 1)
                    wait(pe, s["x_ready"], t)
                    for j in range(4):
                        pe.wait_ge(s["oT_lo"], 4 * t + j + 1)
                        for h in range(4 * j, 4 * j + 4):
                            last = three_products(nc, pY[0:TT, 0:H], oTh[:, h], oTl[:, h], wo[:, 0, h], wo[:, 1, h],
                                                  start=(h == 0), stop=(h == NH - 1))
                    last.then_inc(s["y_done"], 1)
                    pe.wait_ge(s["xn_ready"], t + 1)
                    for c in range(KC):
                        last = nc.tensor.transpose(pX[:, c * TT:(c + 1) * TT], xn[:, c * 128:(c + 1) * 128],
                                                   g.ident[0:TT, 0:TT])
                    last.then_inc(s["xT_done"], 1)
                    pe.wait_ge(s["xT_lo"], t + 1)
                    wait(pe, s["lg_taken"], t)
                    for c in range(KC):
                        last = three_products(nc, pL[0:TT, 0:NE], cur[:, 0, c], cur[:, 1, c], gw[:, 0, c], gw[:, 1, c],
                                              start=(c == 0), stop=(c == KC - 1))
                    last.then_inc(s["lg_done"], 1)

            each(pe, NT // 2, pair)


def experts_phase(nc, g, io):
    NC4 = 4
    TC = TOK // NC4
    SUB = TC // TT
    with phase(nc) as (ctx, a):
        stg = a.sb("e_stg", [128, 2, KC, 2, M])
        std = a.sb("e_std", [128, 2, 2, H])
        wg = a.sb("e_wg", [128, 2, 2, KC, 384], F16)
        wd = a.sb("e_wd", [128, 2, 2, 2, H], F16)
        sg = a.sb("e_sg", [128, 2, 2, TC])
        hb = a.sb("e_h", [128, 2, 2, TC])
        hh = a.sb("e_hh", [128, 2, 2, TC], F16)
        hl = a.sb("e_hl", [128, 2, 2, TC], F16)
        ps = [[a.ps(f"e_p{n}{i}", [128, 512]) for n in "abc"] for i in range(2)]
        pd = [a.ps(f"e_pd{i}", [128, 2, H]) for i in range(2)]
        w_in = [a.sem(f"e_w_in{i}") for i in range(2)]
        names = "cleared w_hi w_lo up_done sg_ready h_ready h_hi h_lo down_done acc"
        s = {n: a.sem("e_" + n) for n in names.split()}
        block = ctx.enter_context(nc.Block())
        ND = 2 * NC4

        def steps(eng, step):
            step(0, 0, 0, 0)
            with eng.Fori(0, (NE - 2) // 2) as i:
                step(2 * i + 1, 1, i, i + 1)
                step(2 * i + 2, 0, i + 1, i + 1)
            for e in range(NE - 1, NX):
                step(e, e % 2, e // 2, (e + 1) // 2)

        @block.sync
        def _(sp):
            sp.wait_ge(s["cleared"], 4)

            def load(e, par, shared=None):
                if shared is None:
                    srcs = [t[ds(e, 1), :, :].rearrange("a p n -> (a p) n") for t in (io.w_gate, io.w_up, io.w_down)]
                else:
                    part = slice(shared * M, shared * M + M)
                    srcs = [io.sw_gate[:, part], io.sw_up[:, part], io.sw_down[part, :]]
                for n in range(2):
                    sp.dma_start(stg[:, par, :, n, :], srcs[n].rearrange("(c p) m -> p c m", p=128))\
                        .then_inc(w_in[par], 16)
                sp.dma_start(std[:, par, 0, :], srcs[2][0:128]).then_inc(w_in[par], 16)
                sp.dma_start(std[64:64 + MT, par, 1, :], srcs[2][128:M]).then_inc(w_in[par], 16)

            load(0, 0)
            load(1, 1)
            with sp.Fori(0, (NE - 2) // 2) as i:
                for k in range(2):
                    sp.wait_ge(s["w_lo"], 5 * (2 * i + k) + 5)
                    load(2 * i + k + 2, k)
            for n in range(2):
                sp.wait_ge(s["w_lo"], 5 * (NE - 2 + n) + 5)
                load(0, n, shared=n)

        @block.gpsimd
        def _(pool):
            for t in (wg, std, hb, sg):
                nc.gpsimd.memset(t[:], 0.0).then_inc(s["cleared"], 1)

            def step(e, par, half, nxt):
                for c in range(NC4):
                    n = NC4 * e + c
                    pool.wait_ge(s["h_hi"], n + 1)
                    nc.gpsimd.tensor_tensor(hl[:, c % 2], hb[:, c % 2], hh[:, c % 2],
                                            ALU.subtract).then_inc(s["h_lo"], 1)

            with pool.Fori(0, NX) as e:
                step(e, 0, 0, 0)

        def main(t, par, c, n):
            return t[:, par, n, c, 0:256].rearrange("p (u m) -> p u m", m=128)

        def tail(t, par, c, n):
            return t[:, par, n, c, 256:384].rearrange("p (u m) -> p u m", m=64)[:, :, 0:MT]

        @block.scalar
        def _(act):
            act.wait_ge(s["cleared"], 4)

            def split(par, half, e):
                act.wait_ge(w_in[par], 64 * half + 64)
                for c in range(KC):
                    nc.scalar.activation(main(wg, par, c, 0), stg[:, par, c, :, 0:128], ACT.Copy,
                                         scale=WS).then_inc(s["w_hi"], 1)
                    nc.scalar.activation(tail(wg, par, c, 0), stg[:, par, c, :, 128:M], ACT.Copy,
                                         scale=WS).then_inc(s["w_hi"], 1)
                nc.scalar.activation(wd[:, par, 0], std[:, par], ACT.Copy, scale=WS).then_inc(s["w_hi"], 1)

            split(0, 0, 0)

            def step(e, par, half, nxt):
                for c in range(NC4):
                    n = NC4 * e + c
                    act.wait_ge(s["up_done"], n + 1)
                    nc.scalar.activation(sg[:, c % 2, 0], ps[c % 2][0][:, 0:TC], ACT.Silu,
                                         scale=1 / WS).then_inc(s["sg_ready"], 1)
                    nc.scalar.activation(sg[64:64 + MT, c % 2, 1], ps[c % 2][2][0:MT, 0:TC], ACT.Silu,
                                         scale=1 / WS).then_inc(s["sg_ready"], 1)
                    if c == 1 and not (isinstance(e, int) and e == NX - 1):
                        wait(act, s["down_done"], ND * e)
                        split(1 - par, nxt, e + 1)
                    act.wait_ge(s["h_ready"], 2 * n + 2)
                    nc.scalar.activation(hh[:, c % 2], hb[:, c % 2], ACT.Copy).then_inc(s["h_hi"], 1)

            steps(act, step)

        @block.vector
        def _(dve):
            def split(par, e):
                at = 0
                for c in range(KC):
                    for part, cols in ((main, slice(0, 128)), (tail, slice(128, M))):
                        at += 1
                        dve.wait_ge(s["w_hi"], 5 * e + at)
                        nc.vector.scalar_tensor_tensor(part(wg, par, c, 1), stg[:, par, c, :, cols], WS,
                                                       part(wg, par, c, 0), ALU.mult,
                                                       ALU.subtract).then_inc(s["w_lo"], 1)
                dve.wait_ge(s["w_hi"], 5 * e + 5)
                nc.vector.scalar_tensor_tensor(wd[:, par, 1], std[:, par], WS, wd[:, par, 0], ALU.mult,
                                               ALU.subtract).then_inc(s["w_lo"], 1)

            dve.wait_ge(s["cleared"], 4)
            split(0, 0)

            def accumulate(e, c):
                for i in range(2):
                    dve.wait_ge(s["down_done"], ND * e + 2 * c + i + 1)
                    for j in range(2):
                        t = SUB * c + 2 * i + j
                        w = g.comb[:, t, ds(e, 1)]
                        last = nc.vector.scalar_tensor_tensor(g.xs[:, t], pd[i][0:TT, j], w, g.xs[:, t], ALU.mult,
                                                              ALU.add)
                    last.then_inc(s["acc"], 1)

            def step(e, par, half, nxt):
                for c in range(NC4):
                    n = NC4 * e + c
                    wait(dve, s["h_lo"], n - 1)
                    dve.wait_ge(s["sg_ready"], 2 * n + 1)
                    nc.vector.scalar_tensor_tensor(hb[:, c % 2, 0], ps[c % 2][1][:, 0:TC], 1 / WS, sg[:, c % 2, 0],
                                                   ALU.mult, ALU.mult).then_inc(s["h_ready"], 1)
                    dve.wait_ge(s["sg_ready"], 2 * n + 2)
                    nc.vector.scalar_tensor_tensor(hb[64:64 + MT, c % 2, 1], ps[c % 2][2][64:64 + MT, 0:TC], 1 / WS,
                                                   sg[64:64 + MT, c % 2, 1], ALU.mult,
                                                   ALU.mult).then_inc(s["h_ready"], 1)
                    if c:
                        accumulate(e, c - 1)
                    elif not (isinstance(e, int) and e == 0):
                        accumulate(e - 1, NC4 - 1)
                    if c == 1 and not (isinstance(e, int) and e == NX - 1):
                        split(1 - par, e + 1)

            steps(dve, step)
            accumulate(NX - 1, NC4 - 1)

        @block.tensor
        def _(pe):
            def down(e, par, c):
                n = NC4 * e + c
                pe.wait_ge(s["h_lo"], n + 1)
                for i in range(2):
                    wait(pe, s["acc"], ND * e + 2 * c + i - 1)
                    for j in range(2):
                        cols = slice((2 * i + j) * TT, (2 * i + j + 1) * TT)
                        for k in range(2):
                            last = three_products(nc, pd[i][0:TT, j], hh[:, c % 2, k, cols], hl[:, c % 2, k, cols],
                                                  wd[:, par, 0, k], wd[:, par, 1, k], start=(k == 0), stop=(k == 1))
                    last.then_inc(s["down_done"], 1)

            def step(e, par, half, nxt):
                for c in range(NC4):
                    n = NC4 * e + c
                    if c == 0:
                        pe.wait_ge(s["w_lo"], 5 * e + 5)
                    wait(pe, s["h_ready"], 2 * (n - 1))
                    cols = slice(c * TC, (c + 1) * TC)
                    for b in range(3):
                        for k in range(KC):
                            m = slice(128 * b, 128 * b + 128)
                            last = three_products(nc, ps[c % 2][b][:, 0:TC], wg[:, par, 0, k, m], wg[:, par, 1, k, m],
                                                  g.xT[:, 0, k, cols], g.xT[:, 1, k, cols],
                                                  start=(k == 0), stop=(k == KC - 1))
                    last.then_inc(s["up_done"], 1)
                    if c:
                        down(e, par, c - 1)
                    elif not (isinstance(e, int) and e == 0):
                        down(e - 1, 1 - par, NC4 - 1)

            steps(pe, step)
            down(NX - 1, (NX - 1) % 2, NC4 - 1)


def q1_phase(nc, g, io):
    with phase(nc) as (ctx, a):
        wst = a.sb("r_wst", [128, KC, H])
        bq = a.sb("r_bq", [TT, H])
        wT = a.sb("r_wT", [128, 2, KC, H], F16)
        wn = a.sb("r_wn", [128, KC, H])
        wa = a.sb("r_wa", [128, 2, KC])
        pm = a.sb("r_pm", [128, 2])
        st6 = a.sb("r_st6", [TT, 6])
        mv = a.sb("r_mv", [TT, 2])
        ve = a.sb("r_ve", [TT, 1])
        rs = a.sb("r_rs", [TT, 1])
        xn = a.sb("r_xn", [TT, H])
        am = a.sb("r_am", [TT, 2])
        xq = a.sb("r_xq", [TT, H], F16)
        xT = a.sb("r_xT", [128, KC, TT], F16)
        qb = a.sb("r_qb", [TT, H])
        bd = a.sb("r_bd", [128, 2, 2, 2, KC, 2, HP], F16)
        pW = [a.ps(f"r_pW{i}", [128, 512]) for i in range(2)]
        pX = a.ps("r_pX", [128, KC, TT], F16)
        pQ = a.ps("r_pQ", [128, 512])
        pT = a.ps("r_pT", [128, KC, TT])
        w_in, b_in, gate = a.sem("r_w_in"), a.sem("r_b_in"), a.sem("r_gate")
        out_done = [a.sem(f"r_out{i}") for i in range(2)]
        at = {}
        names = "dve wT_done wT_hi pads var rstd xq_ready xT_done xT_taken q_done q_ready qT_done qT_hi qT_lo"
        s = {n: a.sem("r_" + n) for n in names.split()}
        block = ctx.enter_context(nc.Block())

        @block.sync
        def _(sp):
            sp.dma_start(wst[:], io.wq.rearrange("(c p) n -> p c n", p=128)).then_inc(w_in, 16)
            sp.dma_start(bq[:], io.bq1.rearrange("(a n) -> a n", a=1).to_broadcast([TT, H])).then_inc(b_in, 16)
            def pair(i):
                for k in range(2):
                    t = 2 * i + k
                    sp.wait_ge(s["qT_lo"], 4 * t + 4)
                    for b in range(2):
                        sp.dma_start(io.q1[ds(2 * t + b, 1)].rearrange("a h p k c -> p (a h) (k c)"),
                                     bd[:, k, b].rearrange("p h k e q -> p h (k e q)")).then_inc(out_done[k], 16)

            each(sp, NT // 2, pair)
            for k in range(2):
                sp.wait_ge(out_done[k], 32 * (NT // 2))

        @block.gpsimd
        def _(pool):
            nc.gpsimd.memset(bd[:], 0.0).then_inc(s["pads"], 1)
            def tile(t):
                pool.wait_ge(s["var"], t + 1)
                nc.gpsimd.tensor_tensor(rs[:], ve[:], g.mhalf[0:TT, 0:1], ALU.pow).then_inc(s["rstd"], 1)

            each(pool, NT, tile)

        @block.scalar
        def _(act):
            for c in range(KC):
                act.wait_ge(s["wT_done"], c + 1)
                nc.scalar.activation(wT[:, 0, c], pW[c][:, 0:H], ACT.Copy).then_inc(s["wT_hi"], 1)
            act.wait_ge(s["pads"], 1)
            def pair(i):
                for k in range(2):
                    t = 2 * i + k
                    act.wait_ge(s["xT_done"], t + 1)
                    nc.scalar.activation(xT[:], pX[:], ACT.Copy).then_inc(s["xT_taken"], 1)
                    act.wait_ge(s["qT_done"], t + 1)
                    wait(act, out_done[k], 32 * i)
                    for e in range(2):
                        nc.scalar.activation(bd[:, k, :, 0, :, e, 0:S].rearrange("p b k q -> p k b q"),
                                             pT[:].rearrange("p k (b q) -> p k b q", b=2), ACT.Copy,
                                             scale=pm[:, e:e + 1]).then_inc(s["qT_hi"], 1)

            each(act, NT // 2, pair)

        @block.vector
        def _(dve):
            own = Counted(dve, s["dve"])
            own(nc.vector.tensor_scalar(pm[:], g.evenodd[:], HD1 ** -0.5 / WS, None, ALU.mult))
            dve.wait_ge(w_in, 16)
            quantise_rows(nc, own, wst[:], wn[:], wa[:, 0], wa[:, 1], dequantise=True)
            at["wn"] = own.n
            for c in range(KC):
                dve.wait_ge(s["wT_hi"], c + 1)
                own(nc.vector.tensor_tensor(wT[:, 1, c], pW[c][:, 0:H], wT[:, 0, c], ALU.subtract))
            dve.wait_ge(b_in, 16)
            base, per, own.marks = own.n, 8, 0
            def pair(i):
                for k in range(2):
                    t = 2 * i + k
                    own.n = base + per * t
                    xrow = g.xs[:, ds(t, 1), :].rearrange("p a n -> p (a n)")
                    own(nc.vector.bn_stats(st6[:], xrow)).done()
                    passed(dve, gate)
                    own(nc.vector.bn_aggr(mv[:], st6[:])).done()
                    nc.vector.tensor_scalar(ve[:], mv[:, 1:2], LN_EPS, None, ALU.add).then_inc(s["var"], 1)
                    dve.wait_ge(s["rstd"], t + 1)
                    own(nc.vector.tensor_scalar(xn[:], xrow, mv[:, 0:1], rs[:], ALU.subtract, ALU.mult)).done()
                    own(nc.vector.tensor_reduce(am[:, 0:1], xn[:], AX.X, ALU.max, apply_absolute_value=True)).done()
                    own(nc.vector.tensor_scalar(am[:, 0:1], am[:, 0:1], 1 / 127.0, 1e-8, ALU.mult, ALU.max)).done()
                    own(nc.vector.reciprocal(am[:, 1:2], am[:, 0:1])).done()
                    own(nc.vector.tensor_scalar(xn[:], xn[:], am[:, 1:2], MAGIC, ALU.mult, ALU.add)).done()
                    own(nc.vector.tensor_scalar(xn[:], xn[:], MAGIC, 127.0, ALU.subtract, ALU.min)).done()
                    nc.vector.tensor_scalar(xq[:], xn[:], -127.0, None, ALU.max).then_inc(s["xq_ready"], 1)
                    dve.wait_ge(s["q_done"], t + 1)
                    nc.vector.scalar_tensor_tensor(qb[:], pQ[0:TT, 0:H], am[:, 0:1], bq[:], ALU.mult,
                                                   ALU.add).then_inc(s["q_ready"], 1)
                    dve.wait_ge(s["qT_hi"], 2 * t + 2)
                    for e in range(2):
                        for b in range(2):
                            nc.vector.scalar_tensor_tensor(
                                bd[:, k, b, 1, :, e, 0:S], pT[:].rearrange("p k (b q) -> p b k q", b=2)[:, b],
                                pm[:, e:e + 1], bd[:, k, b, 0, :, e, 0:S], ALU.mult,
                                ALU.subtract).then_inc(s["qT_lo"], 1)

            each(dve, NT // 2, pair)
            assert own.marks == 4 * per

        @block.tensor
        def _(pe):
            pe.wait_ge(s["dve"], at["wn"])
            for c in range(KC):
                for o in range(KC):
                    last = nc.tensor.transpose(pW[c][:, o * 128:(o + 1) * 128], wn[:, o, c * 128:(c + 1) * 128],
                                               g.ident[:])
                last.then_inc(s["wT_done"], 1)
            def tile(t):
                pe.wait_ge(s["xq_ready"], t + 1)
                for c in range(KC):
                    last = nc.tensor.transpose(pX[:, c], xq[:, c * 128:(c + 1) * 128], g.ident16[0:TT, 0:TT])
                last.then_inc(s["xT_done"], 1)
                pe.wait_ge(s["xT_taken"], t + 1)
                for c in range(KC):
                    for n in range(2):
                        last = nc.tensor.matmul(pQ[0:TT, 0:H], xT[:, c], wT[:, n, c], start=(c == 0 and n == 0),
                                                stop=(c == KC - 1 and n == 1))
                last.then_inc(s["q_done"], 1)
                pe.wait_ge(s["q_ready"], t + 1)
                for c in range(KC):
                    last = nc.tensor.transpose(pT[:, c], qb[:, c * 128:(c + 1) * 128], g.ident[0:TT, 0:TT])
                last.then_inc(s["qT_done"], 1)

            each(pe, NT, tile)


def quantise_rows(nc, own, w, out, scale, recip, dequantise):
    own(nc.vector.tensor_reduce(scale, w, AX.X, ALU.max, apply_absolute_value=True)).done()
    own(nc.vector.tensor_scalar(scale, scale, 1 / 127.0, 1e-8, ALU.mult, ALU.max)).done()
    own(nc.vector.reciprocal(recip, scale)).done()
    for c in range(w.shape[1]):
        own(nc.vector.tensor_scalar(out[:, c], w[:, c], recip[:, c:c + 1], MAGIC, ALU.mult, ALU.add))
    own.done()
    own(nc.vector.tensor_scalar(out, out, MAGIC, 127.0, ALU.subtract, ALU.min)).done()
    own(nc.vector.tensor_scalar(out, out, -127.0, None, ALU.max)).done()
    if dequantise:
        for c in range(w.shape[1]):
            own(nc.vector.tensor_scalar(out[:, c], out[:, c], scale[:, c:c + 1], None, ALU.mult))
        own.done()


def round_any(nc, own, x, tmp):
    big = 2.0 ** 23
    mag, low, sgn = (tmp[:, n] for n in range(3))
    own(nc.vector.tensor_scalar(sgn, x, 0.0, 2.0, ALU.is_ge, ALU.mult)).done()
    own(nc.vector.tensor_scalar(sgn, sgn, 1.0, None, ALU.subtract)).done()
    own(nc.vector.tensor_tensor(mag, x, sgn, ALU.mult)).done()
    own(nc.vector.tensor_scalar(low, mag, big, None, ALU.min)).done()
    own(nc.vector.tensor_tensor(mag, mag, low, ALU.subtract))
    own.done()
    own(nc.vector.tensor_scalar(low, low, big, big, ALU.add, ALU.subtract)).done()
    own(nc.vector.tensor_tensor(mag, mag, low, ALU.add)).done()
    own(nc.vector.tensor_tensor(x, mag, sgn, ALU.mult)).done()


WORK1 = [("ctx", 0, 0), ("ctx", 0, 1)]
for _j in range(3):
    for _b in range(2):
        WORK1.append(("keys", _j, _b))
        if _j < 2:
            WORK1.append(("ctx", _j + 1, _b))
    WORK1 += [("vals", _j, 0), ("vals", _j, 1)]


def attention1_order():
    order, u = [], 0
    for r in range(NR):
        order.append(("scores", r, 0))
        if r:
            order += [("values", r - 1, 0), ("values", r - 1, 1), ("turn", r - 1, 2)]
        if u < 9:
            order.append(("unit", u, 0))
            u += 1
        if r:
            order.append(("values", r - 1, 2))
        if r in (0, 1, 2):
            order.append(("unit", u, 0))
            u += 1
        order += [("turn", r, 0), ("turn", r, 1)]
    return order + [("values", 7, 0), ("values", 7, 1), ("turn", 7, 2), ("values", 7, 2)]


def attn1_phase(nc, g, io):
    ORDER = attention1_order()
    AT = {w: n for n, w in enumerate(WORK1)}
    NW = len(WORK1)
    GK = 4 * KP
    with phase(nc) as (ctx, a):
        wst = a.sb("b_wst", [128, 4, H])
        wT = a.sb("b_wT", [128, 2, KC, 2 * H], F16)
        bk = a.sb("b_bk", [128, 2, KC])
        cx = a.sb("b_ctx", [KP, 2, KT, H])
        cT = a.sb("b_cT", [128, 2, 2, KC, GK], F16)
        kn = a.sb("b_kn", [128, 2, 2, 2, SE], F16)
        ks = a.sb("b_ks", [96, 2, 2, 4, SE], F16)
        vv = a.sb("b_vv", [KP, 2, KT, 8, 2, 32], F16)
        qs = a.sb("b_qs", [96, 2, 2, 4, 128], F16)
        pr = a.sb("b_pr", [128, 2, SE])
        pTh = a.sb("b_pTh", [KP, 2, KT, 128], F16)
        pTl = a.sb("b_pTl", [KP, 2, KT, 128], F16)
        nmax = a.sb("b_nmax", [128, 2, NR])
        rsum = a.sb("b_rsum", [128, 2, NR])
        inv = a.sb("b_inv", [128, 2, NR])
        os_ = a.sb("b_os", [128, NR, 32])
        ot = a.sb("b_ot", [128, 2, NR, 2, HD1])
        ps_s = a.ps("b_ps", [128, 3, 512])
        ps_t = [a.ps(f"b_pt{i}", [128, 512]) for i in range(2)]
        ps_w = [a.ps(f"b_pw{i}", [128, 512]) for i in range(2)]
        ps_o = a.ps("b_po", [128, NR, 2, 32])
        w_in, b_in = a.sem("b_w_in"), a.sem("b_b_in")
        ctx_in = [a.sem(f"b_ctx_in{i}") for i in range(2)]
        q_in = [a.sem(f"b_q_in{i}") for i in range(2)]
        k_in = [a.sem(f"b_k_in{i}") for i in range(2)]
        stored = [a.sem(f"b_stored{i}") for i in range(2)]
        names = ("w_turned w_hi w_lo scores_done nmax_ready exp_done turn_done turn_hi turn_lo values_done "
                 "ot_free o_half inv_ready o_taken work_done work_hi work_taken own")
        s = {n: a.sem("b_" + n) for n in names.split()}
        block = ctx.enter_context(nc.Block())

        @block.sync
        def _(sp):
            sp.sem_inc(s["ot_free"], 2)
            sp.dma_start(wst[:], io.wkv.rearrange("(c p) n -> p c n", p=128)).then_inc(w_in, 16)
            with nc.allow_non_contiguous_dma(reason="256 values"):
                sp.dma_start(bk[:, 0], io.bkv[0:H].rearrange("(c p) -> p c", p=128)).then_inc(b_in, 16)

            def load_ctx(G, par):
                src = io.ctx[ds(G, 1), :, :].rearrange("a (p k) d -> (a p) k d", k=KT)
                sp.dma_start(cx[0:120, par], src[0:120]).then_inc(ctx_in[par], 16)
                sp.dma_start(cx[120:KP, par], src[120:KP]).then_inc(ctx_in[par], 16)

            def load_q(G, par):
                for n, part in enumerate((0, 1, 0)):
                    src = io.q1[ds(G, 1), part].rearrange("a (j r) k c -> (a r) k j c", j=4)
                    for k in range(2):
                        sp.dma_start(qs[32 * n:32 * n + 32, par, k], src[:, k]).then_inc(q_in[par], 16)

            def stack_keys(G, par):
                sp.wait_ge(s["work_taken"], NW * G + AT["keys", 2, 1] + 1)
                for n, part in enumerate((0, 0, 1)):
                    for j in range(4):
                        sp.dma_start(ks[32 * n:32 * n + 32, par, :, j], kn[32 * j:32 * j + 32, par, part])\
                            .then_inc(k_in[par], 16)

            load_ctx(0, 0)
            load_ctx(1, 1)
            load_q(0, 0)
            stack_keys(0, 0)

            def step(g_, par, half, load, produce):
                if load:
                    sp.wait_ge(s["work_done"], NW * g_ + AT["ctx", 2, 1] + 1)
                    load_ctx(g_ + 2, par)
                if produce:
                    wait(sp, s["scores_done"], NR * g_)
                    load_q(g_ + 1, 1 - par)
                    stack_keys(g_ + 1, 1 - par)
                sp.wait_ge(s["o_taken"], g_ + 1)
                with nc.allow_non_contiguous_dma(reason="16 columns of a head"):
                    for e in range(2):
                        sp.dma_start(io.o1[ds(g_ * S, S), :].rearrange("q (r e d) -> q r e d", e=2, d=HD1)[:, :, e, :],
                                     ot[HP * e:HP * e + S, par, :, e]).then_inc(stored[par], 16)
                sp.wait_ge(stored[par], 32 * half + 32)
                sp.sem_inc(s["ot_free"], 1)

            step(0, 0, 0, True, True)
            with sp.Fori(0, (B - 4) // 2) as i:
                step(2 * i + 1, 1, i, True, True)
                step(2 * i + 2, 0, i + 1, True, True)
            step(B - 3, 1, (B - 3) // 2, True, True)
            step(B - 2, 0, (B - 2) // 2, False, True)
            step(B - 1, 1, (B - 1) // 2, False, False)
            for k in range(2):
                sp.wait_ge(stored[k], 32 * (B // 2))

        def steps(step):
            def run(eng):
                step(0, 0, 0, 0, True)
                with eng.Fori(0, (B - 2) // 2) as i:
                    step(2 * i + 1, 1, i, i + 1, True)
                    step(2 * i + 2, 0, i + 1, i + 1, True)
                step(B - 1, 1, (B - 1) // 2, B // 2, False)
            return run

        @block.scalar
        def _(act):
            for c in range(KC):
                act.wait_ge(s["w_turned"], c + 1)
                nc.scalar.activation(wT[:, 0, c], ps_w[c][:], ACT.Copy, scale=WS).then_inc(s["w_hi"], 1)

            def unit(G, par, half, u):
                for n in (2 * u, 2 * u + 1):
                    what, j, i = WORK1[n]
                    act.wait_ge(s["work_done"], NW * G + n + 1)
                    bank = ps_w[n % 2]
                    if what == "ctx":
                        for c in range(KC):
                            ins = nc.scalar.activation(
                                cT[:, (j + par) % 2, 0, c, 2 * KP * i:2 * KP * (i + 1)]
                                .rearrange("p (k q) -> p k q", q=KP),
                                bank[:, 0:4 * KP].rearrange("p (k c q) -> p k c q", k=2, c=KC)[:, :, c], ACT.Copy)
                    elif what == "keys":
                        if j == 0 and i == 0:
                            wait(act, k_in[par], 192 * half)
                        ins = nc.scalar.activation(kn[:, par, 0, i, GK * j:GK * (j + 1)], bank[:, 0:GK],
                                                   ACT.Identity, bias=bk[:, 1, i:i + 1])
                    else:
                        kt = 4 * j + 2 * i
                        ins = nc.scalar.activation(vv[:, par, kt:kt + 2, :, 0].rearrange("p k h d -> p (k h) d"),
                                                   bank[0:KP, :].rearrange("p (k d) -> p k d", d=32), ACT.Copy)
                    ins.then_inc(s["work_hi"], 1)

            act.wait_ge(s["own"], 1)
            for u in range(9):
                unit(0, 0, 0, u)

            def step(g_, par, half, nxt, produce):
                for what, r, gr in ORDER:
                    R = NR * g_ + r
                    if what == "scores":
                        act.wait_ge(s["nmax_ready"], R + 1)
                        nc.scalar.activation(pr[:, r % 2], pr[:, r % 2], ACT.Exp, scale=-1.0,
                                             bias=nmax[:, par, r:r + 1],
                                             accum_out=rsum[:, par, r:r + 1]).then_inc(s["exp_done"], 1)
                    elif what == "turn":
                        q = 3 * r + gr
                        act.wait_ge(s["turn_done"], 3 * NR * g_ + q + 1)
                        nc.scalar.activation(pTh[:, r % 2, 4 * gr:4 * gr + 4].rearrange("p k c -> p (k c)"),
                                             ps_t[q % 2][0:KP, :], ACT.Copy).then_inc(s["turn_hi"], 1)
                    elif what == "values" and gr == 2 and r == NR - 1:
                        act.wait_ge(s["values_done"], g_ + 1)
                        nc.scalar.activation(os_[:], ps_o[:, :, 1], ACT.Copy).then_inc(s["o_half"], 1)
                    elif what == "unit" and produce:
                        unit(g_ + 1, 1 - par, nxt, r)

            steps(step)(act)

        @block.vector
        def _(dve):
            dve.wait_ge(b_in, 16)
            nc.vector.tensor_scalar(bk[:, 1], bk[:, 0], WS, None, ALU.mult).then_inc(s["own"], 1)
            for c in range(KC):
                dve.wait_ge(s["w_hi"], c + 1)
                nc.vector.scalar_tensor_tensor(wT[:, 1, c], ps_w[c][:], WS, wT[:, 0, c], ALU.mult,
                                               ALU.subtract).then_inc(s["w_lo"], 1)
            dve.wait_ge(s["own"], 1)

            def unit(G, par, u):
                for n in (2 * u, 2 * u + 1):
                    what, j, i = WORK1[n]
                    dve.wait_ge(s["work_hi"], NW * G + n + 1)
                    bank = ps_w[n % 2]
                    if what == "ctx":
                        for c in range(KC):
                            cols = slice(2 * KP * i, 2 * KP * (i + 1))
                            ins = nc.vector.tensor_tensor(
                                cT[:, (j + par) % 2, 1, c, cols].rearrange("p (k q) -> p k q", q=KP),
                                bank[:, 0:4 * KP].rearrange("p (k c q) -> p k c q", k=2, c=KC)[:, :, c],
                                cT[:, (j + par) % 2, 0, c, cols].rearrange("p (k q) -> p k q", q=KP), ALU.subtract)
                    elif what == "keys":
                        cols = slice(GK * j, GK * (j + 1))
                        ins = nc.vector.scalar_tensor_tensor(kn[:, par, 1, i, cols], bank[:, 0:GK], bk[:, 1, i:i + 1],
                                                             kn[:, par, 0, i, cols], ALU.add, ALU.subtract)
                    else:
                        kt = 4 * j + 2 * i
                        ins = nc.vector.tensor_tensor(vv[:, par, kt:kt + 2, :, 1].rearrange("p k h d -> p (k h) d"),
                                                      bank[0:KP, :].rearrange("p (k d) -> p k d", d=32),
                                                      vv[:, par, kt:kt + 2, :, 0].rearrange("p k h d -> p (k h) d"),
                                                      ALU.subtract)
                    ins.then_inc(s["work_taken"], 1)

            for u in range(9):
                unit(0, 0, u)

            def step(g_, par, half, nxt, produce):
                for what, r, gr in ORDER:
                    R = NR * g_ + r
                    if what == "scores":
                        dve.wait_ge(s["scores_done"], R + 1)
                        nc.vector.tensor_scalar(pr[:, r % 2].rearrange("p (a k) -> p a k", k=500), ps_s[:, :, 0:500],
                                                -1.0, None, ALU.mult, ALU.min,
                                                accum_out=nmax[:, par, r:r + 1]).then_inc(s["nmax_ready"], 1)
                    elif what == "turn":
                        q = 3 * r + gr
                        dve.wait_ge(s["turn_hi"], 3 * NR * g_ + q + 1)
                        part = (slice(None), r % 2, slice(4 * gr, 4 * gr + 4))
                        nc.vector.tensor_tensor(pTl[part].rearrange("p k c -> p (k c)"), ps_t[q % 2][0:KP, :],
                                                pTh[part].rearrange("p k c -> p (k c)"),
                                                ALU.subtract).then_inc(s["turn_lo"], 1)
                    elif what == "values" and gr == 2 and r == NR - 1:
                        n = 4 * g_
                        dve.wait_ge(s["exp_done"], NR * g_ + NR)
                        nc.vector.tensor_scalar(inv[:, par], rsum[:, par], WS, None, ALU.mult).then_inc(s["inv_ready"], 1)
                        dve.wait_ge(s["inv_ready"], 3 * g_ + 1)
                        nc.vector.reciprocal(inv[:, par], inv[:, par]).then_inc(s["inv_ready"], 1)
                        dve.wait_ge(s["ot_free"], g_ + 1)
                        dve.wait_ge(s["o_half"], g_ + 1)
                        both = ot[:, par].rearrange("p r e d -> p r (e d)")
                        nc.vector.tensor_tensor(both, ps_o[:, :, 0], os_[:], ALU.add).then_inc(s["inv_ready"], 1)
                        dve.wait_ge(s["inv_ready"], 3 * g_ + 3)
                        nc.vector.tensor_tensor(both, both, inv[:, par].unsqueeze(2).to_broadcast([128, NR, 32]),
                                                ALU.mult).then_inc(s["o_taken"], 1)
                    elif what == "unit" and produce:
                        unit(g_ + 1, 1 - par, r)

            steps(step)(dve)

        @block.tensor
        def _(pe):
            pe.wait_ge(w_in, 16)
            for c in range(KC):
                for o in range(4):
                    last = nc.tensor.transpose(ps_w[c][:, o * 128:(o + 1) * 128], wst[:, o, c * 128:(c + 1) * 128],
                                               g.ident[:])
                last.then_inc(s["w_turned"], 1)
            pe.wait_ge(s["w_lo"], KC)

            def unit(G, par, half, u):
                for n in (2 * u, 2 * u + 1):
                    what, j, i = WORK1[n]
                    bank = ps_w[n % 2]
                    wait(pe, s["work_taken"], NW * G + n - 1)
                    if what == "ctx":
                        if j == 0 and i == 0:
                            pe.wait_ge(ctx_in[par], 32 * half + 32)
                        for k in range(2):
                            for c in range(KC):
                                last = nc.tensor.transpose(bank[:, (2 * k + c) * KP:(2 * k + c + 1) * KP],
                                                           cx[:, par, 4 * j + 2 * i + k, c * 128:(c + 1) * 128],
                                                           g.ident[0:KP, 0:KP])
                    else:
                        pe.wait_ge(s["work_taken"], NW * G + AT["ctx", j, 1] + 1)
                        if what == "keys":
                            for c in range(KC):
                                m = slice(128 * i, 128 * i + 128)
                                last = three_products(nc, bank[:, 0:GK], wT[:, 0, c, m], wT[:, 1, c, m],
                                                      cT[:, (j + par) % 2, 0, c], cT[:, (j + par) % 2, 1, c],
                                                      start=(c == 0), stop=(c == KC - 1))
                        else:
                            for k in range(2):
                                keys = slice((2 * i + k) * KP, (2 * i + k + 1) * KP)
                                for c in range(KC):
                                    last = three_products(nc, bank[0:KP, k * H:(k + 1) * H],
                                                          cT[:, (j + par) % 2, 0, c, keys],
                                                          cT[:, (j + par) % 2, 1, c, keys], wT[:, 0, c, H:2 * H],
                                                          wT[:, 1, c, H:2 * H], start=(c == 0), stop=(c == KC - 1))
                    last.then_inc(s["work_done"], 1)

            for u in range(9):
                unit(0, 0, 0, u)

            def step(g_, par, half, nxt, produce):
                for what, r, gr in ORDER:
                    R = NR * g_ + r
                    if what == "scores":
                        if r == 0:
                            pe.wait_ge(q_in[par], 96 * half + 96)
                            pe.wait_ge(k_in[par], 192 * half + 192)
                            pe.wait_ge(s["work_taken"], NW * g_ + NW)
                        wait(pe, s["nmax_ready"], R)
                        for j in range(3):
                            last = nc.tensor.matmul(ps_s[:, j, 0:500], qs[:, par, r // 4, r % 4],
                                                    ks[:, par, r // 4, r % 4, 500 * j:500 * j + 500],
                                                    start=True, stop=True)
                        last.then_inc(s["scores_done"], 1)
                    elif what == "turn":
                        q = 3 * r + gr
                        if gr == 0:
                            pe.wait_ge(s["exp_done"], R + 1)
                        wait(pe, s["turn_lo"], 3 * NR * g_ + q - 1)
                        for j in range(4):
                            kt = 4 * gr + j
                            last = nc.tensor.transpose(ps_t[q % 2][0:KP, 128 * j:128 * j + 128],
                                                       pr[:, r % 2, kt * KP:(kt + 1) * KP], g.ident[:])
                        last.then_inc(s["turn_done"], 1)
                    elif what == "values":
                        if gr == 0 and r == 0:
                            wait(pe, s["o_taken"], g_)
                        pe.wait_ge(s["turn_lo"], 3 * NR * g_ + 3 * r + gr + 1)
                        for kt in range(4 * gr, 4 * gr + 4):
                            nc.tensor.matmul(ps_o[:, r], pTh[:, r % 2, kt], vv[:, par, kt, r], start=(kt == 0),
                                             stop=False)
                            last = nc.tensor.matmul(ps_o[:, r, 0], pTl[:, r % 2, kt], vv[:, par, kt, r, 0],
                                                    start=False, stop=(kt == KT - 1))
                        if gr == 2 and r == NR - 1:
                            last.then_inc(s["values_done"], 1)
                    elif produce:
                        unit(g_ + 1, 1 - par, nxt, r)

            steps(step)(pe)


def final_phase(nc, g, io):
    with phase(nc) as (ctx, a):
        yt = a.sb("f_yt", [TT, 2, H])
        wp = a.sb("f_wp", [128, KC, H])
        wpn = a.sb("f_wpn", [128, KC, H])
        wpT = a.sb("f_wpT", [128, 2, KC, H], F16)
        wa = a.sb("f_wa", [128, 2, KC])
        w1 = a.sb("f_w1", [128, FB, H])
        w2 = a.sb("f_w2", [128, KC, F])
        w1n = a.sb("f_w1n", [128, FB, H], F16)
        w2n = a.sb("f_w2n", [128, KC, F], F16)
        w1T = a.sb("f_w1T", [128, KC, F], F16)
        w2T = a.sb("f_w2T", [128, FB, H], F16)
        b1 = a.sb("f_b1", [128, FB])
        rows = a.sb("f_rows", [TT, 3, H])
        sc = a.sb("f_sc", [128, 16])
        mx = a.sb("f_mx", [128, 2])
        ma = a.sb("f_ma", [128, 2])
        ot = a.sb("f_ot", [TT, 2, H])
        ob = a.sb("f_ob", [TT, H])
        am = a.sb("f_am", [TT, 2])
        oq = a.sb("f_oq", [TT, H], F16)
        oT = a.sb("f_oT", [128, KC, TT], F16)
        st6 = a.sb("f_st6", [TT, 6])
        mv = a.sb("f_mv", [TT, 2])
        ve = a.sb("f_ve", [TT, 1])
        rs = a.sb("f_rs", [TT, 1])
        xn = a.sb("f_xn", [TT, H])
        xq = a.sb("f_xq", [TT, H], F16)
        xT = a.sb("f_xT", [128, KC, TT], F16)
        hb = a.sb("f_hb", [128, FB, TT])
        hq = a.sb("f_hq", [128, FB, TT], F16)
        tmp = a.sb("f_tmp", [128, 3, H])
        p0 = [a.ps(f"f_p0{i}", [128, 512]) for i in range(2)]
        p16 = a.ps("f_p16", [128, 1024], F16)
        pO = a.ps("f_pO", [128, KC, TT], F16)
        pX = a.ps("f_pX", [128, KC, TT], F16)
        pY = a.ps("f_pY", [128, H])
        pH = [a.ps(f"f_pH{i}", [128, 4, TT]) for i in range(2)]
        w_in, gate = a.sem("f_w_in"), a.sem("f_gate")
        o_in = [a.sem(f"f_o_in{i}") for i in range(2)]
        out_done = [a.sem(f"f_out{i}") for i in range(2)]
        at = {}
        names = ("dve max_ready max_all wT_done wT_hi w16_done w16_taken oq_ready oT_done oT_taken y_done "
                 "var rstd xq_ready xT_done xT_taken h_done hq_ready z_done out_ready")
        s = {n: a.sem("f_" + n) for n in names.split()}
        block = ctx.enter_context(nc.Block())
        S1, S2, SW1, SW2, RS1, RW1, RW2, P1, P2, R1, R2, KAP, RS2 = range(13)

        def col(n, rows=128):
            return sc[0:rows, n:n + 1]

        @block.sync
        def _(sp):
            sp.dma_start(wp[:], io.wp.rearrange("(c p) n -> p c n", p=128)).then_inc(w_in, 16)
            sp.dma_start(w1[:], io.W1.rearrange("(c p) n -> p c n", p=128)).then_inc(w_in, 16)
            sp.dma_start(w2[:], io.W2.rearrange("(c p) n -> p c n", p=128)).then_inc(w_in, 16)
            with nc.allow_non_contiguous_dma(reason="1024 values"):
                sp.dma_start(b1[:], io.b1.rearrange("(c p) -> p c", p=128)).then_inc(w_in, 16)
            for n, v in enumerate((io.bkv[H:2 * H], io.bp, io.b2)):
                sp.dma_start(rows[:, n], v.rearrange("(a n) -> a n", a=1).to_broadcast([TT, H])).then_inc(w_in, 16)
            for n, v in enumerate((io.s1, io.s2)):
                sp.dma_start(col(n), v.rearrange("(a n) -> a n", a=1).to_broadcast([128, 1])).then_inc(w_in, 16)
            def pair(i):
                for k in range(2):
                    t = 2 * i + k
                    wait(sp, s["oq_ready"], t)
                    sp.dma_start(ot[:, k], io.o1[ds(t * TT, TT), :]).then_inc(o_in[k], 16)
                    sp.wait_ge(s["out_ready"], t + 1)
                    sp.dma_start(io.out[ds(t * TT, TT), :], yt[:, k]).then_inc(out_done[k], 16)

            each(sp, NT // 2, pair)
            for k in range(2):
                sp.wait_ge(out_done[k], 16 * (NT // 2))

        @block.gpsimd
        def _(pool):
            pool.wait_ge(s["max_ready"], 2)
            nc.gpsimd.partition_all_reduce(ma[:], mx[:], 128, bass.bass_isa.ReduceOp.max).then_inc(s["max_all"], 1)
            def tile(t):
                pool.wait_ge(s["var"], t + 1)
                nc.gpsimd.tensor_tensor(rs[:], ve[:], g.mhalf[0:TT, 0:1], ALU.pow).then_inc(s["rstd"], 1)

            each(pool, NT, tile)

        @block.scalar
        def _(act):
            for c in range(KC):
                act.wait_ge(s["wT_done"], c + 1)
                nc.scalar.activation(wpT[:, 0, c], p0[c][:, 0:H], ACT.Copy, scale=WS).then_inc(s["wT_hi"], 1)
            for n in range(4):
                act.wait_ge(s["w16_done"], n + 1)
                if n < 2:
                    out, src = w1T[:, n], p16[:]
                else:
                    out, src = w2T[:, 4 * (n - 2):4 * (n - 2) + 4].rearrange("p f n -> p (f n)"), p16[:]
                nc.scalar.activation(out, src, ACT.Copy).then_inc(s["w16_taken"], 1)
            def tile(t):
                act.wait_ge(s["oT_done"], t + 1)
                nc.scalar.activation(oT[:], pO[:], ACT.Copy).then_inc(s["oT_taken"], 1)
                act.wait_ge(s["xT_done"], t + 1)
                nc.scalar.activation(xT[:], pX[:], ACT.Copy).then_inc(s["xT_taken"], 1)

            each(act, NT, tile)

        @block.vector
        def _(dve):
            own = Counted(dve, s["dve"])
            dve.wait_ge(w_in, 16 * 9)
            nc.vector.tensor_reduce(mx[:, 0:1], w1[:], AX.XY, ALU.max, apply_absolute_value=True)\
                .then_inc(s["max_ready"], 1)
            nc.vector.tensor_reduce(mx[:, 1:2], w2[:], AX.XY, ALU.max, apply_absolute_value=True)\
                .then_inc(s["max_ready"], 1)
            quantise_rows(nc, own, wp[:], wpn[:], wa[:, 0], wa[:, 1], dequantise=True)
            at["wp"] = own.n
            dve.wait_ge(s["max_all"], 1)
            own(nc.vector.tensor_scalar(sc[:, SW1:SW2 + 1], ma[:], 1 / 7.0, None, ALU.mult)).done()
            own(nc.vector.reciprocal(sc[:, RW1:RW2 + 1], sc[:, SW1:SW2 + 1]))
            own(nc.vector.reciprocal(col(RS1), col(S1)))
            own(nc.vector.reciprocal(col(RS2), col(S2)))
            own(nc.vector.tensor_tensor(sc[:, P1:P2 + 1], sc[:, S1:S2 + 1], sc[:, SW1:SW2 + 1], ALU.mult)).done()
            own(nc.vector.reciprocal(sc[:, R1:R2 + 1], sc[:, P1:P2 + 1]))
            own(nc.vector.tensor_tensor(col(KAP), col(P1), col(RS2), ALU.mult)).done()
            for w, wn, r in ((w1, w1n, RW1), (w2, w2n, RW2)):
                own(nc.vector.tensor_scalar(w[:], w[:], col(r), MAGIC, ALU.mult, ALU.add)).done()
                own(nc.vector.tensor_scalar(w[:], w[:], MAGIC, 7.0, ALU.subtract, ALU.min)).done()
                own(nc.vector.tensor_scalar(wn[:], w[:], -8.0, None, ALU.max)).done()
            at["w16"] = own.n
            for b, r, rows_ in ((b1[:], R1, 128), (rows[:, 2], R2, TT)):
                own(nc.vector.tensor_scalar(b, b, col(r, rows_), -2.0 ** 31, ALU.mult, ALU.max)).done()
                own(nc.vector.tensor_scalar(b, b, 2.0 ** 31, None, ALU.min)).done()
                round_any(nc, own, b, tmp[0:rows_, :, 0:b.shape[1]])
            own(nc.vector.tensor_scalar(rows[:, 2], rows[:, 2], col(P2, TT), None, ALU.mult)).done()
            for c in range(KC):
                dve.wait_ge(s["wT_hi"], c + 1)
                own(nc.vector.scalar_tensor_tensor(wpT[:, 1, c], p0[c][:, 0:H], WS, wpT[:, 0, c], ALU.mult,
                                                   ALU.subtract))
            own.done()
            at["prep"] = own.n
            base, per, own.marks = own.n, 19, 0
            def pair(i):
                for k in range(2):
                    t = 2 * i + k
                    own.n = base + per * t
                    xrow = g.xs[:, ds(t, 1), :].rearrange("p a n -> p (a n)")
                    dve.wait_ge(o_in[k], 16 * i + 16)
                    own(nc.vector.tensor_tensor(ob[:], ot[:, k], rows[:, 0], ALU.add)).done()
                    own(nc.vector.tensor_reduce(am[:, 0:1], ob[:], AX.X, ALU.max, apply_absolute_value=True)).done()
                    own(nc.vector.tensor_scalar(am[:, 0:1], am[:, 0:1], 1 / 127.0, 1e-8, ALU.mult, ALU.max)).done()
                    own(nc.vector.reciprocal(am[:, 1:2], am[:, 0:1])).done()
                    own(nc.vector.tensor_scalar(ob[:], ob[:], am[:, 1:2], MAGIC, ALU.mult, ALU.add)).done()
                    own(nc.vector.tensor_scalar(ob[:], ob[:], MAGIC, 127.0, ALU.subtract, ALU.min)).done()
                    own(nc.vector.tensor_scalar(am[:, 1:2], am[:, 0:1], 1 / WS, None, ALU.mult)).done()
                    nc.vector.tensor_scalar(oq[:], ob[:], -127.0, None, ALU.max).then_inc(s["oq_ready"], 1)
                    own(nc.vector.tensor_tensor(xrow, xrow, rows[:, 1], ALU.add)).done()
                    dve.wait_ge(s["y_done"], t + 1)
                    own(nc.vector.scalar_tensor_tensor(xrow, pY[0:TT, :], am[:, 1:2], xrow, ALU.mult,
                                                       ALU.add)).done()
                    passed(dve, gate)
                    own(nc.vector.bn_stats(st6[:], xrow)).done()
                    passed(dve, gate)
                    own(nc.vector.bn_aggr(mv[:], st6[:])).done()
                    nc.vector.tensor_scalar(ve[:], mv[:, 1:2], LN_EPS, None, ALU.add).then_inc(s["var"], 1)
                    dve.wait_ge(s["rstd"], t + 1)
                    own(nc.vector.tensor_scalar(xn[:], xrow, mv[:, 0:1], rs[:], ALU.subtract, ALU.mult)).done()
                    own(nc.vector.tensor_scalar(xn[:], xn[:], col(RS1, TT), MAGIC, ALU.mult, ALU.add)).done()
                    own(nc.vector.tensor_scalar(xn[:], xn[:], MAGIC, 7.0, ALU.subtract, ALU.min)).done()
                    nc.vector.tensor_scalar(xq[:], xn[:], -8.0, None, ALU.max).then_inc(s["xq_ready"], 1)
                    for j in range(2):
                        part = hb[:, 4 * j:4 * j + 4]
                        dve.wait_ge(s["h_done"], 2 * t + j + 1)
                        own(nc.vector.tensor_tensor(part, pH[j][:], b1[:, 4 * j:4 * j + 4].unsqueeze(2)
                                                    .to_broadcast([128, 4, TT]), ALU.add))
                    own.done()
                    own(nc.vector.tensor_scalar(hb[:], hb[:], 0.0, col(KAP), ALU.max, ALU.mult)).done()
                    own(nc.vector.tensor_scalar(hb[:], hb[:], MAGIC, MAGIC, ALU.add, ALU.subtract)).done()
                    nc.vector.tensor_scalar(hq[:], hb[:], 15.0, None, ALU.min).then_inc(s["hq_ready"], 1)
                    own(nc.vector.tensor_tensor(xn[:], xrow, rows[:, 2], ALU.add)).done()
                    dve.wait_ge(s["z_done"], t + 1)
                    wait(dve, out_done[k], 16 * i)
                    nc.vector.scalar_tensor_tensor(yt[:, k], pY[0:TT, :], col(P2, TT), xn[:], ALU.mult,
                                                   ALU.add).then_inc(s["out_ready"], 1)

            each(dve, NT // 2, pair)
            assert own.marks == 4 * per

        @block.tensor
        def _(pe):
            pe.wait_ge(s["dve"], at["wp"])
            for c in range(KC):
                for o in range(KC):
                    last = nc.tensor.transpose(p0[c][:, o * 128:(o + 1) * 128], wpn[:, o, c * 128:(c + 1) * 128],
                                               g.ident[:])
                last.then_inc(s["wT_done"], 1)
            pe.wait_ge(s["dve"], at["w16"])
            for n in range(4):
                wait(pe, s["w16_taken"], n)
                for o in range(8):
                    if n < 2:
                        src = w1n[:, o, n * 128:(n + 1) * 128]
                    else:
                        f = 4 * (n - 2) + o // 2
                        src = w2n[:, o % 2, f * 128:(f + 1) * 128]
                    last = nc.tensor.transpose(p16[:, o * 128:(o + 1) * 128], src, g.ident16[:])
                last.then_inc(s["w16_done"], 1)
            pe.wait_ge(s["dve"], at["prep"])
            def tile(t):
                pe.wait_ge(s["oq_ready"], t + 1)
                for c in range(KC):
                    last = nc.tensor.transpose(pO[:, c], oq[:, c * 128:(c + 1) * 128], g.ident16[0:TT, 0:TT])
                last.then_inc(s["oT_done"], 1)
                pe.wait_ge(s["oT_taken"], t + 1)
                wait(pe, s["out_ready"], t)
                for c in range(KC):
                    for n in range(2):
                        last = nc.tensor.matmul(pY[0:TT, :], oT[:, c], wpT[:, n, c], start=(c == 0 and n == 0),
                                                stop=(c == KC - 1 and n == 1))
                last.then_inc(s["y_done"], 1)
                pe.wait_ge(s["xq_ready"], t + 1)
                for c in range(KC):
                    last = nc.tensor.transpose(pX[:, c], xq[:, c * 128:(c + 1) * 128], g.ident16[0:TT, 0:TT])
                last.then_inc(s["xT_done"], 1)
                pe.wait_ge(s["xT_taken"], t + 1)
                for j in range(2):
                    for f in range(4):
                        for c in range(KC):
                            cols = slice((4 * j + f) * 128, (4 * j + f + 1) * 128)
                            last = nc.tensor.matmul(pH[j][:, f], w1T[:, c, cols], xT[:, c], start=(c == 0),
                                                    stop=(c == KC - 1))
                    last.then_inc(s["h_done"], 1)
                pe.wait_ge(s["hq_ready"], t + 1)
                for f in range(FB):
                    last = nc.tensor.matmul(pY[0:TT, :], hq[:, f], w2T[:, f], start=(f == 0), stop=(f == FB - 1))
                last.then_inc(s["z_done"], 1)

            each(pe, NT, tile)


class G:
    pass


def build(nc, io):
    with ExitStack() as ctx:
        a = Alloc(nc, ctx)
        g = G()
        g.ident = a.sb("ident", [128, 128])
        g.ident16 = a.sb("ident16", [128, 128], F16)
        g.blk16 = a.sb("blk16", [128, 8])
        g.evenodd = a.sb("evenodd", [128, 2])
        g.mhalf = a.sb("mhalf", [128, NH])
        constants(nc, g)
        q0_phase(nc, g, io)
        attn0_phase(nc, g, io)
        g.xs = a.sb("xs", [TT, NT, H])
        with ExitStack() as inner:
            b = Alloc(nc, inner)
            g.xT = b.sb("xT", [128, 2, KC, TOK], F16)
            g.comb = b.sb("comb", [TT, NT, NX])
            mix0_phase(nc, g, io)
            experts_phase(nc, g, io)

        q1_phase(nc, g, io)
        attn1_phase(nc, g, io)
        final_phase(nc, g, io)


_NAMES = dict(
    x="x", ctx="ctx_2048", mask="mask_1xSxS2_ff0", Wq="L0_xattn_Wq", bq="L0_xattn_bq", Wk="L0_xattn_Wk",
    bk="L0_xattn_bk", Wv="L0_xattn_Wv", bv="L0_xattn_bv", Wo="L0_xattn_Wo", qn_w="L0_xattn_qn_w",
    kn_w="L0_xattn_kn_w", gate_w="L0_ffn_gate_w", w_gate="L0_ffn_w_gate", w_up="L0_ffn_w_up",
    w_down="L0_ffn_w_down", sw_gate="L0_ffn_sw_gate", sw_up="L0_ffn_sw_up", sw_down="L0_ffn_sw_down",
    wq="L1_xattn_wq", bq1="L1_xattn_bq", wkv="L1_xattn_wkv", bkv="L1_xattn_bkv", wp="L1_xattn_wp",
    bp="L1_xattn_bp", W1="L1_ffn_W1", b1="L1_ffn_b1", W2="L1_ffn_W2", b2="L1_ffn_b2", s1="L1_ffn_s_act1",
    s2="L1_ffn_s_act2")


class Tensors:
    pass


def kernel(**inputs):
    import concourse.bacc as bacc
    from concourse.bass_utils import run_bass_kernel_spmd

    nc = bacc.Bacc("TRN2", target_bir_lowering=False, num_devices=1)
    io, arrays = Tensors(), {}
    for name, full in _NAMES.items():
        arr = np.ascontiguousarray(inputs[full])
        if name == "x":
            arr = arr.reshape(TOK, H)
        arrays[full] = arr
        io.__dict__[name] = nc.dram_tensor(full, arr.shape, mybir.dt.from_np(arr.dtype), kind="ExternalInput").ap()
    io.out = nc.dram_tensor("out", [TOK, H], F32, kind="ExternalOutput").ap()
    for name, shape, dt in (("qh", [B, 128, NR * 128], F16), ("ql", [B, 128, NR * 128], F16),
                            ("o0", [TOK, NH * HD], F32), ("q1", [B, 2, 128, KC, 128], F16), ("o1", [TOK, H], F32)):
        io.__dict__[name] = nc.dram_tensor("scratch_" + name, shape, dt, kind="Internal").ap()
    build(nc, io)
    r = run_bass_kernel_spmd(nc, [arrays], core_ids=[0])
    return r.results[0]["out"].reshape(B, S, H)
```

```python
import numpy as np
import concourse.bass as bass
from concourse import mybir
from contextlib import ExitStack, contextmanager

F32 = mybir.dt.float32
F16 = mybir.dt.float16
ALU = mybir.AluOpType
ACT = mybir.ActivationFunctionType
AX = mybir.AxisListType
ds = bass.ds

B, S, SE, H = 32, 56, 1500, 256
TOK = B * S
TT = 2 * S
NT = TOK // TT
KC = H // 128
KT, KP = 12, 125
NH, NKV, HD = 16, 4, 128
KVW = NKV * HD
NR = 8
RP = 2 * S
HD1 = H // NH
NE, NX, M = 32, 34, 176
EPG, NG, TOPG, TOPK = 8, 4, 2, 6
MT = M - 128
F = 1024
FB = F // 128
WS = 64.0
MAGIC = 12582912.0
LN_EPS, RMS_EPS = 1e-5, 1e-6


class Counted:

    def __init__(self, eng, sem):
        self.eng, self.sem, self.n = eng, sem, 0

    def __call__(self, ins):
        ins.then_inc(self.sem, 1)
        self.n += 1
        return self

    def done(self):
        self.eng.wait_ge(self.sem, self.n)


def wait(eng, sem, value):
    if isinstance(value, int) and value <= 0:
        return
    eng.wait_ge(sem, value)


def each(eng, n, body):
    body(0)
    with eng.Fori(1, n) as i:
        body(i)


def later(tile, d):
    n, par, half = tile
    return n + d, (par + d) % 2, half + (par + d) // 2


def exists(tile, count):
    return not isinstance(tile[0], int) or 0 <= tile[0] < count


def pipeline(eng, count, steps):
    low, high = min(d for _, d in steps), max(d for _, d in steps)

    def turn(tile):
        for stage, d in steps:
            if exists(later(tile, d), count):
                stage(*later(tile, d))

    first = 2 - low
    pairs = (count - high - first) // 2
    for t in range(-high, first):
        turn((t, t % 2, t // 2))
    with eng.Fori(0, pairs) as i:
        for k in range(first, first + 2):
            turn((2 * i + k, k % 2, i + k // 2))
    for t in range(first + 2 * pairs, count - low):
        turn((t, t % 2, t // 2))


def passed(eng, gate):
    eng.sem_inc(gate, 1)


def three_products(nc, out, a_hi, a_lo, b_hi, b_lo, start, stop):
    nc.tensor.matmul(out, a_hi, b_hi, start=start, stop=False)
    nc.tensor.matmul(out, a_hi, b_lo, start=False, stop=False)
    return nc.tensor.matmul(out, a_lo, b_hi, start=False, stop=stop)


class Alloc:
    def __init__(self, nc, ctx):
        self.nc, self.ctx, self.sems = nc, ctx, []

    def sb(self, name, shape, dt=F32):
        return self.ctx.enter_context(self.nc.sbuf_tensor(name, shape, dt))

    def ps(self, name, shape, dt=F32):
        return self.ctx.enter_context(self.nc.psum_tensor(name, shape, dt))

    def sem(self, name):
        self.sems.append(self.nc.alloc_semaphore(name))
        return self.sems[-1]


@contextmanager
def phase(nc):
    with ExitStack() as ctx:
        a = Alloc(nc, ctx)
        yield ctx, a
    nc.clear_and_free_semaphores(a.sems)
    nc.all_engine_barrier()


def constants(nc, g):
    with phase(nc) as (ctx, a):
        made = a.sem("const_made")
        block = ctx.enter_context(nc.Block())

        @block.gpsimd
        def _(pool):
            c = Counted(pool, made)
            c(nc.gpsimd.memset(g.ident[:], 0.0))
            c(nc.gpsimd.memset(g.ident16[:], 0.0))
            c(nc.gpsimd.memset(g.blk16[:], 1.0))
            c(nc.gpsimd.memset(g.mhalf[:], -0.5)).done()
            for t in (g.ident, g.ident16):
                c(nc.gpsimd.affine_select(out=t[:], in_=t[:], compare_op=ALU.not_equal, fill=1.0, base=0,
                                          pattern=[[-1, 128]], channel_multiplier=1))
            c(nc.gpsimd.affine_select(out=g.blk16[:], in_=g.blk16[:], compare_op=ALU.is_ge, fill=0.0, base=0,
                                      pattern=[[-16, 8]], channel_multiplier=1)).done()
            c(nc.gpsimd.affine_select(out=g.blk16[:], in_=g.blk16[:], compare_op=ALU.is_ge, fill=0.0, base=15,
                                      pattern=[[16, 8]], channel_multiplier=-1)).done()

        @block.vector
        def _(dve):
            dve.wait_ge(made, 8)
            nc.vector.tensor_reduce(g.evenodd[:], g.blk16[:].rearrange("p (c e) -> p e c", e=2), AX.X, ALU.add)


def q0_phase(nc, g, io):
    with phase(nc) as (ctx, a):
        wst = a.sb("q_wst", [128, KC, NH * HD])
        wqh = a.sb("q_wqh", [128, KC, NH * HD], F16)
        wql = a.sb("q_wql", [128, KC, NH * HD], F16)
        bq = a.sb("q_bq", [TT, NH * HD])
        wcol = a.sb("q_wcol", [128, 3])
        xt = a.sb("q_x", [TT, 2, H])
        st6 = a.sb("q_st6", [TT, 6])
        mv = a.sb("q_mv", [TT, 2])
        ve = a.sb("q_ve", [TT, 1])
        rs = a.sb("q_rs", [TT, 1])
        xn = a.sb("q_xn", [TT, H])
        xTh = a.sb("q_xTh", [128, KC, TT], F16)
        xTl = a.sb("q_xTl", [128, KC, TT], F16)
        qb = a.sb("q_qb", [TT, 2, NH * HD])
        qq = a.sb("q_qq", [TT, 2, NH * HD])
        qn = a.sb("q_qn", [TT, 2, NH * HD])
        ss = a.sb("q_ss", [TT, NH])
        ssv = a.sb("q_ssv", [TT, 2, NH])
        rq = a.sb("q_rq", [TT, 2, NH])
        qTh = a.sb("q_qTh", [128, 2, 2, NR, 2, S], F16)
        qTl = a.sb("q_qTl", [128, 2, 2, NR, 2, S], F16)
        pX = a.ps("q_pX", [128, 512])
        pQ = [a.ps(f"q_pQ{i}", [128, 512]) for i in range(4)]
        pT = [a.ps(f"q_pT{i}", [128, 512]) for i in range(2)]
        w_in, b_in = a.sem("q_w_in"), a.sem("q_b_in")
        x_in = [a.sem(f"q_x_in{i}") for i in range(2)]
        out_done = [a.sem(f"q_out{i}") for i in range(2)]
        w_hi = a.sem("q_w_hi")
        dve_own, pool_own, gate, q_sum = a.sem("q_dve"), a.sem("q_pool"), a.sem("q_gate"), a.sem("q_sum")
        var_ready, rstd_ready, xn_ready = a.sem("q_var"), a.sem("q_rstd"), a.sem("q_xn")
        xT_done, xT_hi, xT_lo = a.sem("q_xTd"), a.sem("q_xTh_"), a.sem("q_xTl_")
        q_done, q_biased, q_sq, q_ss, q_norm = (a.sem("q_" + s) for s in ("done", "biased", "sq", "ssd", "norm"))
        qT_done, qT_hi, qT_lo = a.sem("q_qTd"), a.sem("q_qTh_"), a.sem("q_qTl_")
        block = ctx.enter_context(nc.Block())

        @block.sync
        def _(sp):
            sp.dma_start(wst[:], io.Wq.rearrange("(c p) n -> p c n", p=128)).then_inc(w_in, 16)
            sp.dma_start(bq[:], io.bq.rearrange("(a n) -> a n", a=1).to_broadcast([TT, NH * HD])).then_inc(b_in, 16)
            sp.dma_start(wcol[:, 0:1], io.qn_w.rearrange("(p a) -> p a", a=1)).then_inc(b_in, 16)
            sp.dma_start(wcol[:, 1:2], io.kn_w.rearrange("(p a) -> p a", a=1)).then_inc(b_in, 16)

            def load(t, k, _):
                wait(sp, xn_ready, t - 1)
                sp.dma_start(xt[:, k, :], io.x[ds(t * TT, TT), :]).then_inc(x_in[k], 16)

            def store(t, k, _):
                sp.wait_ge(qT_lo, 8 * t + 8)
                for b in range(2):
                    for buf, o in ((qTh, io.qh), (qTl, io.ql)):
                        sp.dma_start(o[ds(2 * t + b, 1), :, :].rearrange("a p n -> p (a n)"),
                                     buf[:, k, b].rearrange("p r e q -> p (r e q)")).then_inc(out_done[k], 16)

            pipeline(sp, NT, [(load, 4), (store, -2)])
            for k in range(2):
                sp.wait_ge(out_done[k], 64 * (NT // 2))

        @block.gpsimd
        def _(pool):

            def rstd(t, k, _):
                pool.wait_ge(var_ready, t + 1)
                nc.gpsimd.tensor_tensor(rs[:], ve[:], g.mhalf[0:TT, 0:1], ALU.pow).then_inc(rstd_ready, 1)

            def normalise(t, k, _):
                pool.wait_ge(q_ss, t + 1)
                nc.gpsimd.tensor_tensor(rq[:, k], ssv[:, k], g.mhalf[0:TT, 0:NH], ALU.pow).then_inc(pool_own, 1)
                pool.wait_ge(pool_own, t + 1)
                wait(pool, qT_done, 4 * t - 4)
                nc.gpsimd.tensor_tensor(qn[:, k].rearrange("p (h d) -> p h d", d=HD),
                                        qb[:, k].rearrange("p (h d) -> p h d", d=HD),
                                        rq[:, k].unsqueeze(2).to_broadcast([TT, NH, HD]),
                                        ALU.mult).then_inc(q_norm, 1)

            pipeline(pool, NT, [(rstd, 2), (normalise, -1)])

        @block.scalar
        def _(act):
            act.wait_ge(w_in, 16)
            for c in range(KC):
                nc.scalar.activation(wqh[:, c, :], wst[:, c, :], ACT.Copy, scale=WS).then_inc(w_hi, 1)

            def split_x(t, k, _):
                act.wait_ge(xT_done, t + 1)
                nc.scalar.activation(xTh[:], pX[:, 0:KC * TT].rearrange("p (c q) -> p c q", q=TT),
                                     ACT.Copy).then_inc(xT_hi, 1)

            def square(t, k, _):
                act.wait_ge(q_biased, 4 * t + 4)
                wait(act, q_ss, t - 1)
                nc.scalar.activation(qq[:, k], qb[:, k], ACT.Square).then_inc(q_sq, 1)

            def split_q(t, k, half):
                wait(act, out_done[k], 64 * half)
                for j in range(4):
                    act.wait_ge(qT_done, 4 * t + j + 1)
                    nc.scalar.activation(qTh[:, k, :, 2 * j:2 * j + 2, :, 0:S].rearrange("p b r e q -> p b (r e) q"),
                                         pT[j % 2][:, 0:4 * TT].rearrange("p (h b q) -> p b h q", h=4, b=2),
                                         ACT.Copy, scale=wcol[:, 2:3]).then_inc(qT_hi, 1)

            pipeline(act, NT, [(split_x, 1), (square, 0), (split_q, -2)])

        @block.vector
        def _(dve):
            own = Counted(dve, dve_own)
            dve.wait_ge(b_in, 48)
            own(nc.vector.tensor_tensor(wcol[:, 2:3], wcol[:, 0:1], wcol[:, 1:2], ALU.mult)).done()
            own(nc.vector.tensor_scalar(wcol[:, 2:3], wcol[:, 2:3], float(HD) ** -0.5, None, ALU.mult))
            for c in range(KC):
                dve.wait_ge(w_hi, c + 1)
                own(nc.vector.scalar_tensor_tensor(wql[:, c, :], wst[:, c, :], WS, wqh[:, c, :],
                                                   ALU.mult, ALU.subtract))
            own.done()
            base = own.n

            def bias(t, k, _):
                wait(dve, q_norm, t - 1)
                for j in range(4):
                    cols = slice(j * 512, (j + 1) * 512)
                    dve.wait_ge(q_done, 4 * t + j + 1)
                    nc.vector.scalar_tensor_tensor(qb[:, k, cols], pQ[j][0:TT, :], 1 / WS, bq[:, cols], ALU.mult,
                                                   ALU.add).then_inc(q_biased, 1)

            def variance(t, k, half):
                dve.wait_ge(x_in[k], 16 * half + 16)
                nc.vector.bn_stats(st6[:], xt[:, k, :]).then_inc(dve_own, 1)
                dve.wait_ge(dve_own, base + 2 * t + 1)
                passed(dve, gate)
                nc.vector.bn_aggr(mv[:], st6[:]).then_inc(dve_own, 1)
                dve.wait_ge(dve_own, base + 2 * t + 2)
                nc.vector.tensor_scalar(ve[:], mv[:, 1:2], LN_EPS, None, ALU.add).then_inc(var_ready, 1)

            def split_x(t, k, _):
                dve.wait_ge(xT_hi, t + 1)
                nc.vector.tensor_tensor(xTl[:], pX[:, 0:KC * TT].rearrange("p (c q) -> p c q", q=TT), xTh[:],
                                        ALU.subtract).then_inc(xT_lo, 1)

            def split_q(t, k, _):
                for j in range(4):
                    dve.wait_ge(qT_hi, 4 * t + j + 1)
                    for b in range(2):
                        nc.vector.scalar_tensor_tensor(
                            qTl[:, k, b, 2 * j:2 * j + 2, :, 0:S].rearrange("p r e q -> p (r e) q"),
                            pT[j % 2][:, 0:4 * TT].rearrange("p (h b q) -> p b h q", h=4, b=2)[:, b],
                            wcol[:, 2:3],
                            qTh[:, k, b, 2 * j:2 * j + 2, :, 0:S].rearrange("p r e q -> p (r e) q"),
                            ALU.mult, ALU.subtract).then_inc(qT_lo, 1)

            def sum_squares(t, k, _):
                dve.wait_ge(q_sq, t + 1)
                nc.vector.tensor_reduce(ss[:], qq[:, k].rearrange("p (h d) -> p h d", d=HD), AX.X,
                                        ALU.add).then_inc(q_sum, 1)
                dve.wait_ge(q_sum, t + 1)
                nc.vector.tensor_scalar(ssv[:, k], ss[:], 1.0 / HD, RMS_EPS, ALU.mult, ALU.add).then_inc(q_ss, 1)

            def normalise(t, k, _):
                dve.wait_ge(rstd_ready, t + 1)
                nc.vector.tensor_scalar(xn[:], xt[:, k, :], mv[:, 0:1], rs[:], ALU.subtract,
                                        ALU.mult).then_inc(xn_ready, 1)

            pipeline(dve, NT, [(variance, 2), (bias, 0), (sum_squares, -1), (split_x, 1), (split_q, -2),
                               (normalise, 2)])

        @block.tensor
        def _(pe):
            pe.wait_ge(dve_own, 4)

            def project(t, k, _):
                pe.wait_ge(xT_lo, t + 1)
                for j in range(4):
                    wait(pe, q_biased, 4 * t + j - 3)
                    for c in range(KC):
                        cols = slice(j * 512, (j + 1) * 512)
                        last = three_products(nc, pQ[j][0:TT, :], xTh[:, c, :], xTl[:, c, :], wqh[:, c, cols],
                                              wql[:, c, cols], start=(c == 0), stop=(c == KC - 1))
                    last.then_inc(q_done, 1)

            def turn_x(t, k, _):
                pe.wait_ge(xn_ready, t + 1)
                for c in range(KC):
                    last = nc.tensor.transpose(pX[:, c * TT:(c + 1) * TT], xn[:, c * 128:(c + 1) * 128],
                                               g.ident[0:TT, 0:TT])
                last.then_inc(xT_done, 1)

            def turn_q(t, k, _):
                pe.wait_ge(q_norm, t + 1)
                for j in range(4):
                    wait(pe, qT_lo, 8 * t + 2 * j - 2)
                    for h in range(4):
                        last = nc.tensor.transpose(pT[j % 2][:, h * TT:(h + 1) * TT],
                                                   qn[:, k, (4 * j + h) * HD:(4 * j + h + 1) * HD],
                                                   g.ident[0:TT, 0:TT])
                    last.then_inc(qT_done, 1)

            pipeline(pe, NT, [(project, 0), (turn_x, 1), (turn_q, -2)])


ORDER0 = {
    "tensor": """
        S0 T23< K0 V21< C1 V22< V23< T0 U0 K1 T1 T2 C2 S1 R0 U1 V0 V1 K2 C3 T3 T4 U2 R1 S2 V2 C4 T5 K3 V3 R2 V4
        T6 K4 U3 T7 T8 C5 S3 U4 V5 K5 V6 R3 C6 T9 V7 T10 V8 K6 R4 T11 V9 U5 R5 S4 C7 U6 V10 V11 K7 R6 T12 C8 S5
        T13 U7 T14 K8 V12 C9 V13 R7 V14 K9 T15 U8 C10 S6 T16 U9 K10 T17 V15 V16 R8 C11 T18 T19 V17 R9 K11 S7 U10
        V18 U11 R10 T20 V19 R11 T21 V20 T22 C0>""",
    "scalar": """
        S0 C1 O7< T0 U0 T1 T2 C2 R0 U1 S1 C3 T3 T4 U2 R1 O0 C4 T5 S2 R2 T6 U3 T7 T8 C5 U4 O1 S3 R3 C6 T9 T10 O2
        R4 T11 U5 R5 C7 U6 S4 O3 R6 T12 C8 T13 U7 T14 S5 C9 R7 O4 T15 U8 C10 T16 U9 S6 T17 R8 C11 T18 T19 O5 R9
        U10 S7 U11 R10 T20 R11 T21 O6 T22 C0> T23""",
    "vector": """
        S0 T23< K0 C1 Q0 T0 U0 K1 T1 T2 C2 Q1 S1 R0 U1 K2 C3 T3 T4 Q2 U2 R1 S2 C4 T5 K3 R2 Q3 T6 K4 U3 T7 T8 C5
        Q4 S3 U4 K5 R3 C6 Q5 T9 T10 K6 R4 T11 Q6 U5 R5 S4 C7 U6 K7 R6 T12 C8 Q7 S5 T13 U7 T14 K8 C9 R7 Q8 K9 T15
        U8 C10 S6 Q9 T16 U9 K10 T17 R8 C11 T18 Q10 T19 R9 K11 S7 U10 Q11 U11 R10 T20 R11 T21 T22 C0>""",
}
ORDER1 = {
    "tensor": """
        S0 T22< T23< K0 S1 V20< V21< V22< V23< T0 T1 U0 K1 T2 T3 V0 V1 S2 C3 U1 T4 T5 S3 K2 T6 V2 U2 V3 T7 V4 T8
        V5 C4 C5 T9 V6 T10 S4 K3 T11 K4 S5 V7 V8 V9 T12 T13 K5 V10 U3 T14 T15 V11 V12 S6 U4 T16 T17 U5 V13 S7
        C0> T18 T19 V14 V15 V16 V17 C1> C2> V18 T20 V19 T21""",
    "scalar": """
        S0 K0 O0< T0 T1 S1 U0 K1 T2 T3 C3 U1 T4 S2 T5 K2 T6 S3 U2 T7 T8 C4 C5 T9 T10 K3 T11 S4 K4 T12 T13 S5 K5
        U3 T14 T15 U4 T16 T17 S6 U5 C0> T18 T19 S7 C1> C2> T20 T21 T22 T23""",
    "vector": """
        S0 T22< T23< S1 K0 O0< T0 T1 U0 K1 T2 T3 S2 C3 U1 T4 S3 T5 K2 T6 U2 T7 T8 C4 C5 T9 S4 T10 K3 T11 S5 K4
        T12 T13 K5 U3 T14 T15 S6 U4 T16 T17 S7 U5 C0> T18 T19 C1> C2> T20 T21""",
}
WORK_STEPS = "CKRU"
NQ = 3 * NR


def listing(text):
    steps = []
    for token in text.split():
        off = {"<": -1, ">": 1}.get(token[-1], 0)
        steps.append((token[0], int(token[1:].rstrip("<>")), off))
    return steps


def work_of(pe):
    steps = [(kind, n) for kind, n, off in pe if kind in WORK_STEPS and off == 1]
    return steps + [(kind, n) for kind, n, off in pe if kind in WORK_STEPS and off == 0]


def batches(eng, steps, attend, work):
    def turn(batch):
        for kind, n, off in steps:
            makes = kind in WORK_STEPS + "Q"
            at = later(batch, off + 1 if makes else off)
            if exists(at, B):
                (work if makes else attend)(kind, n, at)

    for g_ in (-2, -1, 0):
        turn((g_, g_ % 2, g_ // 2))
    with eng.Fori(0, (B - 4) // 2) as i:
        turn((2 * i + 1, 1, i))
        turn((2 * i + 2, 0, i + 1))
    for g_ in range(B - 3, B + 1):
        turn((g_, g_ % 2, g_ // 2))


def attn0_phase(nc, g, io):
    order = {eng: listing(text) for eng, text in ORDER0.items()}
    WORK = work_of(order["tensor"])
    AT = {w: n for n, w in enumerate(WORK)}
    NW = len(WORK)
    HI = {w: n for n, w in enumerate([w for w in WORK if w[0] != "K"])}
    NHI = len(HI)
    with phase(nc) as (ctx, a):
        wst = a.sb("a_wst", [128, 2, KC, KVW])
        wk = a.sb("a_wk", [128, KC, 2, KVW], F16)
        wv = a.sb("a_wv", [128, KC, 2, KVW], F16)
        bk = a.sb("a_bk", [KP, KVW])
        cx = a.sb("a_ctx", [KP, 2, KT, H])
        cTh = a.sb("a_cTh", [128, 2, KC, KP], F16)
        cTl = a.sb("a_cTl", [128, 2, KC, KP], F16)
        kb = a.sb("a_kb", [KP, 4, KVW])
        ksq = a.sb("a_ksq", [KP, 2, KVW])
        ssk = a.sb("a_ssk", [KP, 2, NKV])
        rk = a.sb("a_rk", [KP, 2, 2, NKV])
        kTh = a.sb("a_kTh", [128, 2, NKV, SE], F16)
        kTl = a.sb("a_kTl", [128, 2, NKV, SE], F16)
        vh = a.sb("a_vh", [KP, 2, KT, KVW], F16)
        vl = a.sb("a_vl", [KP, 2, KT, KVW], F16)
        qh = a.sb("a_qh", [128, 2, NR, RP], F16)
        ql = a.sb("a_ql", [128, 2, NR, RP], F16)
        pr = a.sb("a_pr", [RP, 2, SE])
        pTh = a.sb("a_pTh", [KP, 2, KT, RP], F16)
        pTl = a.sb("a_pTl", [KP, 2, KT, RP], F16)
        nmax = a.sb("a_nmax", [RP, 2, NR])
        rsum = a.sb("a_rsum", [RP, 2, NR])
        inv = a.sb("a_inv", [RP, 2, NR])
        mask = a.sb("a_mask", [RP, SE])
        ot = a.sb("a_ot", [RP, 2, NR, HD])
        ps_s = a.ps("a_ps", [128, 3, 512])
        ps_t = [a.ps(f"a_pt{i}", [128, 512]) for i in range(2)]
        ps_w = [a.ps(f"a_pw{i}", [128, 512]) for i in range(2)]
        ps_o = a.ps("a_po", [128, HD])
        w_in = [a.sem(f"a_w_in{i}") for i in range(2)]
        pool_own, pool_gate = a.sem("a_pool_own"), a.sem("a_pool_gate")
        b_in, w_hi, w_lo, gate = a.sem("a_b_in"), a.sem("a_w_hi"), a.sem("a_w_lo"), a.sem("a_gate")
        ctx_in = [a.sem(f"a_ctx_in{i}") for i in range(2)]
        q_in = [a.sem(f"a_q_in{i}") for i in range(2)]
        stored = [a.sem(f"a_stored{i}") for i in range(2)]
        names = ("scores_done nmax_ready exp_done turn_done turn_hi turn_lo values_done inv_ready o_taken ot_free "
                 "work_done work_hi work_taken k_squared k_ssq inv_scaled k_normed own")
        s = {n: a.sem("a_" + n) for n in names.split()}
        block = ctx.enter_context(nc.Block())

        @block.sync
        def _(sp):
            sp.sem_inc(s["ot_free"], 2)
            for n, w in enumerate((io.Wk, io.Wv)):
                sp.dma_start(wst[:, n], w.rearrange("(c p) n -> p c n", p=128)).then_inc(w_in[n], 16)
            sp.dma_start(bk[:], io.bk.rearrange("(a n) -> a n", a=1).to_broadcast([KP, KVW])).then_inc(b_in, 16)

            def load_ctx(G, par):
                src = io.ctx[ds(G, 1), :, :].rearrange("a (p k) d -> (a p) k d", k=KT)
                sp.dma_start(cx[0:120, par], src[0:120]).then_inc(ctx_in[par], 16)
                sp.dma_start(cx[120:KP, par], src[120:KP]).then_inc(ctx_in[par], 16)

            def load_q(G, par):
                for t, o in ((qh, io.qh), (ql, io.ql)):
                    sp.dma_start(t[:, par].rearrange("p r c -> p (r c)"),
                                 o[ds(G, 1), :, :].rearrange("a p n -> p (a n)")).then_inc(q_in[par], 16)

            sp.wait_ge(s["own"], 1)
            for e in range(2):
                sp.dma_start(mask[S * e:S * e + S, :], io.mask[0]).then_inc(b_in, 16)
            load_ctx(0, 0)
            load_ctx(1, 1)
            load_q(0, 0)

            def step(g_, par, half, nxt, produce):
                if produce:
                    wait(sp, s["scores_done"], NR * g_)
                    load_q(g_ + 1, 1 - par)
                sp.wait_ge(s["o_taken"], NR * g_ + NR)
                for e in range(2):
                    sp.dma_start(io.o0[ds(g_ * S, S), :].rearrange("q (r e d) -> q r e d", e=2, d=HD)[:, :, e, :],
                                 ot[S * e:S * e + S, par]).then_inc(stored[par], 16)
                sp.wait_ge(stored[par], 32 * half + 32)
                sp.sem_inc(s["ot_free"], 1)

            def step_ctx(g_, par, half, nxt, produce, load):
                if load:
                    sp.wait_ge(s["work_done"], NW * g_ + AT["C", KT - 1] + 1)
                    load_ctx(g_ + 2, par)
                step(g_, par, half, nxt, produce)

            step_ctx(0, 0, 0, 0, True, True)
            with sp.Fori(0, (B - 4) // 2) as i:
                step_ctx(2 * i + 1, 1, i, i + 1, True, True)
                step_ctx(2 * i + 2, 0, i + 1, i + 1, True, True)
            step_ctx(B - 3, 1, (B - 3) // 2, 0, True, True)
            step_ctx(B - 2, 0, (B - 2) // 2, 0, True, False)
            step_ctx(B - 1, 1, (B - 1) // 2, 0, False, False)
            for k in range(2):
                sp.wait_ge(stored[k], 32 * (B // 2))

        @block.scalar
        def _(act):
            for n, w in enumerate((wk, wv)):
                act.wait_ge(w_in[n], 16)
                nc.scalar.activation(w[:, :, 0, :], wst[:, n], ACT.Copy, scale=WS).then_inc(w_hi, 1)

            def work(kind, kt, batch):
                if kind == "K":
                    return
                G, par, _ = batch
                n = AT[kind, kt]
                act.wait_ge(s["work_done"], NW * G + n + 1)
                bank = ps_w[n % 2]
                if kind == "C":
                    out, src = cTh[:, kt % 2], bank[:, 0:KC * KP].rearrange("p (c k) -> p c k", k=KP)
                elif kind == "U":
                    out, src = vh[:, par, kt], bank[0:KP, :]
                else:
                    out = kTh[:, par, :, kt * KP:(kt + 1) * KP]
                    src = bank[:, 0:NKV * KP].rearrange("p (h k) -> p h k", k=KP)
                nc.scalar.activation(out, src, ACT.Copy).then_inc(s["work_hi"], 1)

            def attend(kind, n, batch):
                b, par, _ = batch
                if kind == "S":
                    act.wait_ge(s["nmax_ready"], NR * b + n + 1)
                    nc.scalar.activation(pr[:, n % 2], pr[:, n % 2], ACT.Exp, scale=-1.0,
                                         bias=nmax[:, par, n:n + 1],
                                         accum_out=rsum[:, par, n:n + 1]).then_inc(s["exp_done"], 1)
                elif kind == "T":
                    r, third = n // 3, n % 3
                    act.wait_ge(s["turn_done"], NQ * b + n + 1)
                    nc.scalar.activation(pTh[:, r % 2, 4 * third:4 * third + 4].rearrange("p k c -> p (k c)"),
                                         ps_t[n % 2][0:KP, 0:4 * RP], ACT.Copy).then_inc(s["turn_hi"], 1)
                else:
                    if n == 0:
                        act.wait_ge(s["ot_free"], b + 1)
                    act.wait_ge(s["inv_ready"], NR * b + n + 1)
                    act.wait_ge(s["values_done"], NR * b + n + 1)
                    nc.scalar.activation(ot[:, par, n], ps_o[0:RP, :], ACT.Copy,
                                         scale=inv[:, par, n:n + 1]).then_inc(s["o_taken"], 1)

            batches(act, order["scalar"], attend, work)

        @block.vector
        def _(dve):
            nc.vector.memset(mask[:], 0.0).then_inc(s["own"], 1)
            for n, w in enumerate((wk, wv)):
                dve.wait_ge(w_hi, n + 1)
                nc.vector.scalar_tensor_tensor(w[:, :, 1, :], wst[:, n], WS, w[:, :, 0, :], ALU.mult,
                                               ALU.subtract).then_inc(w_lo, 1)
            dve.wait_ge(b_in, 48)

            def work(kind, kt, batch):
                G, par, _ = batch
                if kind == "Q":
                    dve.wait_ge(s["k_squared"], KT * G + kt + 1)
                    wait(dve, s["k_normed"], KT * G + kt - 1)
                    nc.vector.tensor_reduce(ssk[:, kt % 2], ksq[:, kt % 2].rearrange("p (h d) -> p h d", d=HD),
                                            AX.X, ALU.add).then_inc(s["k_ssq"], 1)
                    return
                n = AT[kind, kt]
                bank = ps_w[n % 2]
                if kind == "K":
                    dve.wait_ge(s["work_done"], NW * G + n + 1)
                    nc.vector.scalar_tensor_tensor(kb[:, kt % 4], bank[0:KP, :], 1 / WS, bk[:], ALU.mult,
                                                   ALU.add).then_inc(s["work_taken"], 1)
                    return
                dve.wait_ge(s["work_hi"], NHI * G + HI[kind, kt] + 1)
                if kind == "C":
                    out, hi = cTl[:, kt % 2], cTh[:, kt % 2]
                    src = bank[:, 0:KC * KP].rearrange("p (c k) -> p c k", k=KP)
                elif kind == "U":
                    out, hi, src = vl[:, par, kt], vh[:, par, kt], bank[0:KP, :]
                else:
                    cols = slice(kt * KP, (kt + 1) * KP)
                    out, hi = kTl[:, par, :, cols], kTh[:, par, :, cols]
                    src = bank[:, 0:NKV * KP].rearrange("p (h k) -> p h k", k=KP)
                nc.vector.tensor_tensor(out, src, hi, ALU.subtract).then_inc(s["work_taken"], 1)

            def attend(kind, n, batch):
                b, par, _ = batch
                if kind == "S":
                    dve.wait_ge(s["scores_done"], NR * b + n + 1)
                    passed(dve, gate)
                    nc.vector.tensor_tensor_reduce(
                        out=pr[:, n % 2].rearrange("p (a k) -> p a k", k=500), in0=ps_s[0:RP, :, 0:500],
                        in1=mask[:].rearrange("p (a k) -> p a k", k=500), scale=-1.0, scalar=3.0e38,
                        op0=ALU.add, op1=ALU.min, accum_out=nmax[:, par, n:n + 1]).then_inc(s["nmax_ready"], 1)
                    return
                r, third = n // 3, n % 3
                if third == 0:
                    R = NR * b + r
                    dve.wait_ge(s["exp_done"], R + 1)
                    nc.vector.tensor_scalar(inv[:, par, r:r + 1], rsum[:, par, r:r + 1], WS, None,
                                            ALU.mult).then_inc(s["inv_scaled"], 1)
                    dve.wait_ge(s["inv_scaled"], R + 1)
                    nc.vector.reciprocal(inv[:, par, r:r + 1], inv[:, par, r:r + 1]).then_inc(s["inv_ready"], 1)
                dve.wait_ge(s["turn_hi"], NQ * b + n + 1)
                part = (slice(None), r % 2, slice(4 * third, 4 * third + 4))
                nc.vector.tensor_tensor(pTl[part].rearrange("p k c -> p (k c)"), ps_t[n % 2][0:KP, 0:4 * RP],
                                        pTh[part].rearrange("p k c -> p (k c)"),
                                        ALU.subtract).then_inc(s["turn_lo"], 1)

            batches(dve, order["vector"], attend, work)

        @block.gpsimd
        def _(pool):
            def tile(G, kt):
                pool.wait_ge(s["work_taken"], NW * G + AT["K", kt] + 1)
                wait(pool, s["k_ssq"], KT * G + kt - 1)
                nc.gpsimd.tensor_tensor(ksq[:, kt % 2], kb[:, kt % 4], kb[:, kt % 4],
                                        ALU.mult).then_inc(s["k_squared"], 1)
                pool.wait_ge(s["k_ssq"], KT * G + kt + 1)
                passed(pool, pool_gate)
                nc.gpsimd.tensor_scalar(rk[:, kt % 2, 0], ssk[:, kt % 2], 1.0 / HD, RMS_EPS, ALU.mult,
                                        ALU.add).then_inc(pool_own, 1)
                pool.wait_ge(pool_own, 2 * (KT * G + kt) + 1)
                nc.gpsimd.tensor_tensor(rk[:, kt % 2, 1], rk[:, kt % 2, 0], g.mhalf[0:KP, 0:NKV],
                                        ALU.pow).then_inc(pool_own, 1)
                pool.wait_ge(pool_own, 2 * (KT * G + kt) + 2)
                k4 = kb[:, kt % 4].rearrange("p (h d) -> p h d", d=HD)
                nc.gpsimd.tensor_tensor(k4, k4, rk[:, kt % 2, 1].unsqueeze(2).to_broadcast([KP, NKV, HD]),
                                        ALU.mult).then_inc(s["k_normed"], 1)

            def batch(G):
                for kt in range(KT):
                    tile(G, kt)

            each(pool, B, batch)

        @block.tensor
        def _(pe):
            def work(kind, kt, batch):
                G, par, half = batch
                n = AT[kind, kt]
                bank = ps_w[n % 2]
                wait(pe, s["work_taken"], NW * G + n - 1)
                if kind == "C":
                    if kt == 0:
                        pe.wait_ge(ctx_in[par], 32 * half + 32)
                    for c in range(KC):
                        last = nc.tensor.transpose(bank[:, c * KP:(c + 1) * KP],
                                                   cx[:, par, kt, c * 128:(c + 1) * 128], g.ident[0:KP, 0:KP])
                elif kind in "KU":
                    pe.wait_ge(s["work_taken"], NW * G + AT["C", kt] + 1)
                    w = wk if kind == "K" else wv
                    if isinstance(G, int) and G == 0 and kt == 0:
                        pe.wait_ge(w_lo, 1 if kind == "K" else 2)
                    for c in range(KC):
                        last = three_products(nc, bank[0:KP, :], cTh[:, kt % 2, c], cTl[:, kt % 2, c],
                                              w[:, c, 0], w[:, c, 1], start=(c == 0), stop=(c == KC - 1))
                else:
                    pe.wait_ge(s["k_normed"], KT * G + kt + 1)
                    for h in range(NKV):
                        last = nc.tensor.transpose(bank[:, h * KP:(h + 1) * KP],
                                                   kb[:, kt % 4, h * HD:(h + 1) * HD], g.ident[0:KP, 0:KP])
                last.then_inc(s["work_done"], 1)

            def attend(kind, n, batch):
                b, par, half = batch
                if kind == "S":
                    if n == 0:
                        pe.wait_ge(q_in[par], 32 * half + 32)
                        pe.wait_ge(s["work_taken"], NW * b + NW)
                    wait(pe, s["nmax_ready"], NR * b + n)
                    for j in range(3):
                        cols = slice(500 * j, 500 * j + 500)
                        last = three_products(nc, ps_s[0:RP, j, 0:500], qh[:, par, n], ql[:, par, n],
                                              kTh[:, par, n // 2, cols], kTl[:, par, n // 2, cols], True, True)
                    last.then_inc(s["scores_done"], 1)
                    return
                r, third = n // 3, n % 3
                if kind == "T":
                    if third == 0:
                        pe.wait_ge(s["exp_done"], NR * b + r + 1)
                    wait(pe, s["turn_lo"], NQ * b + n - 1)
                    for j in range(4):
                        kt = 4 * third + j
                        last = nc.tensor.transpose(ps_t[n % 2][0:KP, RP * j:RP * j + RP],
                                                   pr[:, r % 2, kt * KP:(kt + 1) * KP],
                                                   g.ident[0:RP, 0:RP])
                    last.then_inc(s["turn_done"], 1)
                else:
                    if third == 0:
                        wait(pe, s["o_taken"], NR * b + r)
                    pe.wait_ge(s["turn_lo"], NQ * b + n + 1)
                    for kt in range(4 * third, 4 * third + 4):
                        cols = slice((r // 2) * HD, (r // 2 + 1) * HD)
                        last = three_products(nc, ps_o[0:RP, :], pTh[:, r % 2, kt], pTl[:, r % 2, kt],
                                              vh[:, par, kt, cols], vl[:, par, kt, cols],
                                              start=(kt == 0), stop=(kt == KT - 1))
                    if third == 2:
                        last.then_inc(s["values_done"], 1)

            batches(pe, order["tensor"], attend, work)


def mix0_phase(nc, g, io):
    with phase(nc) as (ctx, a):
        wst = a.sb("m_wst", [128, NH, H])
        wo = a.sb("m_wo", [128, 2, NH, H], F16)
        gst = a.sb("m_gst", [128, KC, NE])
        gw = a.sb("m_gw", [128, 2, KC, NE], F16)
        bv = a.sb("m_bv", [128, NKV])
        ot = a.sb("m_ot", [TT, 2, NH * HD])
        xt = a.sb("m_x", [TT, 2, H])
        oTh = a.sb("m_oTh", [128, 2, NH, TT], F16)
        oTl = a.sb("m_oTl", [128, 2, NH, TT], F16)
        st6 = a.sb("m_st6", [TT, 6])
        mv = a.sb("m_mv", [TT, 2])
        ve = a.sb("m_ve", [TT, 1])
        rs = a.sb("m_rs", [TT, 1])
        xn = a.sb("m_xn", [TT, H])
        cur = a.sb("m_cur", [128, 2, KC, TT], F16)
        lg = a.sb("m_lg", [TT, NT, NE])
        sc = a.sb("m_sc", [TT, NT, NE])
        gm = a.sb("m_gm", [TT, NT, 16])
        g8 = a.sb("m_g8", [TT, NT, 8])
        gr = a.sb("m_gr", [TT, NT, 16])
        gk = a.sb("m_gk", [TT, NT, 2, NG])
        ms = a.sb("m_ms", [TT, NT, NE + 8])
        er = a.sb("m_er", [TT, NT, NE + 8])
        sm = a.sb("m_sm", [TT, NT])
        pT = [a.ps(f"m_pT{i}", [128, 512]) for i in range(4)]
        pY = a.ps("m_pY", [128, 512])
        pX = a.ps("m_pX", [128, 512])
        pL = a.ps("m_pL", [128, 512])
        w_in = [a.sem(f"m_w_in{i}") for i in range(4)]
        b_in, g_in, gate = a.sem("m_b_in"), a.sem("m_g_in"), a.sem("m_gate")
        o_in = [a.sem(f"m_o_in{i}") for i in range(2)]
        x_in = [a.sem(f"m_x_in{i}") for i in range(2)]
        names = ("w_hi w_lo g_hi oT_done oT_hi oT_lo y_done x_ready var rstd xn_ready xT_done xT_hi xT_lo kept "
                 "lg_done lg_taken dve exp")
        s = {n: a.sem("m_" + n) for n in names.split()}
        block = ctx.enter_context(nc.Block())

        @block.sync
        def _(sp):
            sp.dma_start(gst[:], io.gate_w.rearrange("(c p) n -> p c n", p=128)).then_inc(g_in, 16)
            with nc.allow_non_contiguous_dma(reason="512 values"):
                sp.dma_start(bv[:], io.bv.rearrange("(h p) -> p h", p=128)).then_inc(b_in, 16)
            for n in range(4):
                sp.dma_start(wst[:, 4 * n:4 * n + 4],
                             io.Wo[512 * n:512 * n + 512, :].rearrange("(h p) n -> p h n", p=128)).then_inc(w_in[n], 16)

            def load_o(t, k, _):
                wait(sp, s["oT_done"], 4 * t - 4)
                sp.dma_start(ot[:, k, :], io.o0[ds(t * TT, TT), :]).then_inc(o_in[k], 16)

            def load_x(t, k, _):
                wait(sp, s["x_ready"], t - 1)
                sp.dma_start(xt[:, k, :], io.x[ds(t * TT, TT), :]).then_inc(x_in[k], 16)

            pipeline(sp, NT, [(load_o, 2), (load_x, 1)])

        @block.gpsimd
        def _(pool):
            def rstd(t, k, _):
                pool.wait_ge(s["var"], t + 1)
                nc.gpsimd.tensor_tensor(rs[:], ve[:], g.mhalf[0:TT, 0:1], ALU.pow).then_inc(s["rstd"], 1)

            def keep(t, k, _):
                pool.wait_ge(s["xT_lo"], t + 1)
                for n in range(2):
                    nc.gpsimd.tensor_copy(g.xT[:, n, :, ds(t * TT, TT)], cur[:, n]).then_inc(s["kept"], 1)

            pipeline(pool, NT, [(rstd, 0), (keep, -1)])

        @block.scalar
        def _(act):
            act.wait_ge(g_in, 16)
            nc.scalar.activation(gw[:, 0], gst[:], ACT.Copy, scale=WS).then_inc(s["g_hi"], 1)
            for n in range(4):
                act.wait_ge(w_in[n], 16)
                part = slice(4 * n, 4 * n + 4)
                nc.scalar.activation(wo[:, 0, part], wst[:, part], ACT.Copy, scale=WS).then_inc(s["w_hi"], 1)
            act.wait_ge(b_in, 16)

            def split_o(t, k, _):
                for j in range(4):
                    act.wait_ge(s["oT_done"], 4 * t + j + 1)
                    nc.scalar.activation(oTh[:, k, 4 * j:4 * j + 4].rearrange("p h q -> p (h q)"),
                                         pT[j][:, 0:4 * TT], ACT.Identity, bias=bv[:, j:j + 1])\
                        .then_inc(s["oT_hi"], 1)

            def split_x(t, k, _):
                act.wait_ge(s["xT_done"], t + 1)
                wait(act, s["kept"], 2 * t)
                nc.scalar.activation(cur[:, 0], pX[:, 0:KC * TT].rearrange("p (c q) -> p c q", q=TT),
                                     ACT.Copy).then_inc(s["xT_hi"], 1)

            def take_logits(t, k, _):
                act.wait_ge(s["lg_done"], t + 1)
                nc.scalar.activation(lg[:, ds(t, 1), :].rearrange("p a n -> p (a n)"), pL[0:TT, 0:NE],
                                     ACT.Copy).then_inc(s["lg_taken"], 1)

            pipeline(act, NT, [(split_o, 1), (take_logits, -2), (split_x, -1)])
            act.wait_ge(s["lg_taken"], NT)
            nc.scalar.activation(sc[:], lg[:], ACT.Exp, scale=-1.0 / WS).then_inc(s["exp"], 1)

        @block.vector
        def _(dve):
            own = Counted(dve, s["dve"])
            own(nc.vector.memset(gm[:], -5.0))
            own(nc.vector.memset(ms[:], -5.0))
            dve.wait_ge(s["g_hi"], 1)
            own(nc.vector.scalar_tensor_tensor(gw[:, 1], gst[:], WS, gw[:, 0], ALU.mult, ALU.subtract))
            for n in range(4):
                dve.wait_ge(s["w_hi"], n + 1)
                part = slice(4 * n, 4 * n + 4)
                nc.vector.scalar_tensor_tensor(wo[:, 1, part], wst[:, part], WS, wo[:, 0, part],
                                               ALU.mult, ALU.subtract).then_inc(s["w_lo"], 1)
            base = own.n

            def split_o(t, k, _):
                for j in range(4):
                    dve.wait_ge(s["oT_hi"], 4 * t + j + 1)
                    part = (slice(None), k, slice(4 * j, 4 * j + 4))
                    nc.vector.scalar_tensor_tensor(oTl[part].rearrange("p h q -> p (h q)"), pT[j][:, 0:4 * TT],
                                                   bv[:, j:j + 1], oTh[part].rearrange("p h q -> p (h q)"),
                                                   ALU.add, ALU.subtract).then_inc(s["oT_lo"], 1)

            def residual(t, k, half):
                xrow = g.xs[:, ds(t, 1), :].rearrange("p a n -> p (a n)")
                dve.wait_ge(x_in[k], 16 * half + 16)
                dve.wait_ge(s["y_done"], t + 1)
                nc.vector.scalar_tensor_tensor(xrow, pY[0:TT, 0:H], 1 / WS, xt[:, k], ALU.mult,
                                               ALU.add).then_inc(s["x_ready"], 1)
                dve.wait_ge(s["x_ready"], t + 1)
                passed(dve, gate)
                nc.vector.bn_stats(st6[:], xrow).then_inc(s["dve"], 1)
                dve.wait_ge(s["dve"], base + 2 * t + 1)
                passed(dve, gate)
                nc.vector.bn_aggr(mv[:], st6[:]).then_inc(s["dve"], 1)
                dve.wait_ge(s["dve"], base + 2 * t + 2)
                nc.vector.tensor_scalar(ve[:], mv[:, 1:2], LN_EPS, None, ALU.add).then_inc(s["var"], 1)

            def normalise(t, k, _):
                xrow = g.xs[:, ds(t, 1), :].rearrange("p a n -> p (a n)")
                dve.wait_ge(s["rstd"], t + 1)
                nc.vector.tensor_scalar(xn[:], xrow, mv[:, 0:1], rs[:], ALU.subtract,
                                        ALU.mult).then_inc(s["xn_ready"], 1)

            def split_x(t, k, _):
                dve.wait_ge(s["xT_hi"], t + 1)
                nc.vector.tensor_tensor(cur[:, 1], pX[:, 0:KC * TT].rearrange("p (c q) -> p c q", q=TT),
                                        cur[:, 0], ALU.subtract).then_inc(s["xT_lo"], 1)

            pipeline(dve, NT, [(normalise, -1), (split_o, 1), (split_x, -1), (residual, 0)])
            own.n = base + 2 * NT
            dve.wait_ge(s["exp"], 1)
            own(nc.vector.tensor_scalar(sc[:], sc[:], 1.0, None, ALU.add)).done()
            own(nc.vector.reciprocal(sc[:], sc[:])).done()
            own(nc.vector.tensor_reduce(gm[:, :, 0:NG], sc[:].rearrange("p t (g e) -> p t g e", e=EPG), AX.X,
                                        ALU.max)).done()
            for t in range(NT):
                own(nc.vector.max(g8[:, t], gm[:, t]))
            own.done()
            own(nc.vector.memset(g8[:, :, TOPG:8], -5.0)).done()
            for t in range(NT):
                own(nc.vector.match_replace(out=gr[:, t], in_to_replace=g8[:, t], in_values=gm[:, t], imm_value=9.0))
            own.done()
            own(nc.vector.tensor_scalar(gk[:, :, 0], gr[:, :, 0:NG], 9.0, None, ALU.is_equal)).done()
            own(nc.vector.tensor_scalar(gk[:, :, 1], gk[:, :, 0], 1.0, None, ALU.subtract)).done()
            for e in range(NG):
                cols = slice(EPG * e, EPG * e + EPG)
                own(nc.vector.tensor_tensor(ms[:, :, cols], sc[:, :, cols],
                                            gk[:, :, 0, e:e + 1].to_broadcast([TT, NT, EPG]), ALU.mult))
            own.done()
            for e in range(NG):
                cols = slice(EPG * e, EPG * e + EPG)
                own(nc.vector.tensor_tensor(ms[:, :, cols], ms[:, :, cols],
                                            gk[:, :, 1, e:e + 1].to_broadcast([TT, NT, EPG]), ALU.add))
            own.done()
            for t in range(NT):
                own(nc.vector.max(g8[:, t], ms[:, t]))
            own.done()
            own(nc.vector.memset(g8[:, :, TOPK:8], -5.0)).done()
            for t in range(NT):
                own(nc.vector.match_replace(out=er[:, t], in_to_replace=g8[:, t], in_values=ms[:, t], imm_value=9.0))
            own.done()
            own(nc.vector.tensor_scalar(er[:, :, 0:NE], er[:, :, 0:NE], 9.0, None, ALU.is_equal)).done()
            own(nc.vector.tensor_tensor(er[:, :, 0:NE], er[:, :, 0:NE], sc[:], ALU.mult)).done()
            own(nc.vector.tensor_reduce(sm[:], er[:, :, 0:NE], AX.X, ALU.add)).done()
            own(nc.vector.tensor_scalar(sm[:], sm[:], WS, None, ALU.mult)).done()
            own(nc.vector.reciprocal(sm[:], sm[:])).done()
            own(nc.vector.tensor_tensor(g.comb[:, :, 0:NE], er[:, :, 0:NE],
                                        sm[:].unsqueeze(2).to_broadcast([TT, NT, NE]), ALU.mult))
            own(nc.vector.memset(g.comb[:, :, NE:NX], 1.0 / WS)).done()

        @block.tensor
        def _(pe):

            def turn_o(t, k, half):
                pe.wait_ge(o_in[k], 16 * half + 16)
                for j in range(4):
                    wait(pe, s["oT_lo"], 4 * t + j - 3)
                    for h in range(4):
                        last = nc.tensor.transpose(pT[j][:, h * TT:(h + 1) * TT],
                                                   ot[:, k, (4 * j + h) * HD:(4 * j + h + 1) * HD],
                                                   g.ident[0:TT, 0:TT])
                    last.then_inc(s["oT_done"], 1)

            def project(t, k, _):
                if isinstance(t, int) and t == 0:
                    pe.wait_ge(s["w_lo"], 4)
                    pe.wait_ge(s["dve"], 3)
                wait(pe, s["x_ready"], t)
                for j in range(4):
                    pe.wait_ge(s["oT_lo"], 4 * t + j + 1)
                    for h in range(4 * j, 4 * j + 4):
                        last = three_products(nc, pY[0:TT, 0:H], oTh[:, k, h], oTl[:, k, h], wo[:, 0, h],
                                              wo[:, 1, h], start=(h == 0), stop=(h == NH - 1))
                last.then_inc(s["y_done"], 1)

            def turn_x(t, k, _):
                pe.wait_ge(s["xn_ready"], t + 1)
                for c in range(KC):
                    last = nc.tensor.transpose(pX[:, c * TT:(c + 1) * TT], xn[:, c * 128:(c + 1) * 128],
                                               g.ident[0:TT, 0:TT])
                last.then_inc(s["xT_done"], 1)

            def route(t, k, _):
                pe.wait_ge(s["xT_lo"], t + 1)
                wait(pe, s["lg_taken"], t)
                for c in range(KC):
                    last = three_products(nc, pL[0:TT, 0:NE], cur[:, 0, c], cur[:, 1, c], gw[:, 0, c],
                                          gw[:, 1, c], start=(c == 0), stop=(c == KC - 1))
                last.then_inc(s["lg_done"], 1)

            pipeline(pe, NT, [(turn_o, 1), (route, -2), (project, 0), (turn_x, -1)])


def experts_phase(nc, g, io):
    NC4 = 4
    TC = TOK // NC4
    SUB = TC // TT
    with phase(nc) as (ctx, a):
        stg = a.sb("e_stg", [128, 2, KC, 2, M])
        std = a.sb("e_std", [128, 2, 2, H])
        wg = a.sb("e_wg", [128, 2, 2, KC, 384], F16)
        wd = a.sb("e_wd", [128, 2, 2, 2, H], F16)
        sg = a.sb("e_sg", [128, 2, 2, TC])
        hb = a.sb("e_h", [128, 2, 2, TC])
        hh = a.sb("e_hh", [128, 2, 2, TC], F16)
        hl = a.sb("e_hl", [128, 2, TC], F16)
        ps = [[a.ps(f"e_p{n}{i}", [128, 512]) for n in "abc"] for i in range(2)]
        pd = [a.ps(f"e_pd{i}", [128, 2, H]) for i in range(2)]
        w_in = [a.sem(f"e_w_in{i}") for i in range(2)]
        names = "std_cleared cleared w_hi w_lo up_done sg_ready h_ready h_hi h_lo down_done acc"
        s = {n: a.sem("e_" + n) for n in names.split()}
        block = ctx.enter_context(nc.Block())
        ND = 2 * NC4

        def steps(eng, step):
            step(0, 0, 0, 0)
            with eng.Fori(0, (NE - 2) // 2) as i:
                step(2 * i + 1, 1, i, i + 1)
                step(2 * i + 2, 0, i + 1, i + 1)
            for e in range(NE - 1, NX):
                step(e, e % 2, e // 2, (e + 1) // 2)

        @block.sync
        def _(sp):
            sp.wait_ge(s["std_cleared"], 1)

            def load(e, par, shared=None):
                if shared is None:
                    srcs = [t[ds(e, 1), :, :].rearrange("a p n -> (a p) n") for t in (io.w_gate, io.w_up, io.w_down)]
                else:
                    part = slice(shared * M, shared * M + M)
                    srcs = [io.sw_gate[:, part], io.sw_up[:, part], io.sw_down[part, :]]
                for n in range(2):
                    sp.dma_start(stg[:, par, :, n, :], srcs[n].rearrange("(c p) m -> p c m", p=128))\
                        .then_inc(w_in[par], 16)
                sp.dma_start(std[:, par, 0, :], srcs[2][0:128]).then_inc(w_in[par], 16)
                sp.dma_start(std[64:64 + MT, par, 1, :], srcs[2][128:M]).then_inc(w_in[par], 16)
                sp.dma_start(std[0:MT, par, 1, :], srcs[2][128:M]).then_inc(w_in[par], 16)

            load(0, 0)
            load(1, 1)
            with sp.Fori(0, (NE - 2) // 2) as i:
                for k in range(2):
                    sp.wait_ge(s["w_lo"], 5 * (2 * i + k) + 5)
                    load(2 * i + k + 2, k)
            for n in range(2):
                sp.wait_ge(s["w_lo"], 5 * (NE - 2 + n) + 5)
                load(0, n, shared=n)

        @block.gpsimd
        def _(pool):
            for t in (hb, sg):
                nc.gpsimd.memset(t[:], 0.0).then_inc(s["cleared"], 1)

            def step(e):
                for c in range(NC4):
                    n = NC4 * e + c
                    pool.wait_ge(s["h_hi"], n + 1)
                    wait(pool, s["h_lo"], 2 * n)
                    nc.gpsimd.tensor_tensor(hl[:, c % 2], hb[:, c % 2, 0], hh[:, c % 2, 0],
                                            ALU.subtract).then_inc(s["h_lo"], 1)
                    pool.wait_ge(s["h_lo"], 2 * n + 1)
                    nc.gpsimd.tensor_tensor(hh[0:MT, c % 2, 1], hb[64:64 + MT, c % 2, 1],
                                            hh[64:64 + MT, c % 2, 1], ALU.subtract).then_inc(s["h_lo"], 1)

            each(pool, NX, step)

        def main(t, par, c, n):
            return t[:, par, n, c, 0:256].rearrange("p (u m) -> p u m", m=128)

        def tail(t, par, c, n):
            return t[:, par, n, c, 256:384].rearrange("p (u m) -> p u m", m=64)[:, :, 0:MT]

        @block.scalar
        def _(act):
            act.wait_ge(s["cleared"], 3)

            def split(par, half, e):
                act.wait_ge(w_in[par], 80 * half + 80)
                for c in range(KC):
                    nc.scalar.activation(main(wg, par, c, 0), stg[:, par, c, :, 0:128], ACT.Copy,
                                         scale=WS).then_inc(s["w_hi"], 1)
                    nc.scalar.activation(tail(wg, par, c, 0), stg[:, par, c, :, 128:M], ACT.Copy,
                                         scale=WS).then_inc(s["w_hi"], 1)
                nc.scalar.activation(wd[:, par, 0], std[:, par], ACT.Copy, scale=WS).then_inc(s["w_hi"], 1)

            split(0, 0, 0)

            def step(e, par, half, nxt):
                for c in range(NC4):
                    n = NC4 * e + c
                    act.wait_ge(s["up_done"], n + 1)
                    nc.scalar.activation(sg[:, c % 2, 0], ps[c % 2][0][:, 0:TC], ACT.Silu,
                                         scale=1 / WS).then_inc(s["sg_ready"], 1)
                    nc.scalar.activation(sg[64:64 + MT, c % 2, 1], ps[c % 2][2][0:MT, 0:TC], ACT.Silu,
                                         scale=1 / WS).then_inc(s["sg_ready"], 1)
                    if c == 1 and not (isinstance(e, int) and e == NX - 1):
                        wait(act, s["down_done"], ND * e)
                        split(1 - par, nxt, e + 1)
                    act.wait_ge(s["h_ready"], 2 * n + 2)
                    nc.scalar.activation(hh[:, c % 2], hb[:, c % 2], ACT.Copy).then_inc(s["h_hi"], 1)

            steps(act, step)

        @block.vector
        def _(dve):
            def split(par, e):
                at = 0
                for c in range(KC):
                    for part, cols in ((main, slice(0, 128)), (tail, slice(128, M))):
                        at += 1
                        dve.wait_ge(s["w_hi"], 5 * e + at)
                        nc.vector.scalar_tensor_tensor(part(wg, par, c, 1), stg[:, par, c, :, cols], WS,
                                                       part(wg, par, c, 0), ALU.mult,
                                                       ALU.subtract).then_inc(s["w_lo"], 1)
                dve.wait_ge(s["w_hi"], 5 * e + 5)
                nc.vector.scalar_tensor_tensor(wd[:, par, 1], std[:, par], WS, wd[:, par, 0], ALU.mult,
                                               ALU.subtract).then_inc(s["w_lo"], 1)

            nc.vector.memset(std[:], 0.0).then_inc(s["std_cleared"], 1)
            nc.vector.memset(wg[:], 0.0).then_inc(s["cleared"], 1)
            dve.wait_ge(s["cleared"], 3)
            split(0, 0)

            def accumulate(e, c):
                for i in range(2):
                    dve.wait_ge(s["down_done"], ND * e + 2 * c + i + 1)
                    for j in range(2):
                        t = SUB * c + 2 * i + j
                        w = g.comb[:, t, ds(e, 1)]
                        last = nc.vector.scalar_tensor_tensor(g.xs[:, t], pd[i][0:TT, j], w, g.xs[:, t], ALU.mult,
                                                              ALU.add)
                    last.then_inc(s["acc"], 1)

            def step(e, par, half, nxt):
                for c in range(NC4):
                    n = NC4 * e + c
                    wait(dve, s["h_lo"], 2 * (n - 1))
                    dve.wait_ge(s["sg_ready"], 2 * n + 1)
                    nc.vector.scalar_tensor_tensor(hb[:, c % 2, 0], ps[c % 2][1][:, 0:TC], 1 / WS, sg[:, c % 2, 0],
                                                   ALU.mult, ALU.mult).then_inc(s["h_ready"], 1)
                    dve.wait_ge(s["sg_ready"], 2 * n + 2)
                    nc.vector.scalar_tensor_tensor(hb[64:64 + MT, c % 2, 1], ps[c % 2][2][64:64 + MT, 0:TC], 1 / WS,
                                                   sg[64:64 + MT, c % 2, 1], ALU.mult,
                                                   ALU.mult).then_inc(s["h_ready"], 1)
                    if c:
                        accumulate(e, c - 1)
                    elif not (isinstance(e, int) and e == 0):
                        accumulate(e - 1, NC4 - 1)
                    if c == 1 and not (isinstance(e, int) and e == NX - 1):
                        split(1 - par, e + 1)

            steps(dve, step)
            accumulate(NX - 1, NC4 - 1)

        @block.tensor
        def _(pe):
            def down(e, par, c):
                n = NC4 * e + c
                pe.wait_ge(s["h_lo"], 2 * n + 2)
                for i in range(2):
                    wait(pe, s["acc"], ND * e + 2 * c + i - 1)
                    for j in range(2):
                        cols = slice((2 * i + j) * TT, (2 * i + j + 1) * TT)
                        out = pd[i][0:TT, j]
                        three_products(nc, out, hh[:, c % 2, 0, cols], hl[:, c % 2, cols], wd[:, par, 0, 0],
                                       wd[:, par, 1, 0], start=True, stop=False)
                        for k in range(2):
                            last = nc.tensor.matmul(out, hh[:, c % 2, 1, cols], wd[:, par, k, 1], start=False,
                                                    stop=(k == 1))
                    last.then_inc(s["down_done"], 1)

            def step(e, par, half, nxt):
                for c in range(NC4):
                    n = NC4 * e + c
                    if c == 0:
                        pe.wait_ge(s["w_lo"], 5 * e + 5)
                    wait(pe, s["h_ready"], 2 * (n - 1))
                    cols = slice(c * TC, (c + 1) * TC)
                    for b in range(3):
                        for k in range(KC):
                            m = slice(128 * b, 128 * b + 128)
                            last = three_products(nc, ps[c % 2][b][:, 0:TC], wg[:, par, 0, k, m], wg[:, par, 1, k, m],
                                                  g.xT[:, 0, k, cols], g.xT[:, 1, k, cols],
                                                  start=(k == 0), stop=(k == KC - 1))
                    last.then_inc(s["up_done"], 1)
                    if c:
                        down(e, par, c - 1)
                    elif not (isinstance(e, int) and e == 0):
                        down(e - 1, 1 - par, NC4 - 1)

            steps(pe, step)
            down(NX - 1, (NX - 1) % 2, NC4 - 1)


def q1_phase(nc, g, io):
    with phase(nc) as (ctx, a):
        wst = a.sb("r_wst", [128, KC, H])
        bq = a.sb("r_bq", [TT, H])
        wT = a.sb("r_wT", [128, 2, KC, H], F16)
        wn = a.sb("r_wn", [128, KC, H])
        wa = a.sb("r_wa", [128, 2, KC])
        pm = a.sb("r_pm", [128, 2])
        st6 = a.sb("r_st6", [TT, 6])
        mv = a.sb("r_mv", [TT, 2, 2])
        ve = a.sb("r_ve", [TT, 2])
        rs = a.sb("r_rs", [TT, 2])
        xn = a.sb("r_xn", [TT, H])
        am = a.sb("r_am", [TT, 2, 2])
        xq = a.sb("r_xq", [TT, 2, H], F16)
        xT = a.sb("r_xT", [128, KC, TT], F16)
        qb = a.sb("r_qb", [TT, 2, H])
        bd = a.sb("r_bd", [128, 2, 2, 2, KC, 2, S], F16)
        pW = [a.ps(f"r_pW{i}", [128, 512]) for i in range(2)]
        pX = a.ps("r_pX", [128, KC, TT], F16)
        pQ = a.ps("r_pQ", [128, 512])
        pT = [a.ps(f"r_pT{i}", [128, KC, TT]) for i in range(2)]
        w_in, b_in, gate = a.sem("r_w_in"), a.sem("r_b_in"), a.sem("r_gate")
        out_done = [a.sem(f"r_out{i}") for i in range(2)]
        at = {}
        names = "dve wT_done wT_hi pads var rstd xq_ready xT_done xT_taken q_done q_ready qT_done qT_hi qT_lo quant"
        s = {n: a.sem("r_" + n) for n in names.split()}
        block = ctx.enter_context(nc.Block())

        @block.sync
        def _(sp):
            sp.dma_start(wst[:], io.wq.rearrange("(c p) n -> p c n", p=128)).then_inc(w_in, 16)
            sp.dma_start(bq[:], io.bq1.rearrange("(a n) -> a n", a=1).to_broadcast([TT, H])).then_inc(b_in, 16)

            def store(t, k, _):
                sp.wait_ge(s["qT_lo"], 4 * t + 4)
                for b in range(2):
                    sp.dma_start(io.q1[ds(2 * t + b, 1)].rearrange("a h p k c -> p (a h) (k c)"),
                                 bd[:, k, b].rearrange("p h k e q -> p h (k e q)")).then_inc(out_done[k], 16)

            pipeline(sp, NT, [(store, 0)])
            for k in range(2):
                sp.wait_ge(out_done[k], 32 * (NT // 2))

        @block.gpsimd
        def _(pool):
            nc.gpsimd.memset(bd[:], 0.0).then_inc(s["pads"], 1)

            def rstd(t, k, _):
                pool.wait_ge(s["var"], t + 1)
                nc.gpsimd.tensor_tensor(rs[:, k:k + 1], ve[:, k:k + 1], g.mhalf[0:TT, 0:1],
                                        ALU.pow).then_inc(s["rstd"], 1)

            pipeline(pool, NT, [(rstd, 0)])

        @block.scalar
        def _(act):
            for c in range(KC):
                act.wait_ge(s["wT_done"], c + 1)
                nc.scalar.activation(wT[:, 0, c], pW[c][:, 0:H], ACT.Copy).then_inc(s["wT_hi"], 1)
            act.wait_ge(s["pads"], 1)

            def take_x(t, k, _):
                act.wait_ge(s["xT_done"], t + 1)
                nc.scalar.activation(xT[:], pX[:], ACT.Copy).then_inc(s["xT_taken"], 1)

            def split_q(t, k, half):
                act.wait_ge(s["qT_done"], t + 1)
                wait(act, out_done[k], 32 * half)
                for e in range(2):
                    nc.scalar.activation(bd[:, k, :, 0, :, e, 0:S].rearrange("p b k q -> p k b q"),
                                         pT[k][:].rearrange("p k (b q) -> p k b q", b=2), ACT.Copy,
                                         scale=pm[:, e:e + 1]).then_inc(s["qT_hi"], 1)

            pipeline(act, NT, [(take_x, 0), (split_q, -1)])

        @block.vector
        def _(dve):
            own = Counted(dve, s["dve"])
            own(nc.vector.tensor_scalar(pm[:], g.evenodd[:], HD1 ** -0.5 / WS, None, ALU.mult))
            dve.wait_ge(w_in, 16)
            quantise_rows(nc, own, wst[:], wn[:], wa[:, 0], wa[:, 1], dequantise=True)
            at["wn"] = own.n
            for c in range(KC):
                dve.wait_ge(s["wT_hi"], c + 1)
                own(nc.vector.tensor_tensor(wT[:, 1, c], pW[c][:, 0:H], wT[:, 0, c], ALU.subtract))
            dve.wait_ge(b_in, 16)
            vector, quant = own.n, 0

            def variance(t, k, _):
                own.n = vector + 2 * t
                xrow = g.xs[:, ds(t, 1), :].rearrange("p a n -> p (a n)")
                own(nc.vector.bn_stats(st6[:], xrow)).done()
                passed(dve, gate)
                own(nc.vector.bn_aggr(mv[:, k], st6[:])).done()
                nc.vector.tensor_scalar(ve[:, k:k + 1], mv[:, k, 1:2], LN_EPS, None, ALU.add).then_inc(s["var"], 1)

            def quantise(t, k, _):
                q = Counted(dve, s["quant"])
                q.n = quant + 6 * t
                xrow = g.xs[:, ds(t, 1), :].rearrange("p a n -> p (a n)")
                scale, recip = am[:, k, 0:1], am[:, k, 1:2]
                dve.wait_ge(s["rstd"], t + 1)
                wait(dve, s["xq_ready"], t)
                q(nc.vector.tensor_scalar(xn[:], xrow, mv[:, k, 0:1], rs[:, k:k + 1], ALU.subtract, ALU.mult)).done()
                q(nc.vector.tensor_reduce(scale, xn[:], AX.X, ALU.max, apply_absolute_value=True)).done()
                q(nc.vector.tensor_scalar(scale, scale, 1 / 127.0, 1e-8, ALU.mult, ALU.max)).done()
                q(nc.vector.reciprocal(recip, scale)).done()
                q(nc.vector.tensor_scalar(xn[:], xn[:], recip, MAGIC, ALU.mult, ALU.add)).done()
                q(nc.vector.tensor_scalar(xn[:], xn[:], MAGIC, 127.0, ALU.subtract, ALU.min)).done()
                nc.vector.tensor_scalar(xq[:, k], xn[:], -127.0, None, ALU.max).then_inc(s["xq_ready"], 1)

            def bias(t, k, _):
                dve.wait_ge(s["q_done"], t + 1)
                nc.vector.scalar_tensor_tensor(qb[:, k], pQ[0:TT, 0:H], am[:, k, 0:1], bq[:], ALU.mult,
                                               ALU.add).then_inc(s["q_ready"], 1)

            def split_q(t, k, _):
                dve.wait_ge(s["qT_hi"], 2 * t + 2)
                for e in range(2):
                    for b in range(2):
                        nc.vector.scalar_tensor_tensor(
                            bd[:, k, b, 1, :, e, 0:S], pT[k][:].rearrange("p k (b q) -> p b k q", b=2)[:, b],
                            pm[:, e:e + 1], bd[:, k, b, 0, :, e, 0:S], ALU.mult,
                            ALU.subtract).then_inc(s["qT_lo"], 1)

            pipeline(dve, NT, [(variance, 2), (quantise, 1), (bias, 0), (split_q, -1)])

        @block.tensor
        def _(pe):
            pe.wait_ge(s["dve"], at["wn"])
            for c in range(KC):
                for o in range(KC):
                    last = nc.tensor.transpose(pW[c][:, o * 128:(o + 1) * 128], wn[:, o, c * 128:(c + 1) * 128],
                                               g.ident[:])
                last.then_inc(s["wT_done"], 1)

            def turn_x(t, k, _):
                pe.wait_ge(s["xq_ready"], t + 1)
                for c in range(KC):
                    last = nc.tensor.transpose(pX[:, c], xq[:, k, c * 128:(c + 1) * 128], g.ident16[0:TT, 0:TT])
                last.then_inc(s["xT_done"], 1)

            def project(t, k, _):
                pe.wait_ge(s["xT_taken"], t + 1)
                wait(pe, s["q_ready"], t)
                for c in range(KC):
                    for n in range(2):
                        last = nc.tensor.matmul(pQ[0:TT, 0:H], xT[:, c], wT[:, n, c], start=(c == 0 and n == 0),
                                                stop=(c == KC - 1 and n == 1))
                last.then_inc(s["q_done"], 1)

            def turn_q(t, k, _):
                pe.wait_ge(s["q_ready"], t + 1)
                wait(pe, s["qT_lo"], 4 * t - 4)
                for c in range(KC):
                    last = nc.tensor.transpose(pT[k][:, c], qb[:, k, c * 128:(c + 1) * 128], g.ident[0:TT, 0:TT])
                last.then_inc(s["qT_done"], 1)

            pipeline(pe, NT, [(turn_x, 0), (project, 0), (turn_q, -1)])


def quantise_rows(nc, own, w, out, scale, recip, dequantise):
    own(nc.vector.tensor_reduce(scale, w, AX.X, ALU.max, apply_absolute_value=True)).done()
    own(nc.vector.tensor_scalar(scale, scale, 1 / 127.0, 1e-8, ALU.mult, ALU.max)).done()
    own(nc.vector.reciprocal(recip, scale)).done()
    for c in range(w.shape[1]):
        own(nc.vector.tensor_scalar(out[:, c], w[:, c], recip[:, c:c + 1], MAGIC, ALU.mult, ALU.add))
    own.done()
    own(nc.vector.tensor_scalar(out, out, MAGIC, 127.0, ALU.subtract, ALU.min)).done()
    own(nc.vector.tensor_scalar(out, out, -127.0, None, ALU.max)).done()
    if dequantise:
        for c in range(w.shape[1]):
            own(nc.vector.tensor_scalar(out[:, c], out[:, c], scale[:, c:c + 1], None, ALU.mult))
        own.done()


def round_any(nc, own, x, tmp):
    big = 2.0 ** 23
    mag, low, sgn = (tmp[:, n] for n in range(3))
    own(nc.vector.tensor_scalar(sgn, x, 0.0, 2.0, ALU.is_ge, ALU.mult)).done()
    own(nc.vector.tensor_scalar(sgn, sgn, 1.0, None, ALU.subtract)).done()
    own(nc.vector.tensor_tensor(mag, x, sgn, ALU.mult)).done()
    own(nc.vector.tensor_scalar(low, mag, big, None, ALU.min)).done()
    own(nc.vector.tensor_tensor(mag, mag, low, ALU.subtract))
    own.done()
    own(nc.vector.tensor_scalar(low, low, big, big, ALU.add, ALU.subtract)).done()
    own(nc.vector.tensor_tensor(mag, mag, low, ALU.add)).done()
    own(nc.vector.tensor_tensor(x, mag, sgn, ALU.mult)).done()


def attn1_phase(nc, g, io):
    order = {eng: listing(text) for eng, text in ORDER1.items()}
    WORK = work_of(order["tensor"])
    AT = {w: n for n, w in enumerate(WORK)}
    NW = len(WORK)
    GK = 4 * KP
    with phase(nc) as (ctx, a):
        wst = a.sb("b_wst", [128, 4, H])
        wT = a.sb("b_wT", [128, 2, KC, 2 * H], F16)
        bk = a.sb("b_bk", [128, 2, KC])
        cx = a.sb("b_ctx", [KP, 2, KT, H])
        cT = a.sb("b_cT", [128, 2, 2, KC, GK], F16)
        kn = a.sb("b_kn", [128, 2, 2, 2, SE], F16)
        ks = a.sb("b_ks", [96, 2, 2, 4, SE], F16)
        vv = a.sb("b_vv", [KP, 2, KT, 8, 2, 32], F16)
        qs = a.sb("b_qs", [96, 2, 2, 4, RP], F16)
        pr = a.sb("b_pr", [RP, 2, SE])
        pTh = a.sb("b_pTh", [KP, 2, KT, RP], F16)
        pTl = a.sb("b_pTl", [KP, 2, KT, RP], F16)
        nmax = a.sb("b_nmax", [RP, 2, NR])
        rsum = a.sb("b_rsum", [RP, 2, NR])
        inv = a.sb("b_inv", [RP, 2, NR])
        os_ = a.sb("b_os", [RP, NR, 32])
        ot = a.sb("b_ot", [RP, 2, NR, 2, HD1])
        ps_s = a.ps("b_ps", [128, 3, 512])
        ps_t = [a.ps(f"b_pt{i}", [128, 512]) for i in range(2)]
        ps_w = [a.ps(f"b_pw{i}", [128, 512]) for i in range(2)]
        ps_o = a.ps("b_po", [128, NR, 2, 32])
        w_in, b_in = a.sem("b_w_in"), a.sem("b_b_in")
        ctx_in = [a.sem(f"b_ctx_in{i}") for i in range(2)]
        q_in = [a.sem(f"b_q_in{i}") for i in range(2)]
        k_in = [a.sem(f"b_k_in{i}") for i in range(2)]
        stored = [a.sem(f"b_stored{i}") for i in range(2)]
        names = ("w_turned w_hi w_lo scores_done nmax_ready exp_done turn_done turn_hi turn_lo values_done "
                 "ot_free o_half inv_ready o_taken work_done work_hi work_taken own")
        s = {n: a.sem("b_" + n) for n in names.split()}
        block = ctx.enter_context(nc.Block())

        @block.sync
        def _(sp):
            sp.sem_inc(s["ot_free"], 2)
            sp.dma_start(wst[:], io.wkv.rearrange("(c p) n -> p c n", p=128)).then_inc(w_in, 16)
            with nc.allow_non_contiguous_dma(reason="256 values"):
                sp.dma_start(bk[:, 0], io.bkv[0:H].rearrange("(c p) -> p c", p=128)).then_inc(b_in, 16)

            def load_ctx(G, par):
                src = io.ctx[ds(G, 1), :, :].rearrange("a (p k) d -> (a p) k d", k=KT)
                sp.dma_start(cx[0:120, par], src[0:120]).then_inc(ctx_in[par], 16)
                sp.dma_start(cx[120:KP, par], src[120:KP]).then_inc(ctx_in[par], 16)

            def load_q(G, par):
                for n, part in enumerate((0, 1, 0)):
                    src = io.q1[ds(G, 1), part].rearrange("a (j r) k c -> (a r) k j c", j=4)
                    for k in range(2):
                        sp.dma_start(qs[32 * n:32 * n + 32, par, k], src[:, k]).then_inc(q_in[par], 16)

            def stack_keys(G, par):
                sp.wait_ge(s["work_taken"], NW * G + AT["K", 5] + 1)
                for n, part in enumerate((0, 0, 1)):
                    for j in range(4):
                        sp.dma_start(ks[32 * n:32 * n + 32, par, :, j], kn[32 * j:32 * j + 32, par, part])\
                            .then_inc(k_in[par], 16)

            load_ctx(0, 0)
            load_ctx(1, 1)
            load_q(0, 0)
            stack_keys(0, 0)

            def step(g_, par, half, load, produce):
                if load:
                    sp.wait_ge(s["work_done"], NW * g_ + AT["C", 5] + 1)
                    load_ctx(g_ + 2, par)
                if produce:
                    wait(sp, s["scores_done"], NR * g_)
                    load_q(g_ + 1, 1 - par)
                    stack_keys(g_ + 1, 1 - par)
                sp.wait_ge(s["o_taken"], g_ + 1)
                with nc.allow_non_contiguous_dma(reason="16 columns of a head"):
                    for e in range(2):
                        sp.dma_start(io.o1[ds(g_ * S, S), :].rearrange("q (r e d) -> q r e d", e=2, d=HD1)[:, :, e, :],
                                     ot[S * e:S * e + S, par, :, e]).then_inc(stored[par], 16)
                sp.wait_ge(stored[par], 32 * half + 32)
                sp.sem_inc(s["ot_free"], 1)

            step(0, 0, 0, True, True)
            with sp.Fori(0, (B - 4) // 2) as i:
                step(2 * i + 1, 1, i, True, True)
                step(2 * i + 2, 0, i + 1, True, True)
            step(B - 3, 1, (B - 3) // 2, True, True)
            step(B - 2, 0, (B - 2) // 2, False, True)
            step(B - 1, 1, (B - 1) // 2, False, False)
            for k in range(2):
                sp.wait_ge(stored[k], 32 * (B // 2))

        @block.scalar
        def _(act):
            for c in range(KC):
                act.wait_ge(s["w_turned"], c + 1)
                nc.scalar.activation(wT[:, 0, c], ps_w[c][:], ACT.Copy, scale=WS).then_inc(s["w_hi"], 1)

            def work(kind, u, batch):
                G, par, half = batch
                j, i = u // 2, u % 2
                n = AT[kind, u]
                act.wait_ge(s["work_done"], NW * G + n + 1)
                bank = ps_w[n % 2]
                if kind == "C":
                    for c in range(KC):
                        ins = nc.scalar.activation(
                            cT[:, (j + par) % 2, 0, c, 2 * KP * i:2 * KP * (i + 1)]
                            .rearrange("p (k q) -> p k q", q=KP),
                            bank[:, 0:4 * KP].rearrange("p (k c q) -> p k c q", k=2, c=KC)[:, :, c], ACT.Copy)
                elif kind == "K":
                    if u == 0:
                        wait(act, k_in[par], 192 * half)
                    ins = nc.scalar.activation(kn[:, par, 0, i, GK * j:GK * (j + 1)], bank[:, 0:GK],
                                               ACT.Identity, bias=bk[:, 1, i:i + 1])
                else:
                    kt = 4 * j + 2 * i
                    ins = nc.scalar.activation(vv[:, par, kt:kt + 2, :, 0].rearrange("p k h d -> p (k h) d"),
                                               bank[0:KP, :].rearrange("p (k d) -> p k d", d=32), ACT.Copy)
                ins.then_inc(s["work_hi"], 1)

            act.wait_ge(s["own"], 1)

            def attend(kind, n, batch):
                b, par, _ = batch
                if kind == "S":
                    act.wait_ge(s["nmax_ready"], NR * b + n + 1)
                    nc.scalar.activation(pr[:, n % 2], pr[:, n % 2], ACT.Exp, scale=-1.0,
                                         bias=nmax[:, par, n:n + 1],
                                         accum_out=rsum[:, par, n:n + 1]).then_inc(s["exp_done"], 1)
                elif kind == "T":
                    r, third = n // 3, n % 3
                    act.wait_ge(s["turn_done"], NQ * b + n + 1)
                    nc.scalar.activation(pTh[:, r % 2, 4 * third:4 * third + 4].rearrange("p k c -> p (k c)"),
                                         ps_t[n % 2][0:KP, 0:4 * RP], ACT.Copy).then_inc(s["turn_hi"], 1)
                else:
                    act.wait_ge(s["values_done"], b + 1)
                    nc.scalar.activation(os_[:], ps_o[0:RP, :, 1], ACT.Copy).then_inc(s["o_half"], 1)

            batches(act, order["scalar"], attend, work)

        @block.vector
        def _(dve):
            dve.wait_ge(b_in, 16)
            nc.vector.tensor_scalar(bk[:, 1], bk[:, 0], WS, None, ALU.mult).then_inc(s["own"], 1)
            for c in range(KC):
                dve.wait_ge(s["w_hi"], c + 1)
                nc.vector.scalar_tensor_tensor(wT[:, 1, c], ps_w[c][:], WS, wT[:, 0, c], ALU.mult,
                                               ALU.subtract).then_inc(s["w_lo"], 1)
            dve.wait_ge(s["own"], 1)

            def work(kind, u, batch):
                G, par, _ = batch
                j, i = u // 2, u % 2
                n = AT[kind, u]
                dve.wait_ge(s["work_hi"], NW * G + n + 1)
                bank = ps_w[n % 2]
                if kind == "C":
                    for c in range(KC):
                        cols = slice(2 * KP * i, 2 * KP * (i + 1))
                        ins = nc.vector.tensor_tensor(
                            cT[:, (j + par) % 2, 1, c, cols].rearrange("p (k q) -> p k q", q=KP),
                            bank[:, 0:4 * KP].rearrange("p (k c q) -> p k c q", k=2, c=KC)[:, :, c],
                            cT[:, (j + par) % 2, 0, c, cols].rearrange("p (k q) -> p k q", q=KP), ALU.subtract)
                elif kind == "K":
                    cols = slice(GK * j, GK * (j + 1))
                    ins = nc.vector.scalar_tensor_tensor(kn[:, par, 1, i, cols], bank[:, 0:GK], bk[:, 1, i:i + 1],
                                                         kn[:, par, 0, i, cols], ALU.add, ALU.subtract)
                else:
                    kt = 4 * j + 2 * i
                    ins = nc.vector.tensor_tensor(vv[:, par, kt:kt + 2, :, 1].rearrange("p k h d -> p (k h) d"),
                                                  bank[0:KP, :].rearrange("p (k d) -> p k d", d=32),
                                                  vv[:, par, kt:kt + 2, :, 0].rearrange("p k h d -> p (k h) d"),
                                                  ALU.subtract)
                ins.then_inc(s["work_taken"], 1)

            def attend(kind, n, batch):
                b, par, _ = batch
                if kind == "S":
                    dve.wait_ge(s["scores_done"], NR * b + n + 1)
                    nc.vector.tensor_scalar(pr[:, n % 2].rearrange("p (a k) -> p a k", k=500), ps_s[0:RP, :, 0:500],
                                            -1.0, None, ALU.mult, ALU.min,
                                            accum_out=nmax[:, par, n:n + 1]).then_inc(s["nmax_ready"], 1)
                elif kind == "T":
                    r, third = n // 3, n % 3
                    dve.wait_ge(s["turn_hi"], NQ * b + n + 1)
                    part = (slice(None), r % 2, slice(4 * third, 4 * third + 4))
                    nc.vector.tensor_tensor(pTl[part].rearrange("p k c -> p (k c)"), ps_t[n % 2][0:KP, 0:4 * RP],
                                            pTh[part].rearrange("p k c -> p (k c)"),
                                            ALU.subtract).then_inc(s["turn_lo"], 1)
                else:
                    dve.wait_ge(s["exp_done"], NR * b + NR)
                    nc.vector.tensor_scalar(inv[:, par], rsum[:, par], WS, None,
                                            ALU.mult).then_inc(s["inv_ready"], 1)
                    dve.wait_ge(s["inv_ready"], 3 * b + 1)
                    nc.vector.reciprocal(inv[:, par], inv[:, par]).then_inc(s["inv_ready"], 1)
                    dve.wait_ge(s["ot_free"], b + 1)
                    dve.wait_ge(s["o_half"], b + 1)
                    both = ot[:, par].rearrange("p r e d -> p r (e d)")
                    nc.vector.tensor_tensor(both, ps_o[0:RP, :, 0], os_[:], ALU.add).then_inc(s["inv_ready"], 1)
                    dve.wait_ge(s["inv_ready"], 3 * b + 3)
                    nc.vector.tensor_tensor(both, both, inv[:, par].unsqueeze(2).to_broadcast([RP, NR, 32]),
                                            ALU.mult).then_inc(s["o_taken"], 1)

            batches(dve, order["vector"], attend, work)

        @block.tensor
        def _(pe):
            pe.wait_ge(w_in, 16)
            for c in range(KC):
                for o in range(4):
                    last = nc.tensor.transpose(ps_w[c][:, o * 128:(o + 1) * 128], wst[:, o, c * 128:(c + 1) * 128],
                                               g.ident[:])
                last.then_inc(s["w_turned"], 1)
            pe.wait_ge(s["w_lo"], KC)

            def work(kind, u, batch):
                G, par, half = batch
                j, i = u // 2, u % 2
                n = AT[kind, u]
                bank = ps_w[n % 2]
                wait(pe, s["work_taken"], NW * G + n - 1)
                if kind == "C":
                    if u == 0:
                        pe.wait_ge(ctx_in[par], 32 * half + 32)
                    for k in range(2):
                        for c in range(KC):
                            last = nc.tensor.transpose(bank[:, (2 * k + c) * KP:(2 * k + c + 1) * KP],
                                                       cx[:, par, 4 * j + 2 * i + k, c * 128:(c + 1) * 128],
                                                       g.ident[0:KP, 0:KP])
                    last.then_inc(s["work_done"], 1)
                    return
                pe.wait_ge(s["work_taken"], NW * G + AT["C", 2 * j + 1] + 1)
                if kind == "K":
                    for c in range(KC):
                        m = slice(128 * i, 128 * i + 128)
                        last = three_products(nc, bank[:, 0:GK], wT[:, 0, c, m], wT[:, 1, c, m],
                                              cT[:, (j + par) % 2, 0, c], cT[:, (j + par) % 2, 1, c],
                                              start=(c == 0), stop=(c == KC - 1))
                else:
                    for k in range(2):
                        keys = slice((2 * i + k) * KP, (2 * i + k + 1) * KP)
                        for c in range(KC):
                            last = three_products(nc, bank[0:KP, k * H:(k + 1) * H],
                                                  cT[:, (j + par) % 2, 0, c, keys],
                                                  cT[:, (j + par) % 2, 1, c, keys], wT[:, 0, c, H:2 * H],
                                                  wT[:, 1, c, H:2 * H], start=(c == 0), stop=(c == KC - 1))
                last.then_inc(s["work_done"], 1)

            def attend(kind, n, batch):
                b, par, half = batch
                if kind == "S":
                    if n == 0:
                        pe.wait_ge(q_in[par], 96 * half + 96)
                        pe.wait_ge(k_in[par], 192 * half + 192)
                        pe.wait_ge(s["work_taken"], NW * b + NW)
                    wait(pe, s["nmax_ready"], NR * b + n)
                    for j in range(3):
                        last = nc.tensor.matmul(ps_s[0:RP, j, 0:500], qs[:, par, n // 4, n % 4],
                                                ks[:, par, n // 4, n % 4, 500 * j:500 * j + 500],
                                                start=True, stop=True)
                    last.then_inc(s["scores_done"], 1)
                    return
                r, third = n // 3, n % 3
                if kind == "T":
                    if third == 0:
                        pe.wait_ge(s["exp_done"], NR * b + r + 1)
                    wait(pe, s["turn_lo"], NQ * b + n - 1)
                    for j in range(4):
                        kt = 4 * third + j
                        last = nc.tensor.transpose(ps_t[n % 2][0:KP, RP * j:RP * j + RP],
                                                   pr[:, r % 2, kt * KP:(kt + 1) * KP],
                                                   g.ident[0:RP, 0:RP])
                    last.then_inc(s["turn_done"], 1)
                else:
                    if n == 0:
                        wait(pe, s["o_taken"], b)
                    pe.wait_ge(s["turn_lo"], NQ * b + n + 1)
                    for kt in range(4 * third, 4 * third + 4):
                        nc.tensor.matmul(ps_o[0:RP, r], pTh[:, r % 2, kt], vv[:, par, kt, r], start=(kt == 0),
                                         stop=False)
                        last = nc.tensor.matmul(ps_o[0:RP, r, 0], pTl[:, r % 2, kt], vv[:, par, kt, r, 0],
                                                start=False, stop=(kt == KT - 1))
                    if n == NQ - 1:
                        last.then_inc(s["values_done"], 1)

            batches(pe, order["tensor"], attend, work)


def final_phase(nc, g, io):
    with phase(nc) as (ctx, a):
        yt = a.sb("f_yt", [TT, 2, H])
        wp = a.sb("f_wp", [128, KC, H])
        wpn = a.sb("f_wpn", [128, KC, H])
        wpT = a.sb("f_wpT", [128, 2, KC, H], F16)
        wa = a.sb("f_wa", [128, 2, KC])
        w1 = a.sb("f_w1", [128, FB, H])
        w2 = a.sb("f_w2", [128, KC, F])
        w1n = a.sb("f_w1n", [128, FB, H], F16)
        w2n = a.sb("f_w2n", [128, KC, F], F16)
        w1T = a.sb("f_w1T", [128, KC, F], F16)
        w2T = a.sb("f_w2T", [128, FB, H], F16)
        b1 = a.sb("f_b1", [128, FB])
        rows = a.sb("f_rows", [TT, 3, H])
        sc = a.sb("f_sc", [128, 16])
        mx = a.sb("f_mx", [128, 2])
        ma = a.sb("f_ma", [128, 2])
        ot = a.sb("f_ot", [TT, 2, H])
        ob = a.sb("f_ob", [TT, H])
        am = a.sb("f_am", [TT, 2, 2])
        oq = a.sb("f_oq", [TT, 2, H], F16)
        oT = a.sb("f_oT", [128, KC, TT], F16)
        st6 = a.sb("f_st6", [TT, 6])
        mv = a.sb("f_mv", [TT, 2, 2])
        ve = a.sb("f_ve", [TT, 1])
        rs = a.sb("f_rs", [TT, 1])
        xn = a.sb("f_xn", [TT, H])
        xr = a.sb("f_xr", [TT, 2, H])
        xq = a.sb("f_xq", [TT, H], F16)
        xT = a.sb("f_xT", [128, KC, TT], F16)
        hb = a.sb("f_hb", [128, FB, TT])
        hq = a.sb("f_hq", [128, FB, TT], F16)
        tmp = a.sb("f_tmp", [128, 3, H])
        p0 = [a.ps(f"f_p0{i}", [128, 512]) for i in range(2)]
        p16 = a.ps("f_p16", [128, 1024], F16)
        pO = p16[:, 0:KC * TT].rearrange("p (c q) -> p c q", q=TT)
        pX = a.ps("f_pX", [128, KC, TT], F16)
        pY = a.ps("f_pY", [128, H])
        pZ = a.ps("f_pZ", [128, H])
        pH = [a.ps(f"f_pH{i}", [128, 4, TT]) for i in range(2)]
        w_in, gate = a.sem("f_w_in"), a.sem("f_gate")
        o_in = [a.sem(f"f_o_in{i}") for i in range(2)]
        out_done = [a.sem(f"f_out{i}") for i in range(2)]
        at = {}
        names = ("dve max_ready max_all wT_done wT_hi w16_done w16_taken oq_ready oT_done oT_taken y_done "
                 "var rstd xq_ready xT_done xT_taken h_done hq_ready z_done out_ready "
                 "prep ob_ready xr_ready xb_ready relu_done quant_o resid quant_x quant_h")
        s = {n: a.sem("f_" + n) for n in names.split()}
        block = ctx.enter_context(nc.Block())
        S1, S2, SW1, SW2, RS1, RW1, RW2, P1, P2, R1, R2, KAP, RS2 = range(13)

        def col(n, rows=128):
            return sc[0:rows, n:n + 1]

        @block.sync
        def _(sp):
            sp.dma_start(wp[:], io.wp.rearrange("(c p) n -> p c n", p=128)).then_inc(w_in, 16)
            sp.dma_start(w1[:], io.W1.rearrange("(c p) n -> p c n", p=128)).then_inc(w_in, 16)
            sp.dma_start(w2[:], io.W2.rearrange("(c p) n -> p c n", p=128)).then_inc(w_in, 16)
            with nc.allow_non_contiguous_dma(reason="1024 values"):
                sp.dma_start(b1[:], io.b1.rearrange("(c p) -> p c", p=128)).then_inc(w_in, 16)
            for n, v in enumerate((io.bkv[H:2 * H], io.bp, io.b2)):
                sp.dma_start(rows[:, n], v.rearrange("(a n) -> a n", a=1).to_broadcast([TT, H])).then_inc(w_in, 16)
            for n, v in enumerate((io.s1, io.s2)):
                sp.dma_start(col(n), v.rearrange("(a n) -> a n", a=1).to_broadcast([128, 1])).then_inc(w_in, 16)

            def load(t, k, _):
                wait(sp, s["oq_ready"], t - 1)
                sp.dma_start(ot[:, k], io.o1[ds(t * TT, TT), :]).then_inc(o_in[k], 16)

            def store(t, k, _):
                sp.wait_ge(s["out_ready"], t + 1)
                sp.dma_start(io.out[ds(t * TT, TT), :], yt[:, k]).then_inc(out_done[k], 16)

            pipeline(sp, NT, [(load, 3), (store, -1)])
            for k in range(2):
                sp.wait_ge(out_done[k], 16 * (NT // 2))

        @block.gpsimd
        def _(pool):
            pool.wait_ge(s["max_ready"], 2)
            nc.gpsimd.partition_all_reduce(ma[:], mx[:], 128, bass.bass_isa.ReduceOp.max).then_inc(s["max_all"], 1)
            pool.wait_ge(s["prep"], 1)

            def bias_o(t, k, half):
                pool.wait_ge(o_in[k], 16 * half + 16)
                nc.gpsimd.tensor_tensor(ot[:, k], ot[:, k], rows[:, 0], ALU.add).then_inc(s["ob_ready"], 1)
                xrow = g.xs[:, ds(t, 1), :].rearrange("p a n -> p (a n)")
                nc.gpsimd.tensor_tensor(xrow, xrow, rows[:, 1], ALU.add).then_inc(s["xr_ready"], 1)

            def rstd(t, k, _):
                pool.wait_ge(s["var"], t + 1)
                nc.gpsimd.tensor_tensor(rs[:], ve[:], g.mhalf[0:TT, 0:1], ALU.pow).then_inc(s["rstd"], 1)
                wait(pool, s["out_ready"], t - 1)
                xrow = g.xs[:, ds(t, 1), :].rearrange("p a n -> p (a n)")
                nc.gpsimd.tensor_tensor(xr[:, k], xrow, rows[:, 2], ALU.add).then_inc(s["xb_ready"], 1)

            pipeline(pool, NT, [(rstd, 1), (bias_o, 3)])

        @block.scalar
        def _(act):
            for c in range(KC):
                act.wait_ge(s["wT_done"], c + 1)
                nc.scalar.activation(wpT[:, 0, c], p0[c][:, 0:H], ACT.Copy, scale=WS).then_inc(s["wT_hi"], 1)
            for n in range(4):
                act.wait_ge(s["w16_done"], n + 1)
                if n < 2:
                    out, src = w1T[:, n], p16[:]
                else:
                    out, src = w2T[:, 4 * (n - 2):4 * (n - 2) + 4].rearrange("p f n -> p (f n)"), p16[:]
                nc.scalar.activation(out, src, ACT.Copy).then_inc(s["w16_taken"], 1)

            def take_o(t, k, _):
                act.wait_ge(s["oT_done"], t + 1)
                nc.scalar.activation(oT[:], pO, ACT.Copy).then_inc(s["oT_taken"], 1)

            def take_x(t, k, _):
                act.wait_ge(s["xT_done"], t + 1)
                nc.scalar.activation(xT[:], pX[:], ACT.Copy).then_inc(s["xT_taken"], 1)

            def relu(t, k, _):
                wait(act, s["hq_ready"], t)
                for j in range(2):
                    act.wait_ge(s["h_done"], 2 * t + j + 1)
                    for f in range(4 * j, 4 * j + 4):
                        nc.scalar.activation(hb[:, f], pH[j][:, f % 4], ACT.Relu,
                                             bias=b1[:, f:f + 1]).then_inc(s["relu_done"], 1)

            pipeline(act, NT, [(take_x, 0), (relu, 0), (take_o, 2)])

        @block.vector
        def _(dve):
            own = Counted(dve, s["dve"])
            dve.wait_ge(w_in, 16 * 9)
            nc.vector.tensor_reduce(mx[:, 0:1], w1[:], AX.XY, ALU.max, apply_absolute_value=True)\
                .then_inc(s["max_ready"], 1)
            nc.vector.tensor_reduce(mx[:, 1:2], w2[:], AX.XY, ALU.max, apply_absolute_value=True)\
                .then_inc(s["max_ready"], 1)
            quantise_rows(nc, own, wp[:], wpn[:], wa[:, 0], wa[:, 1], dequantise=True)
            at["wp"] = own.n
            dve.wait_ge(s["max_all"], 1)
            own(nc.vector.tensor_scalar(sc[:, SW1:SW2 + 1], ma[:], 1 / 7.0, None, ALU.mult)).done()
            own(nc.vector.reciprocal(sc[:, RW1:RW2 + 1], sc[:, SW1:SW2 + 1]))
            own(nc.vector.reciprocal(col(RS1), col(S1)))
            own(nc.vector.reciprocal(col(RS2), col(S2)))
            own(nc.vector.tensor_tensor(sc[:, P1:P2 + 1], sc[:, S1:S2 + 1], sc[:, SW1:SW2 + 1], ALU.mult)).done()
            own(nc.vector.reciprocal(sc[:, R1:R2 + 1], sc[:, P1:P2 + 1]))
            own(nc.vector.tensor_tensor(col(KAP), col(P1), col(RS2), ALU.mult)).done()
            for w, wn, r in ((w1, w1n, RW1), (w2, w2n, RW2)):
                own(nc.vector.tensor_scalar(w[:], w[:], col(r), MAGIC, ALU.mult, ALU.add)).done()
                own(nc.vector.tensor_scalar(w[:], w[:], MAGIC, 7.0, ALU.subtract, ALU.min)).done()
                own(nc.vector.tensor_scalar(wn[:], w[:], -8.0, None, ALU.max)).done()
            at["w16"] = own.n
            for b, r, rows_ in ((b1[:], R1, 128), (rows[:, 2], R2, TT)):
                own(nc.vector.tensor_scalar(b, b, col(r, rows_), -2.0 ** 31, ALU.mult, ALU.max)).done()
                own(nc.vector.tensor_scalar(b, b, 2.0 ** 31, None, ALU.min)).done()
                round_any(nc, own, b, tmp[0:rows_, :, 0:b.shape[1]])
            own(nc.vector.tensor_scalar(rows[:, 2], rows[:, 2], col(P2, TT), None, ALU.mult)).done()
            for c in range(KC):
                dve.wait_ge(s["wT_hi"], c + 1)
                own(nc.vector.scalar_tensor_tensor(wpT[:, 1, c], p0[c][:, 0:H], WS, wpT[:, 0, c], ALU.mult,
                                                   ALU.subtract))
            own.done()
            at["prep"] = own.n
            dve.sem_inc(s["prep"], 1)

            def quantise_o(t, k, _):
                q = Counted(dve, s["quant_o"])
                q.n = 6 * t
                dve.wait_ge(s["ob_ready"], t + 1)
                wait(dve, s["oq_ready"], t)
                scale, recip = am[:, k, 0:1], am[:, k, 1:2]
                q(nc.vector.tensor_reduce(scale, ot[:, k], AX.X, ALU.max, apply_absolute_value=True)).done()
                q(nc.vector.tensor_scalar(scale, scale, 1 / 127.0, 1e-8, ALU.mult, ALU.max)).done()
                q(nc.vector.reciprocal(recip, scale)).done()
                q(nc.vector.tensor_scalar(ob[:], ot[:, k], recip, MAGIC, ALU.mult, ALU.add)).done()
                q(nc.vector.tensor_scalar(ob[:], ob[:], MAGIC, 127.0, ALU.subtract, ALU.min)).done()
                q(nc.vector.tensor_scalar(recip, scale, 1 / WS, None, ALU.mult)).done()
                nc.vector.tensor_scalar(oq[:, k], ob[:], -127.0, None, ALU.max).then_inc(s["oq_ready"], 1)

            def residual(t, k, _):
                q = Counted(dve, s["resid"])
                q.n = 3 * t
                xrow = g.xs[:, ds(t, 1), :].rearrange("p a n -> p (a n)")
                dve.wait_ge(s["xr_ready"], t + 1)
                dve.wait_ge(s["y_done"], t + 1)
                q(nc.vector.scalar_tensor_tensor(xrow, pY[0:TT, :], am[:, k, 1:2], xrow, ALU.mult, ALU.add)).done()
                passed(dve, gate)
                q(nc.vector.bn_stats(st6[:], xrow)).done()
                passed(dve, gate)
                q(nc.vector.bn_aggr(mv[:, k], st6[:])).done()
                nc.vector.tensor_scalar(ve[:], mv[:, k, 1:2], LN_EPS, None, ALU.add).then_inc(s["var"], 1)

            def quantise_x(t, k, _):
                q = Counted(dve, s["quant_x"])
                q.n = 3 * t
                xrow = g.xs[:, ds(t, 1), :].rearrange("p a n -> p (a n)")
                dve.wait_ge(s["rstd"], t + 1)
                wait(dve, s["xq_ready"], t)
                q(nc.vector.tensor_scalar(xn[:], xrow, mv[:, k, 0:1], rs[:], ALU.subtract, ALU.mult)).done()
                q(nc.vector.tensor_scalar(xn[:], xn[:], col(RS1, TT), MAGIC, ALU.mult, ALU.add)).done()
                q(nc.vector.tensor_scalar(xn[:], xn[:], MAGIC, 7.0, ALU.subtract, ALU.min)).done()
                nc.vector.tensor_scalar(xq[:], xn[:], -8.0, None, ALU.max).then_inc(s["xq_ready"], 1)

            def quantise_h(t, k, _):
                dve.wait_ge(s["relu_done"], 8 * t + 8)
                nc.vector.tensor_scalar(hb[:], hb[:], col(KAP), MAGIC, ALU.mult, ALU.add).then_inc(s["quant_h"], 1)
                dve.wait_ge(s["quant_h"], t + 1)
                nc.vector.tensor_scalar(hq[:], hb[:], MAGIC, 15.0, ALU.subtract, ALU.min).then_inc(s["hq_ready"], 1)

            def finish(t, k, half):
                dve.wait_ge(s["xb_ready"], t + 1)
                dve.wait_ge(s["z_done"], t + 1)
                wait(dve, out_done[k], 16 * half)
                nc.vector.scalar_tensor_tensor(yt[:, k], pZ[0:TT, :], col(P2, TT), xr[:, k], ALU.mult,
                                               ALU.add).then_inc(s["out_ready"], 1)

            pipeline(dve, NT, [(quantise_o, 2), (quantise_h, -1), (residual, 1), (finish, -1), (quantise_x, 1)])

        @block.tensor
        def _(pe):
            pe.wait_ge(s["dve"], at["wp"])
            for c in range(KC):
                for o in range(KC):
                    last = nc.tensor.transpose(p0[c][:, o * 128:(o + 1) * 128], wpn[:, o, c * 128:(c + 1) * 128],
                                               g.ident[:])
                last.then_inc(s["wT_done"], 1)
            pe.wait_ge(s["dve"], at["w16"])
            for n in range(4):
                wait(pe, s["w16_taken"], n)
                for o in range(8):
                    if n < 2:
                        src = w1n[:, o, n * 128:(n + 1) * 128]
                    else:
                        f = 4 * (n - 2) + o // 2
                        src = w2n[:, o % 2, f * 128:(f + 1) * 128]
                    last = nc.tensor.transpose(p16[:, o * 128:(o + 1) * 128], src, g.ident16[:])
                last.then_inc(s["w16_done"], 1)
            pe.wait_ge(s["dve"], at["prep"])

            pe.wait_ge(s["w16_taken"], 4)

            def turn_o(t, k, _):
                pe.wait_ge(s["oq_ready"], t + 1)
                for c in range(KC):
                    last = nc.tensor.transpose(pO[:, c], oq[:, k, c * 128:(c + 1) * 128], g.ident16[0:TT, 0:TT])
                last.then_inc(s["oT_done"], 1)

            def project(t, k, _):
                pe.wait_ge(s["oT_taken"], t + 1)
                wait(pe, s["var"], t)
                for c in range(KC):
                    for n in range(2):
                        last = nc.tensor.matmul(pY[0:TT, :], oT[:, c], wpT[:, n, c], start=(c == 0 and n == 0),
                                                stop=(c == KC - 1 and n == 1))
                last.then_inc(s["y_done"], 1)

            def turn_x(t, k, _):
                pe.wait_ge(s["xq_ready"], t + 1)
                for c in range(KC):
                    last = nc.tensor.transpose(pX[:, c], xq[:, c * 128:(c + 1) * 128], g.ident16[0:TT, 0:TT])
                last.then_inc(s["xT_done"], 1)

            def layer1(t, k, _):
                pe.wait_ge(s["xT_taken"], t + 1)
                for j in range(2):
                    wait(pe, s["relu_done"], 8 * t + 4 * j - 4)
                    for f in range(4):
                        for c in range(KC):
                            cols = slice((4 * j + f) * 128, (4 * j + f + 1) * 128)
                            last = nc.tensor.matmul(pH[j][:, f], w1T[:, c, cols], xT[:, c], start=(c == 0),
                                                    stop=(c == KC - 1))
                    last.then_inc(s["h_done"], 1)

            def layer2(t, k, _):
                pe.wait_ge(s["hq_ready"], t + 1)
                wait(pe, s["out_ready"], t)
                for f in range(FB):
                    last = nc.tensor.matmul(pZ[0:TT, :], hq[:, f], w2T[:, f], start=(f == 0), stop=(f == FB - 1))
                last.then_inc(s["z_done"], 1)

            pipeline(pe, NT, [(turn_x, 0), (project, 1), (layer1, 0), (turn_o, 2), (layer2, -1)])


class G:
    pass


def build(nc, io):
    with ExitStack() as ctx:
        a = Alloc(nc, ctx)
        g = G()
        g.ident = a.sb("ident", [128, 128])
        g.ident16 = a.sb("ident16", [128, 128], F16)
        g.blk16 = a.sb("blk16", [128, 8])
        g.evenodd = a.sb("evenodd", [128, 2])
        g.mhalf = a.sb("mhalf", [128, NH])
        constants(nc, g)
        q0_phase(nc, g, io)
        attn0_phase(nc, g, io)
        g.xs = a.sb("xs", [TT, NT, H])
        with ExitStack() as inner:
            b = Alloc(nc, inner)
            g.xT = b.sb("xT", [128, 2, KC, TOK], F16)
            g.comb = b.sb("comb", [TT, NT, NX])
            mix0_phase(nc, g, io)
            experts_phase(nc, g, io)

        q1_phase(nc, g, io)
        attn1_phase(nc, g, io)
        final_phase(nc, g, io)


_NAMES = dict(
    x="x", ctx="ctx_2048", mask="mask_1xSxS2_ff0", Wq="L0_xattn_Wq", bq="L0_xattn_bq", Wk="L0_xattn_Wk",
    bk="L0_xattn_bk", Wv="L0_xattn_Wv", bv="L0_xattn_bv", Wo="L0_xattn_Wo", qn_w="L0_xattn_qn_w",
    kn_w="L0_xattn_kn_w", gate_w="L0_ffn_gate_w", w_gate="L0_ffn_w_gate", w_up="L0_ffn_w_up",
    w_down="L0_ffn_w_down", sw_gate="L0_ffn_sw_gate", sw_up="L0_ffn_sw_up", sw_down="L0_ffn_sw_down",
    wq="L1_xattn_wq", bq1="L1_xattn_bq", wkv="L1_xattn_wkv", bkv="L1_xattn_bkv", wp="L1_xattn_wp",
    bp="L1_xattn_bp", W1="L1_ffn_W1", b1="L1_ffn_b1", W2="L1_ffn_W2", b2="L1_ffn_b2", s1="L1_ffn_s_act1",
    s2="L1_ffn_s_act2")


class Tensors:
    pass


def kernel(**inputs):
    import concourse.bacc as bacc
    from concourse.bass_utils import run_bass_kernel_spmd

    nc = bacc.Bacc("TRN2", target_bir_lowering=False, num_devices=1)
    io, arrays = Tensors(), {}
    for name, full in _NAMES.items():
        arr = np.ascontiguousarray(inputs[full])
        if name == "x":
            arr = arr.reshape(TOK, H)
        arrays[full] = arr
        io.__dict__[name] = nc.dram_tensor(full, arr.shape, mybir.dt.from_np(arr.dtype), kind="ExternalInput").ap()
    io.out = nc.dram_tensor("out", [TOK, H], F32, kind="ExternalOutput").ap()
    for name, shape, dt in (("qh", [B, 128, NR * RP], F16), ("ql", [B, 128, NR * RP], F16),
                            ("o0", [TOK, NH * HD], F32), ("q1", [B, 2, 128, KC, RP], F16), ("o1", [TOK, H], F32)):
        io.__dict__[name] = nc.dram_tensor("scratch_" + name, shape, dt, kind="Internal").ap()
    build(nc, io)
    r = run_bass_kernel_spmd(nc, [arrays], core_ids=[0])
    return r.results[0]["out"].reshape(B, S, H)
```
